# Optimizing a Trainium2 kernel written in Bass

```python
import numpy as np
import jax
import jax.numpy as jnp

def _softmax(x, axis=-1):
    return jax.nn.softmax(x, axis=axis)

def _gelu(x):
    return jax.nn.gelu(x, approximate=True)

def _silu(x):
    return jax.nn.silu(x)

def _sigmoid(x):
    return jax.nn.sigmoid(x)

def _layernorm(x, axis=-1, eps=1e-05):
    m = jnp.mean(x, axis=axis, keepdims=True)
    v = jnp.var(x, axis=axis, keepdims=True)
    return (x - m) / jnp.sqrt(v + eps)

def _scatter_add(tgt, idx, src, axis=0):
    return tgt.at[idx].add(src)

def _segment_sum(src, seg, n):
    return jax.ops.segment_sum(src, seg, n)
kernel_name = 'mk_gnn_preln_d4_gnn_r32_21708d'

def setup_inputs(seed: int=0):
    np.random.seed(seed)
    _w = jnp.asarray

    def _rec_inputs():
        import jax
        import jax.numpy as jnp
        _gk = jax.random.key(seed)
        x = -0.0005121 + 1.001 * jax.random.normal(jax.random.fold_in(_gk, 1), (50000, 64), jnp.float32)
        src = jax.random.randint(jax.random.fold_in(_gk, 2), (50000,), 0, 50000, jnp.int32)
        dst = jnp.minimum((50000 * jax.random.uniform(jax.random.fold_in(_gk, 3), (50000,)) ** 2.0).astype(jnp.int32), 49999)
        _o = jnp.argsort(dst, stable=True)
        src = src[_o]
        dst = dst[_o]
        edge_attr_64 = -5.3897e-05 + 0.999841 * jax.random.normal(jax.random.fold_in(_gk, 12), (50000, 64), jnp.float32)
        edge_type_64 = jax.random.randint(jax.random.fold_in(_gk, 14), (50000,), 0, 64, jnp.int32)
        return (x, src, dst, edge_attr_64, edge_type_64)
    x, src, dst, edge_attr_64, edge_type_64 = _rec_inputs()

    def _L0_gnn_setup():
        import jax, jax.numpy as jnp
        import numpy as np
        N_NODES = 50000
        N_EDGES = 12500
        DIM = 64
        HEADS = 4
        BN_EPS = 1e-05

        def glorot(key, shape, fan_in, fan_out):
            std = np.sqrt(6.0 / (fan_in + fan_out))
            return jax.random.uniform(key, shape, jnp.float32, -std, std)

        def segment_softmax(a, seg, num_segments):
            m = jax.ops.segment_max(a, seg, num_segments=num_segments)
            e = jnp.exp(a - m[seg])
            s = jax.ops.segment_sum(e, seg, num_segments=num_segments)
            return e / (s[seg] + 1e-16)
        key = jax.random.key(seed)
        ks = jax.random.split(key, 6)
        x = jax.random.normal(ks[0], (N_NODES, DIM), jnp.float32)
        edge_attr = jax.random.normal(ks[1], (N_EDGES, DIM), jnp.float32)
        edge_index = jax.random.randint(ks[2], (2, N_EDGES), 0, N_NODES, jnp.int64)
        W = glorot(ks[3], (2 * DIM, HEADS * DIM), 2 * DIM, HEADS * DIM)
        att = glorot(ks[4], (1, HEADS, 2 * DIM), 2 * DIM, 1)
        bias = jnp.zeros((DIM,), jnp.float32)
        bn_gamma = jnp.ones((HEADS,), jnp.float32)
        bn_beta = jnp.zeros((HEADS,), jnp.float32)
        return {'x': x, 'edge_attr': edge_attr, 'W': W, 'att': att, 'bias': bias, 'bn_gamma': bn_gamma, 'bn_beta': bn_beta, 'edge_index': edge_index}
    _L0_gnn_all = _L0_gnn_setup()
    _L0_gnn_in = {k: v for k, v in _L0_gnn_all.items() if k in ('W', 'att', 'bias', 'bn_gamma', 'bn_beta')}
    del _L0_gnn_all

    def _L1_gnn_setup():
        import jax, jax.numpy as jnp
        import numpy as np
        N_NODES = 50000
        N_EDGES = 25000
        D_FEAT = 64
        key = jax.random.key(seed)
        k1, k2, k3 = jax.random.split(key, 3)
        xs = jax.random.normal(k1, (N_NODES, D_FEAT), dtype=jnp.float32)
        src = jax.random.randint(k2, (N_EDGES,), 0, N_NODES, dtype=jnp.int32)
        dst = jax.random.randint(k3, (N_EDGES,), 0, N_NODES, dtype=jnp.int32)
        return {'xs': xs, 'src': src, 'dst': dst}
    _L1_gnn_all = _L1_gnn_setup()
    _L1_gnn_in = {k: v for k, v in _L1_gnn_all.items() if k in ()}
    del _L1_gnn_all

    def _L2_gnn_setup():
        import jax, jax.numpy as jnp
        import numpy as np
        N_NODES = 3125
        N_EDGES = 1250000
        EMBED_DIM = 64
        N_RELATIONS = 64
        key = jax.random.key(seed)
        k1, k2, k3, k4, k5, k6 = jax.random.split(key, 6)
        entity_emb = jax.random.normal(k1, (N_NODES, EMBED_DIM), dtype=jnp.float32)
        heads = jax.random.randint(k2, (N_EDGES,), 0, N_NODES)
        rels = jax.random.randint(k3, (N_EDGES,), 0, N_RELATIONS)
        tails = jax.random.randint(k4, (N_EDGES,), 0, N_NODES)
        rel_embed = 0.01 * jax.random.normal(k5, (N_RELATIONS, EMBED_DIM), dtype=jnp.float32)
        limit = float(np.sqrt(6.0 / (EMBED_DIM + EMBED_DIM)))
        W = jax.random.uniform(k6, (EMBED_DIM, EMBED_DIM), dtype=jnp.float32, minval=-limit, maxval=limit)
        return {'entity_emb': entity_emb, 'heads': heads, 'rels': rels, 'tails': tails, 'rel_embed': rel_embed, 'W': W}
    _L2_gnn_all = _L2_gnn_setup()
    _L2_gnn_in = {k: v for k, v in _L2_gnn_all.items() if k in ('rel_embed', 'W')}
    del _L2_gnn_all

    def _L3_gnn_setup():
        import jax, jax.numpy as jnp
        import numpy as np
        N_NODES = 3125
        N_EDGES = 50000
        IN_FEATS = 64
        OUT_FEATS = 64
        K_HOPS = 2
        key = jax.random.key(seed)
        k1, k2, k3, k4, k5, k6, k7 = jax.random.split(key, 7)
        feat = jax.random.normal(k1, (N_NODES, IN_FEATS), dtype=jnp.float32)
        src = jax.random.randint(k2, (N_EDGES,), 0, N_NODES, dtype=jnp.int64)
        dst = jax.random.randint(k3, (N_EDGES,), 0, N_NODES, dtype=jnp.int64)
        s = 1.0 / np.sqrt(IN_FEATS)
        W = jax.random.uniform(k4, (OUT_FEATS, IN_FEATS), jnp.float32, -s, s)
        b = jax.random.uniform(k5, (OUT_FEATS,), jnp.float32, -s, s)
        Wr = jax.random.uniform(k6, (OUT_FEATS, IN_FEATS), jnp.float32, -s, s)
        br = jax.random.uniform(k7, (OUT_FEATS,), jnp.float32, -s, s)
        return {'feat': feat, 'W': W, 'b': b, 'Wr': Wr, 'br': br, 'src': src, 'dst': dst}
    _L3_gnn_all = _L3_gnn_setup()
    _L3_gnn_in = {k: v for k, v in _L3_gnn_all.items() if k in ('W', 'b', 'Wr', 'br')}
    del _L3_gnn_all
    return {'x': x, 'src': src, 'dst': dst, 'edge_attr_64': edge_attr_64, 'edge_type_64': edge_type_64, 'L0_gnn_W': _L0_gnn_in['W'], 'L0_gnn_att': _L0_gnn_in['att'], 'L0_gnn_bias': _L0_gnn_in['bias'], 'L0_gnn_bn_gamma': _L0_gnn_in['bn_gamma'], 'L0_gnn_bn_beta': _L0_gnn_in['bn_beta'], 'L2_gnn_rel_embed': _L2_gnn_in['rel_embed'], 'L2_gnn_W': _L2_gnn_in['W'], 'L3_gnn_W': _L3_gnn_in['W'], 'L3_gnn_b': _L3_gnn_in['b'], 'L3_gnn_Wr': _L3_gnn_in['Wr'], 'L3_gnn_br': _L3_gnn_in['br']}

def reference(x, src, dst, edge_attr_64, edge_type_64, L0_gnn_W, L0_gnn_att, L0_gnn_bias, L0_gnn_bn_gamma, L0_gnn_bn_beta, L2_gnn_rel_embed, L2_gnn_W, L3_gnn_W, L3_gnn_b, L3_gnn_Wr, L3_gnn_br):
    import jax
    import jax.numpy as jnp

    def _L0_gnn_ref(x, edge_attr, W, att, bias, bn_gamma, bn_beta, edge_index):
        import jax, jax.numpy as jnp
        import numpy as np
        N_NODES = 50000
        N_EDGES = 12500
        DIM = 64
        HEADS = 4
        BN_EPS = 1e-05

        def glorot(key, shape, fan_in, fan_out):
            std = np.sqrt(6.0 / (fan_in + fan_out))
            return jax.random.uniform(key, shape, jnp.float32, -std, std)

        def segment_softmax(a, seg, num_segments):
            m = jax.ops.segment_max(a, seg, num_segments=num_segments)
            e = jnp.exp(a - m[seg])
            s = jax.ops.segment_sum(e, seg, num_segments=num_segments)
            return e / (s[seg] + 1e-16)
        act = jax.nn.softplus
        i, j = (edge_index[0], edge_index[1])
        x_i = x[i]
        x_j = x[j]
        out_i = act(jnp.concatenate([x_i, edge_attr], -1) @ W).reshape(-1, HEADS, DIM)
        out_j = act(jnp.concatenate([x_j, edge_attr], -1) @ W).reshape(-1, HEADS, DIM)
        alpha = act((jnp.concatenate([out_i, out_j], -1) * att).sum(-1))
        mu = alpha.mean(0)
        var = alpha.var(0)
        alpha = (alpha - mu) * jax.lax.rsqrt(var + BN_EPS) * bn_gamma + bn_beta
        alpha = act(alpha)
        alpha = segment_softmax(alpha, i, N_NODES)
        msg = out_j * alpha[:, :, None]
        aggr = jax.ops.segment_sum(msg, i, num_segments=N_NODES)
        out = aggr.mean(1) + bias
        return out

    def _L1_gnn_ref(xs, src, dst):
        import jax, jax.numpy as jnp
        import numpy as np
        N_NODES = 50000
        N_EDGES = 25000
        D_FEAT = 64
        gathered = xs[src]
        sums = jax.ops.segment_sum(gathered, dst, num_segments=N_NODES)
        counts = jax.ops.segment_sum(jnp.ones((src.shape[0],), dtype=xs.dtype), dst, num_segments=N_NODES)
        return sums / jnp.maximum(counts, 1.0)[:, None]

    def _L2_gnn_ref(entity_emb, heads, rels, tails, rel_embed, W):
        import jax, jax.numpy as jnp
        import numpy as np
        N_NODES = 3125
        N_EDGES = 1250000
        EMBED_DIM = 64
        N_RELATIONS = 64
        n, D = entity_emb.shape
        e_h = entity_emb[heads]
        e_t = entity_emb[tails]
        e_r = rel_embed[rels]
        gate = jnp.tanh(e_h + e_r)
        score = jnp.sum(e_t * gate, axis=-1)
        score = score - jax.lax.stop_gradient(jnp.max(score))
        exp_s = jnp.exp(score)
        s_sum = jax.ops.segment_sum(exp_s, heads, num_segments=n)
        attn = exp_s / (s_sum[heads] + 1e-10)
        agg = jax.ops.segment_sum(attn[:, None] * e_t, heads, num_segments=n)
        out = (entity_emb + agg) @ W.T
        return jax.nn.leaky_relu(out, negative_slope=0.2)

    def _L3_gnn_ref(feat, W, b, Wr, br, src, dst):
        import jax, jax.numpy as jnp
        import numpy as np
        N_NODES = 3125
        N_EDGES = 50000
        IN_FEATS = 64
        OUT_FEATS = 64
        K_HOPS = 2
        n = feat.shape[0]
        deg = jax.ops.segment_sum(jnp.ones_like(dst, dtype=feat.dtype), dst, num_segments=n)
        inv_sqrt = jnp.where(deg > 0, deg, 1.0) ** (-0.5)
        h = feat
        for _ in range(K_HOPS):
            h = h * inv_sqrt[:, None]
            msg = h[src]
            h = jax.ops.segment_sum(msg, dst, num_segments=n)
            h = h * inv_sqrt[:, None]
        out = h @ W.T + b
        out = out + feat @ Wr.T + br
        return out
    edge_index = jnp.stack([src, dst])
    h = jnp.maximum(_layernorm(x, axis=-1), 0.0)
    x = x + _L0_gnn_ref(h, edge_attr_64, L0_gnn_W, L0_gnn_att, L0_gnn_bias, L0_gnn_bn_gamma, L0_gnn_bn_beta, edge_index)
    h = jnp.maximum(_layernorm(x, axis=-1), 0.0)
    x = x + _L1_gnn_ref(h, src, dst)
    h = jnp.maximum(_layernorm(x, axis=-1), 0.0)
    x = x + _L2_gnn_ref(h, src, edge_type_64, dst, L2_gnn_rel_embed, L2_gnn_W)
    h = jnp.maximum(_layernorm(x, axis=-1), 0.0)
    x = x + _L3_gnn_ref(h, L3_gnn_W, L3_gnn_b, L3_gnn_Wr, L3_gnn_br, src, dst)
    return x

_drawn_inputs = setup_inputs


def setup_inputs(seed=0):
    import zlib

    import numpy as np

    out = dict(_drawn_inputs(seed))
    spreads = {'L0_gnn_bias': (0.0, 0.1), 'L0_gnn_bn_gamma': (1.0, 0.6), 'L0_gnn_bn_beta': (0.0, 2.0)}
    factors = {'L2_gnn_rel_embed': 45.608}
    for name, (base, spread) in spreads.items():
        noise = np.random.default_rng([zlib.crc32(name.encode()), seed]).standard_normal(out[name].shape)
        drawn = base * np.exp(spread * noise) if base else spread * noise
        out[name] = jnp.asarray(drawn.astype(out[name].dtype))
    for name, factor in factors.items():
        out[name] = (out[name] * factor).astype(out[name].dtype)
    return out
```

```python
import concourse.bass as bass
from concourse import mybir
from contextlib import ExitStack

P = 128
D = 64
N = 50000
TILES = 392
NPAD = TILES * P
K = 4
CHUNK = K * P
CHUNKS = TILES // K
LAST_REAL = N - (CHUNKS - 1) * CHUNK
ROWS = 14
NCHUNKS = TILES // ROWS
SORT_N = 1 << 16
SORT_F = SORT_N // P
HEADS = 4
OOB = 200000.0
SPLIT = 32384
NEG_TOP = 0xFFFF - 0x80
POS_OFF = SPLIT - 0x80
BIG = 1e30
CLAMP = 30.0
LN_EPS = 1e-5
SEGS = 32
SEG_LEN = NPAD // SEGS

fp32 = mybir.dt.float32
i32 = mybir.dt.int32
u32 = mybir.dt.uint32
ALU = mybir.AluOpType
ACT = mybir.ActivationFunctionType
AX = mybir.AxisListType.X


def gnn_kernel(nc, x, rec, src, dst, ident, w0, att, bias0, gamma, beta, headsel, headsum, samehead,
               rel, w2, w3, b3, br3, out, debug=()):
    ctx = ExitStack()
    made = {}

    def dram(name, shape, dt=fp32):
        return nc.dram_tensor(name, shape, dt, kind="Internal").ap()

    h0 = dram("h0", (NPAD, D))
    h1 = dram("h1", (NPAD, D))
    h2 = dram("h2", (NPAD, D))
    x1 = dram("x1", (NPAD, D))
    x2 = dram("x2", (NPAD, D))
    x3 = dram("x3", (NPAD, D))
    feat = dram("feat", (NPAD, D))
    g0 = dram("g0", (NPAD, D))
    g1 = dram("g1", (NPAD, D))
    msg0 = dram("msg0", (NPAD, D))
    msg1 = dram("msg1", (NPAD, D + 1))
    msg2 = dram("msg2", (NPAD, D + 2))
    hop0 = dram("hop0", (NPAD, D))
    hop1 = dram("hop1", (NPAD, D))
    same_src = dram("same_src", (SORT_N,))
    same_dst = dram("same_dst", (SORT_N,))
    sp_j = dram("sp_j", (CHUNKS, 2, P, CHUNK))
    logits = dram("logits", (HEADS, NPAD))
    weights = dram("weights", (HEADS, NPAD))
    types_row = dram("types_row", (TILES, P))

    with ctx:
        def sb_in(c, name, shape, dt=fp32):
            return c.enter_context(nc.sbuf_tensor("sb_" + name, shape, dt))

        def ps_in(c, name, shape):
            return c.enter_context(nc.psum_tensor("ps_" + name, shape, fp32))

        def sem_in(c, name):
            return nc.alloc_semaphore(name=name)

        def sb(name, shape, dt=fp32):
            return sb_in(ctx, name, shape, dt)

        def sem(name):
            return ctx.enter_context(nc.semaphore(name))

        edge_of = sb("edge_of", [P, SORT_F], i32)
        src_of = sb("src_of", [P, SORT_F], i32)
        out_src = sb("out_src", [P, SORT_F], i32)
        from_dst = sb("from_dst", [P, SORT_F], i32)
        out_dst = sb("out_dst", [P, SORT_F], i32)
        dst_of = sb("dst_of", [P, TILES], i32)
        type_of = sb("type_of", [P, TILES])
        inv_deg = sb("inv_deg", [P, NCHUNKS, ROWS])
        eye = sb("eye", [P, P])
        pid = sb("pid", [P, 1])
        ready = sem("ready")

        def await_in_loop(eng, semaphore, value):
            eng.wait_ge(semaphore, value)
            eng.sem_inc(ready, 1)

        with ExitStack() as c:
            c.enter_context(nc.cleanup_on_exit())
            raw = [sb_in(c, "raw_src", [P, SORT_F], i32), sb_in(c, "raw_dst", [P, SORT_F], i32)]
            slot = sb_in(c, "slot", [P, SORT_F], i32)
            pidi = sb_in(c, "pidi", [P, 1], i32)
            signs_i = sb_in(c, "signs_i", [P, 8], i32)
            signs_t = sb_in(c, "signs_t", [P, 8], i32)
            signs = sb_in(c, "signs", [P, 8])
            key = [[sb_in(c, f"key{a}{b}", [P, SORT_F]) for b in range(2)] for a in range(2)]
            below = [sb_in(c, f"below{a}", [P, SORT_F]) for a in range(2)]
            work = [sb_in(c, f"work{a}", [P, SORT_F]) for a in range(2)]
            high = [sb_in(c, f"high{a}", [P, SORT_F], i32) for a in range(2)]
            node = [sb_in(c, f"node{a}", [P, SORT_F + 2]) for a in range(2)]
            same = [sb_in(c, f"same{a}", [P, SORT_F]) for a in range(2)]
            more = [sb_in(c, f"more{a}", [P, SORT_F]) for a in range(2)]
            dest = [sb_in(c, f"dest{a}", [P, SORT_F]) for a in range(2)]
            load_f = [sb_in(c, f"load_f{a}", [P, SORT_F]) for a in range(2)]
            turned = [ps_in(c, f"turned{a}", [P, 4, P]) for a in range(2)]
            final = [ps_in(c, f"final{n}", [P, 4, P]) for n in range(5)]
            loaded = sem_in(c, "loaded")
            counted = sem_in(c, "counted")
            chain = [sem_in(c, f"sort_chain{a}") for a in range(2)]
            signed = sem_in(c, "signed")
            handed = [sem_in(c, f"handed{a}") for a in range(2)]
            moved = [sem_in(c, f"moved{a}") for a in range(2)]
            back = [sem_in(c, f"back{a}") for a in range(2)]
            shifted = [sem_in(c, f"shifted{a}") for a in range(2)]
            flags_out = sem_in(c, "flags_out")
            decoded = [sem_in(c, f"decoded{a}") for a in range(2)]
            final_t = sem_in(c, "final_t")
            final_c = sem_in(c, "final_c")

            block = c.enter_context(nc.Block())
            FIRST_CROSS = 10
            TURNS = 2 * (17 - FIRST_CROSS)

            @block.sync
            def _(sp):
                sp.dma_start(raw[0][:, :], src.rearrange("(p f) -> p f", p=P)).then_inc(loaded, 16)
                sp.dma_start(raw[1][:, :], dst.rearrange("(p f) -> p f", p=P)).then_inc(loaded, 16)
                sp.dma_start(eye[:, :], ident).then_inc(loaded, 16)
                for a in range(2):
                    sp.wait_ge(decoded[a], 1)
                    sp.dma_start(node[a][1:P, 0:1], node[a][0:P - 1, SORT_F:SORT_F + 1]).then_inc(shifted[a], 16)
                    sp.dma_start(node[a][0:P - 1, SORT_F + 1:SORT_F + 2], node[a][1:P, 1:2]).then_inc(shifted[a], 16)
                for a, flags in enumerate((same_src, same_dst)):
                    sp.wait_ge(decoded[a], 2)
                    sp.dma_start(flags.rearrange("(p f) -> p f", p=P), same[a][:, :]).then_inc(flags_out, 16)
                sp.wait_ge(flags_out, 32)

            @block.gpsimd
            def _(pool):
                pool.iota(slot[:, :], pattern=[[1, SORT_F]], base=0, channel_multiplier=SORT_F).then_inc(counted, 1)
                pool.iota(pidi[:, :], pattern=[[0, 1]], base=0, channel_multiplier=1).then_inc(counted, 1)

            @block.vector
            def _(dve):
                v = nc.vector
                done = [0, 0]

                def link(a, ins):
                    done[a] += 1
                    ins.then_inc(chain[a], 1)

                def after(a):
                    if done[a]:
                        dve.wait_ge(chain[a], done[a])

                dve.wait_ge(counted, 2)
                v.tensor_copy(pid[:, :], pidi[:, :]).then_inc(signed, 1)
                v.tensor_scalar(signs_t[:, 0:1], pidi[:, :], 1, None, ALU.logical_shift_right).then_inc(signed, 1)
                dve.wait_ge(signed, 2)
                v.tensor_tensor(signs_t[:, 1:2], pidi[:, :], signs_t[:, 0:1], ALU.bitwise_xor).then_inc(signed, 1)
                dve.wait_ge(signed, 3)
                v.tensor_scalar(signs_i[:, 0:1], pidi[:, :], 1, None, ALU.bitwise_and).then_inc(signed, 1)
                for m in range(1, 8):
                    v.tensor_scalar(signs_i[:, m:m + 1], signs_t[:, 1:2], m - 1, 1, ALU.logical_shift_right,
                                    ALU.bitwise_and).then_inc(signed, 1)
                dve.wait_ge(signed, 11)
                v.tensor_scalar(signs[:, :], signs_i[:, :], -2.0, 1.0, ALU.mult, ALU.add).then_inc(signed, 1)
                dve.wait_ge(signed, 12)
                dve.wait_ge(loaded, 48)
                payload = [slot, raw[0]]
                for a in range(2):
                    link(a, v.tensor_scalar(below[a][:, :], raw[a][:, :], float(SPLIT), None, ALU.is_lt))
                    link(a, v.tensor_scalar(work[a][:, :], raw[a][:, :], -2.0, float(NEG_TOP + POS_OFF), ALU.mult, ALU.add))
                for a in range(2):
                    after(a)
                    link(a, v.tensor_tensor(work[a][:, :], work[a][:, :], below[a][:, :], ALU.mult))
                for a in range(2):
                    after(a)
                    link(a, v.scalar_tensor_tensor(high[a][:, :], raw[a][:, :], float(-POS_OFF), work[a][:, :],
                                                   ALU.add, ALU.add))
                for a in range(2):
                    after(a)
                    link(a, v.tensor_scalar(high[a][:, :], high[a][:, :], 16, None, ALU.logical_shift_left))
                for a in range(2):
                    after(a)
                    link(a, v.tensor_tensor(key[a][0].bitcast(i32)[:, :], high[a][:, :], payload[a][:, :], ALU.bitwise_or))

                def flip(a, b, lo_bit, lo, hi, w=2):
                    t = key[a][b][:, :].rearrange("p (g h l s) -> p g h l s", h=w, l=2, s=1 << lo_bit)[:, :, hi, lo, :]
                    link(a, v.tensor_scalar(t, t, -1.0, None, ALU.mult))

                at = [0, 0]
                turns = [0, 0]
                for a in range(2):
                    after(a)
                    flip(a, 0, 1, 1, 0)
                    flip(a, 0, 1, 1, 1)

                def stage(a, bit, last):
                    s, t = key[a][at[a]], key[a][1 - at[a]]
                    sv = s[:, :].rearrange("p (g two s) -> p g two s", two=2, s=1 << bit)
                    tv = t[:, :].rearrange("p (g two s) -> p g two s", two=2, s=1 << bit)
                    for side, op in ((0, ALU.min), (1, ALU.max)):
                        ins = v.tensor_tensor(tv[:, :, side, :], sv[:, :, 0, :], sv[:, :, 1, :], op)
                        if last:
                            ins.then_inc(handed[a], 1)
                        else:
                            link(a, ins)
                    at[a] = 1 - at[a]

                for k in range(1, 17):
                    if k >= FIRST_CROSS:
                        for bit in range(k - 1, 6, -1):
                            for a in range(2):
                                if bit == k - 1:
                                    dve.wait_ge(moved[a], turns[a] + 1)
                                    turns[a] += 1
                                    at[a] = 1 - at[a]
                                else:
                                    after(a)
                                stage(a, bit - 7, bit == 7)
                        low = 6
                    else:
                        low = k - 1
                    for bit in range(low, -1, -1):
                        for a in range(2):
                            if k >= FIRST_CROSS and bit == 6:
                                dve.wait_ge(moved[a], turns[a] + 1)
                                turns[a] += 1
                                at[a] = 1 - at[a]
                            else:
                                after(a)
                            stage(a, bit, False)
                    if k < 16:
                        for a in range(2):
                            after(a)
                            if k < 8:
                                flip(a, at[a], k, 1, 0)
                                flip(a, at[a], k, 0, 1)
                            else:
                                if k == 8:
                                    flip(a, at[a], 8, 1, 0, w=1)
                                    after(a)
                                ins = v.tensor_scalar(key[a][1 - at[a]][:, :], key[a][at[a]][:, :],
                                                      signs[:, k - 8:k - 7], None, ALU.mult)
                                at[a] = 1 - at[a]
                                if k + 1 >= FIRST_CROSS:
                                    ins.then_inc(handed[a], 2)
                                else:
                                    link(a, ins)
                for a in range(2):
                    after(a)
                    bits = key[a][at[a]].bitcast(i32)
                    link(a, v.tensor_scalar(high[a][:, :], bits[:, :], 16, None, ALU.logical_shift_right))
                    link(a, v.tensor_scalar(raw[a][:, :], bits[:, :], 0xFFFF, None, ALU.bitwise_and))
                    link(a, v.memset(node[a][:, :], -1.0))
                for a in range(2):
                    after(a)
                    link(a, v.tensor_scalar(below[a][:, :], high[a][:, :], 32768.0, None, ALU.is_ge))
                    link(a, v.tensor_scalar(work[a][:, :], high[a][:, :], -2.0, float(NEG_TOP - POS_OFF), ALU.mult, ALU.add))
                    link(a, v.tensor_copy(load_f[a][:, :], raw[a][:, :]))
                for a in range(2):
                    after(a)
                    link(a, v.tensor_tensor(work[a][:, :], work[a][:, :], below[a][:, :], ALU.mult))
                for a in range(2):
                    after(a)
                    v.scalar_tensor_tensor(node[a][:, 1:SORT_F + 1], high[a][:, :], float(POS_OFF), work[a][:, :],
                                           ALU.add, ALU.add).then_inc(decoded[a], 1)
                for a in range(2):
                    dve.wait_ge(decoded[a], 1)
                    dve.wait_ge(shifted[a], 32)
                    v.tensor_tensor(same[a][:, :], node[a][:, 1:SORT_F + 1], node[a][:, 0:SORT_F],
                                    ALU.is_equal).then_inc(decoded[a], 1)
                    link(a, v.tensor_tensor(more[a][:, :], node[a][:, 2:SORT_F + 2], node[a][:, 1:SORT_F + 1],
                                            ALU.is_equal))
                for a in range(2):
                    after(a)
                    v.scalar_tensor_tensor(dest[a][:, :], more[a][:, :], OOB, node[a][:, 1:SORT_F + 1],
                                           ALU.mult, ALU.add).then_inc(decoded[a], 1)

            FINALS = [(0, load_f[0], edge_of, 0), (0, node[0], src_of, 1), (0, dest[0], out_src, 0),
                      (1, load_f[1], from_dst, 0), (1, dest[1], out_dst, 0)]

            @block.tensor
            def _(pe):
                pe.wait_ge(loaded, 48)
                pe.wait_ge(signed, 12)
                at = [0, 0]
                for k in range(1, 10):
                    at = [(b + k) % 2 for b in at]
                at = [(b + 2) % 2 for b in at]
                for k in range(FIRST_CROSS, 17):
                    for half in range(2):
                        n = 2 * (k - FIRST_CROSS) + half
                        for a in range(2):
                            pe.wait_ge(handed[a], 2 * n + 2)
                            if n:
                                pe.wait_ge(moved[a], n)
                            s = key[a][at[a]][:, :]
                            for j in range(4):
                                piece = s[:, j * P:(j + 1) * P] if half == 0 else \
                                    s.rearrange("p (q j) -> p j q", j=4)[:, j, :]
                                ins = nc.tensor.transpose(turned[a][:, j, :], piece, eye[:, :])
                            ins.then_inc(back[a], 1)
                            at[a] = 1 - at[a]
                            at[a] = (at[a] + (k - 7 if half == 0 else 7 + 1)) % 2
                for n, (a, source, _, off) in enumerate(FINALS):
                    pe.wait_ge(decoded[a], 3)
                    for j in range(4):
                        ins = nc.tensor.transpose(final[n][:, j, :], source[:, off + j * P:off + (j + 1) * P], eye[:, :])
                    ins.then_inc(final_t, 1)

            @block.scalar
            def _(act):
                at = [1, 1]
                for k in range(1, 10):
                    at = [(b + k) % 2 for b in at]
                at = [(b + 2) % 2 for b in at]
                for k in range(FIRST_CROSS, 17):
                    for half in range(2):
                        n = 2 * (k - FIRST_CROSS) + half
                        for a in range(2):
                            act.wait_ge(back[a], n + 1)
                            o = key[a][at[a]][:, :]
                            o = o.rearrange("p (q j) -> p j q", j=4) if half == 0 else \
                                o.rearrange("p (j q) -> p j q", j=4)
                            nc.scalar.copy(o, turned[a][:, :, :]).then_inc(moved[a], 1)
                            at[a] = 1 - at[a]
                            at[a] = (at[a] + (k - 7 if half == 0 else 7 + 1)) % 2
                for n, (_, _, target, _) in enumerate(FINALS):
                    act.wait_ge(final_t, n + 1)
                    nc.scalar.copy(target[:, :].rearrange("p (q j) -> p j q", j=4), final[n][:, :, :]).then_inc(final_c, 1)

        if "sort" in debug:
            return

        bias_b = sb("bias_b", [P, D])
        b3_b = sb("b3_b", [P, 2, D])
        gmax = sb("gmax", [P, 1])
        inv_deg2 = sb("inv_deg2", [P, NCHUNKS, ROWS])
        minus_half = sb("minus_half", [P, ROWS])

        def pipeline(eng, count, parts, peel_last=False):
            most = max(lag for _, lag in parts)
            low = (most + 3) // 2 * 2
            high = (count - most if peel_last else count) // 2 * 2 - (2 if peel_last else 0)

            def straight(n):
                for f, lag in parts:
                    m = n - lag
                    if 0 <= m < count:
                        f(m, m % 2, m // 2, m < 2)

            for n in range(low):
                straight(n)
            with eng.Fori(low // 2, high // 2) as i:
                for r in range(2):
                    for f, lag in parts:
                        s = (r - lag) % 2
                        f(i * 2 + (r - lag), s, i + (r - lag - s) // 2, False)
            for n in range(high, count + most):
                straight(n)

        def rows_of(table, m, width=None):
            return table.rearrange("(c p k) f -> p c (k f)", p=P, k=ROWS)[:, bass.ds(m, 1), :]

        node_in = [sem(f"node_in{s}") for s in range(2)]
        node_taken = sem("node_taken")
        node_x = sem("node_x")
        node_sum = sem("node_sum")
        node_cent = sem("node_cent")
        node_sq = sem("node_sq")
        node_var = sem("node_var")
        node_eps = sem("node_eps")
        node_rstd = sem("node_rstd")
        node_norm = sem("node_norm")
        node_h = sem("node_h")
        node_x_out = [sem(f"node_x_out{s}") for s in range(2)]
        node_h_out = [sem(f"node_h_out{s}") for s in range(2)]
        node_base = [0]
        in_base = [0]
        x_out_base = [0]
        h_out_base = [0]

        def node_pass(kind, x_in, x_new, h_new):
            base, ib, xb, hb = node_base[0], in_base[0], x_out_base[0], h_out_base[0]
            xbase = base - NCHUNKS
            with ExitStack() as c:
                c.enter_context(nc.cleanup_on_exit())
                xi = [sb_in(c, f"xi_{kind}{s}", [P, ROWS, D]) for s in range(2)]
                width = {"first": 0, "l0": D, "l1": D + 1, "l2": D + 2}[kind]
                mi = [sb_in(c, f"mi_{kind}{s}", [P, ROWS, max(width, 1)]) for s in range(2)]
                xn = xi if kind == "first" else [sb_in(c, f"xn_{kind}{s}", [P, ROWS, D]) for s in range(2)]
                cent = [sb_in(c, f"cent_{kind}{s}", [P, ROWS, D]) for s in range(2)]
                sq = [sb_in(c, f"sq_{kind}{s}", [P, ROWS, D]) for s in range(2)]
                norm = [sb_in(c, f"norm_{kind}{s}", [P, ROWS, D]) for s in range(2)]
                hn = [sb_in(c, f"hn_{kind}{s}", [P, ROWS, D]) for s in range(2)]
                tmp = [sb_in(c, f"tmp_{kind}{s}", [P, ROWS, D]) for s in range(2)]
                total = [sb_in(c, f"total_{kind}{s}", [P, ROWS]) for s in range(2)]
                var = [sb_in(c, f"var_{kind}{s}", [P, ROWS]) for s in range(2)]
                vare = [sb_in(c, f"vare_{kind}{s}", [P, ROWS]) for s in range(2)]
                rstd = [sb_in(c, f"rstd_{kind}{s}", [P, ROWS]) for s in range(2)]
                small = [sb_in(c, f"small_{kind}{s}", [P, 6, ROWS]) for s in range(2)]
                fs = {n: sem_in(c, f"{kind}_{n}") for n in {
                    "first": (), "l0": ("biased",), "l1": ("clamped", "recip", "scaled", "inv"),
                    "l2": ("gap", "gap2", "expd", "den", "recip", "scaled", "y", "yt", "ytc", "z", "zs", "lrelu", "g",
                           "h2_in0", "h2_in1", "g_out0", "g_out1")}[kind]}
                loads = 1 if kind == "first" else 2
                if kind == "l2":
                    hi = [sb_in(c, f"hi_{s}", [P, ROWS, D]) for s in range(2)]
                    y = [sb_in(c, f"y_{s}", [P, ROWS, D]) for s in range(2)]
                    yt = [sb_in(c, f"yt_{s}", [P, ROWS * D]) for s in range(2)]
                    lr = [sb_in(c, f"lr_{s}", [P, ROWS, D]) for s in range(2)]
                    gn = [sb_in(c, f"gn_{s}", [P, ROWS, D]) for s in range(2)]
                    w2_sb = sb_in(c, "w2_sb", [P, P])
                    ps_yt = ps_in(c, "yt", [P, 1024])
                    ps_z = [ps_in(c, f"z{s}", [P, 1024]) for s in range(2)]
                consts = sem_in(c, f"{kind}_consts")
                block = c.enter_context(nc.Block())
                v = nc.vector

                @block.sync
                def _(sp):
                    def load(m, s, h, first):
                        if not first:
                            await_in_loop(sp, node_cent, base + m - 1)
                            if loads == 2:
                                await_in_loop(sp, node_taken, xbase + m - 1)
                            if kind == "first":
                                await_in_loop(sp, node_x_out[s], xb) if xb else None
                        sp.dma_start(xi[s][:, :, :].rearrange("p k (o f) -> p o (k f)", o=1), rows_of(x_in, m)).then_inc(node_in[s], 16)
                        if loads == 2:
                            table = {"l0": msg0, "l1": msg1, "l2": msg2}[kind]
                            sp.dma_start(mi[s][:, :, :].rearrange("p k (o f) -> p o (k f)", o=1), rows_of(table, m)).then_inc(node_in[s], 16)
                        if kind == "l2":
                            sp.dma_start(hi[s][:, :, :].rearrange("p k (o f) -> p o (k f)", o=1), rows_of(h2, m)).then_inc(fs[f"h2_in{s}"], 16)

                    def store_x(m, s, h, first):
                        await_in_loop(sp, node_x, xbase + m + 1)
                        sp.dma_start(rows_of(x_new, m), xn[s][:, :, :].rearrange("p k (o f) -> p o (k f)", o=1)).then_inc(node_x_out[s], 16)

                    def store_h(m, s, h, first):
                        await_in_loop(sp, node_h, base + m + 1)
                        sp.dma_start(rows_of(h_new, m), hn[s][:, :, :].rearrange("p k (o f) -> p o (k f)", o=1)).then_inc(node_h_out[s], 16)

                    def store_g(m, s, h, first):
                        await_in_loop(sp, fs["g"], m + 1)
                        sp.dma_start(rows_of(g0, m), gn[s][:, :, :].rearrange("p k (o f) -> p o (k f)", o=1)).then_inc(fs[f"g_out{s}"], 16)

                    if kind == "l0":
                        sp.dma_start(bias_b[:, :], bias0.to_broadcast([P, D])).then_inc(consts, 16)
                    if kind == "l2":
                        sp.dma_start(w2_sb[:, :], w2).then_inc(consts, 16)
                    parts = [(load, 0)]
                    if kind != "first":
                        parts.append((store_x, 1))
                    parts.append((store_h, 2))
                    if kind == "l2":
                        parts.append((store_g, 2))
                    pipeline(sp, NCHUNKS, parts)
                    for s in range(2):
                        if kind != "first":
                            await_in_loop(sp, node_x_out[s], xb + 16 * (NCHUNKS // 2))
                        await_in_loop(sp, node_h_out[s], hb + 16 * (NCHUNKS // 2))
                        if kind == "l2":
                            await_in_loop(sp, fs[f"g_out{s}"], 16 * (NCHUNKS // 2))

                @block.gpsimd
                def _(pool):
                    if kind == "first":
                        pool.memset(minus_half[:, :], -0.5).then_inc(consts, 1)
                        pool.wait_ge(consts, 1)

                    def front(m, s, h, first):
                        if kind == "l0":
                            if first:
                                pool.wait_ge(consts, 16)
                            await_in_loop(pool, node_in[s], ib + 16 * loads * (h + 1) if first else h * (16 * loads) + (ib + 16 * loads))
                            if not first:
                                await_in_loop(pool, node_x, xbase + m - 1)
                            pool.tensor_tensor(tmp[s][:, :, :], xi[s][:, :, :],
                                               bias_b[:, :].rearrange("p (o f) -> p o f", o=1).to_broadcast([P, ROWS, D]),
                                               ALU.add).then_inc(fs["biased"], 1)

                    def inv(m, s, h, first):
                        await_in_loop(pool, fs["clamped"], m + 1)
                        pool.tensor_tensor(inv_deg[:, bass.ds(m, 1), :], small[s][:, 0:1, :],
                                           minus_half[:, :].rearrange("p (o k) -> p o k", o=1), ALU.pow).then_inc(fs["inv"], 1)

                    def norm_part(m, s, h, first):
                        await_in_loop(pool, node_eps, base + m + 1)
                        if not first:
                            await_in_loop(pool, node_norm, base + m - 1)
                        pool.tensor_tensor(rstd[s][:, :], vare[s][:, :], minus_half[:, :], ALU.pow).then_inc(node_rstd, 1)
                        await_in_loop(pool, node_rstd, base + m + 1)
                        if not first:
                            await_in_loop(pool, node_h, base + m - 1)
                        pool.tensor_tensor(norm[s][:, :, :], cent[s][:, :, :],
                                           rstd[s][:, :].rearrange("p (k o) -> p k o", o=1).to_broadcast([P, ROWS, D]),
                                           ALU.mult).then_inc(node_norm, 1)

                    def scale_g(m, s, h, first):
                        await_in_loop(pool, node_h, base + m + 1)
                        if not first:
                            await_in_loop(pool, fs[f"g_out{s}"], h * 16)
                        pool.tensor_tensor(gn[s][:, :, :], hn[s][:, :, :],
                                           inv_deg[:, bass.ds(m, 1), :].rearrange("p o k -> p k o").to_broadcast([P, ROWS, D]),
                                           ALU.mult).then_inc(fs["g"], 1)

                    parts = [(front, 0)] if kind == "l0" else []
                    if kind == "l1":
                        parts.append((inv, 0))
                    parts.append((norm_part, 2 if kind == "l2" else 1))
                    if kind == "l2":
                        parts.append((scale_g, 2))
                    pipeline(pool, NCHUNKS, parts)

                @block.vector
                def _(dve):
                    def front(m, s, h, first):
                        wb_in = h * (16 * loads) + (ib + 16 * loads)
                        dve.wait_ge(node_in[s], wb_in)
                        if kind == "first":
                            return
                        if not first:
                            dve.wait_ge(node_x_out[s], h * 16 + xb)
                        if kind == "l0":
                            dve.wait_ge(fs["biased"], m + 1)
                            v.tensor_tensor(xn[s][:, :, :], tmp[s][:, :, :], mi[s][:, :, :], ALU.add).then_inc(node_x, 1)
                            dve.wait_ge(node_x, xbase + m + 1)
                            v.tensor_copy(small[s][:, 5, 0:1], small[s][:, 4, 0:1]).then_inc(node_taken, 1) if False else dve.sem_inc(node_taken, 1)
                        if kind == "l1":
                            if not first:
                                dve.wait_ge(fs["inv"], m - 1)
                            v.tensor_scalar(small[s][:, 0, :], mi[s][:, :, D], 1.0, None, ALU.max).then_inc(fs["clamped"], 1)
                            dve.wait_ge(fs["clamped"], m + 1)
                            v.reciprocal(small[s][:, 1, :], small[s][:, 0, :]).then_inc(fs["recip"], 1)
                            dve.wait_ge(fs["recip"], m + 1)
                            v.tensor_tensor(tmp[s][:, :, :], mi[s][:, :, 0:D],
                                            small[s][:, 1, :].rearrange("p (k o) -> p k o", o=1).to_broadcast([P, ROWS, D]),
                                            ALU.mult).then_inc(fs["scaled"], 1)
                            dve.wait_ge(fs["scaled"], m + 1)
                            dve.sem_inc(node_taken, 1)
                            v.tensor_tensor(xn[s][:, :, :], tmp[s][:, :, :], xi[s][:, :, :], ALU.add).then_inc(node_x, 1)
                            dve.wait_ge(node_x, xbase + m + 1)
                        if kind == "l2":
                            v.tensor_scalar(small[s][:, 0, :], mi[s][:, :, D + 1], -1.0, gmax[:, 0:1], ALU.mult,
                                            ALU.add).then_inc(fs["gap"], 1)
                            dve.wait_ge(fs["gap"], m + 1)
                            v.tensor_scalar(small[s][:, 1, :], small[s][:, 0, :], 0.0, 80.0, ALU.max, ALU.min).then_inc(fs["gap2"], 1)
                            dve.wait_ge(fs["expd"], m + 1)
                            v.scalar_tensor_tensor(small[s][:, 3, :], small[s][:, 2, :], 1e-10, mi[s][:, :, D], ALU.mult,
                                                   ALU.add).then_inc(fs["den"], 1)
                            dve.wait_ge(fs["den"], m + 1)
                            v.reciprocal(small[s][:, 4, :], small[s][:, 3, :]).then_inc(fs["recip"], 1)
                            dve.wait_ge(fs["recip"], m + 1)
                            v.tensor_tensor(tmp[s][:, :, :], mi[s][:, :, 0:D],
                                            small[s][:, 4, :].rearrange("p (k o) -> p k o", o=1).to_broadcast([P, ROWS, D]),
                                            ALU.mult).then_inc(fs["scaled"], 1)
                            dve.wait_ge(fs["scaled"], m + 1)
                            dve.sem_inc(node_taken, 1)
                            dve.wait_ge(fs[f"h2_in{s}"], h * 16 + 16)
                            if not first:
                                dve.wait_ge(fs["yt"], m - 1)
                            v.tensor_tensor(y[s][:, :, :], tmp[s][:, :, :], hi[s][:, :, :], ALU.add).then_inc(fs["y"], 1)

                    def finish_x(m, s, h, first):
                        if kind == "l2":
                            dve.wait_ge(fs["zs"], m + 1)
                            v.tensor_tensor(lr[s][:, :, :].rearrange("p k f -> p (k f)"), ps_z[s][:, 0:ROWS * D],
                                            tmp[s][:, :, :].rearrange("p k f -> p (k f)"), ALU.max).then_inc(fs["lrelu"], 1)
                            dve.wait_ge(fs["lrelu"], m + 1)
                            v.tensor_tensor(xn[s][:, :, :], lr[s][:, :, :], xi[s][:, :, :], ALU.add).then_inc(node_x, 1)
                            dve.wait_ge(node_x, xbase + m + 1)

                    def center(m, s, h, first):
                        v.tensor_reduce(total[s][:, :], xn[s][:, :, :], AX, ALU.add).then_inc(node_sum, 1)
                        dve.wait_ge(node_sum, base + m + 1)
                        if not first:
                            dve.wait_ge(node_norm, base + m - 1)
                        v.scalar_tensor_tensor(cent[s][:, :, :], total[s][:, :].rearrange("p (k o) -> p k o", o=1).to_broadcast([P, ROWS, D]),
                                               -1.0 / D, xn[s][:, :, :], ALU.mult, ALU.add).then_inc(node_cent, 1)

                    def spread(m, s, h, first):
                        dve.wait_ge(node_sq, base + m + 1)
                        v.tensor_reduce(var[s][:, :], sq[s][:, :, :], AX, ALU.add).then_inc(node_var, 1)
                        dve.wait_ge(node_var, base + m + 1)
                        if not first:
                            dve.wait_ge(node_rstd, base + m - 1)
                        v.tensor_scalar(vare[s][:, :], var[s][:, :], 1.0 / D, LN_EPS, ALU.mult, ALU.add).then_inc(node_eps, 1)

                    if kind == "l2":
                        pipeline(dve, NCHUNKS, [(front, 0), (finish_x, 1), (center, 1), (spread, 2)])
                    else:
                        pipeline(dve, NCHUNKS, [(front, 0), (center, 0), (spread, 1)])
                    if kind == "l1":
                        dve.wait_ge(fs["inv"], NCHUNKS)
                        v.tensor_tensor(inv_deg2[:, :, :], inv_deg[:, :, :], inv_deg[:, :, :], ALU.mult).then_inc(consts, 1)
                        dve.wait_ge(consts, 1)

                @block.scalar
                def _(act):
                    def expd(m, s, h, first):
                        act.wait_ge(fs["gap2"], m + 1)
                        if not first:
                            act.wait_ge(fs["den"], m - 1)
                        nc.scalar.activation(small[s][:, 2, :], small[s][:, 1, :], ACT.Exp).then_inc(fs["expd"], 1)

                    def turn_y(m, s, h, first):
                        act.wait_ge(fs["yt"], m + 1)
                        if not first:
                            act.wait_ge(fs["z"], m - 1)
                        nc.scalar.copy(yt[s][:, :], ps_yt[:, 0:ROWS * D]).then_inc(fs["ytc"], 1)

                    def slope(m, s, h, first):
                        act.wait_ge(fs["z"], m + 1)
                        nc.scalar.activation(tmp[s][:, :, :].rearrange("p k f -> p (k f)"), ps_z[s][:, 0:ROWS * D], ACT.Copy,
                                             scale=0.2).then_inc(fs["zs"], 1)

                    def square(m, s, h, first):
                        act.wait_ge(node_cent, base + m + 1)
                        if not first:
                            act.wait_ge(node_var, base + m - 1)
                        nc.scalar.activation(sq[s][:, :, :], cent[s][:, :, :], ACT.Square).then_inc(node_sq, 1)

                    def relu(m, s, h, first):
                        act.wait_ge(node_norm, base + m + 1)
                        if not first:
                            act.wait_ge(node_h_out[s], h * 16 + hb)
                            if kind == "l2":
                                act.wait_ge(fs["g"], m - 1)
                        nc.scalar.activation(hn[s][:, :, :], norm[s][:, :, :], ACT.Relu).then_inc(node_h, 1)

                    if kind == "l2":
                        pipeline(act, NCHUNKS, [(expd, 0), (turn_y, 0), (slope, 0), (square, 1), (relu, 2)])
                    else:
                        pipeline(act, NCHUNKS, [(square, 0), (relu, 1)])

                if kind == "l2":
                    @block.tensor
                    def _(pe):
                        pe.wait_ge(consts, 16)

                        def turn(m, s, h, first):
                            await_in_loop(pe, fs["y"], m + 1)
                            if not (first and m == 0):
                                await_in_loop(pe, fs["ytc"], m)
                            for j in range(ROWS // 2):
                                ins = nc.tensor.transpose(ps_yt[:, j * P:(j + 1) * P],
                                                          y[s][:, 2 * j:2 * j + 2, :].rearrange("p k f -> p (k f)"), eye[:, :])
                            ins.then_inc(fs["yt"], 1)

                        def project(m, s, h, first):
                            await_in_loop(pe, fs["ytc"], m + 1)
                            if not first:
                                await_in_loop(pe, fs["lrelu"], m - 1)
                            for j in range(ROWS // 2):
                                ins = nc.tensor.matmul(ps_z[s][:, j * P:(j + 1) * P], yt[s][:, j * P:(j + 1) * P], w2_sb[:, :],
                                                       start=True, stop=True)
                            ins.then_inc(fs["z"], 1)

                        pipeline(pe, NCHUNKS, [(turn, 0), (project, 0)])
            node_base[0] += NCHUNKS
            in_base[0] += 16 * loads * (NCHUNKS // 2)
            if kind != "first":
                x_out_base[0] += 16 * (NCHUNKS // 2)
            h_out_base[0] += 16 * (NCHUNKS // 2)

        node_pass("first", x, None, h0)
        if "first" in debug:
            return

        with ExitStack() as c:
            c.enter_context(nc.cleanup_on_exit())
            cat = [sb_in(c, f"cat{s}", [P, K, 2 * D + 2]) for s in range(2)]
            hd = [sb_in(c, f"hd{s}", [P, K, D]) for s in range(2)]
            at_edge = [sb_in(c, f"at_edge{s}", [P, K], i32) for s in range(2)]
            at_src = [sb_in(c, f"at_src{s}", [P, K], i32) for s in range(2)]
            xside = [sb_in(c, f"xside{q}", [P, CHUNK]) for q in range(2)]
            clamped = [sb_in(c, f"clamped{q}", [P, 2, CHUNK]) for q in range(2)]
            expd = [sb_in(c, f"expd{q}", [P, 2, CHUNK]) for q in range(2)]
            logd = [sb_in(c, f"logd{q}", [P, 2, CHUNK]) for q in range(2)]
            soft = [[sb_in(c, f"soft{q}{s}", [P, 2, CHUNK]) for s in range(2)] for q in range(2)]
            lrow = [sb_in(c, f"lrow{s}", [HEADS, CHUNK]) for s in range(2)]
            w0_sb = sb_in(c, "w0_sb", [P, 2 * P])
            att_sb = sb_in(c, "att_sb", [P, 4, HEADS])
            zeros = sb_in(c, "zeros", [P, TILES])
            ps_in_side = [ps_in(c, f"in_side{q}", [P, CHUNK]) for q in range(2)]
            ps_side = [ps_in(c, f"side{q}", [P, 2, CHUNK]) for q in range(2)]
            ps_logit = ps_in(c, "logit", [HEADS, CHUNK])
            a_const = sem_in(c, "a_const")
            a_zero = sem_in(c, "a_zero")
            zero_out = sem_in(c, "zero_out")
            a_index = sem_in(c, "a_index")
            rec_in = [sem_in(c, f"rec_in{s}") for s in range(2)]
            hd_in = [sem_in(c, f"hd_in{s}") for s in range(2)]
            a_turned = [sem_in(c, f"a_turned{q}") for q in range(2)]
            a_edge_rows = sem_in(c, "a_edge_rows")
            a_side = [sem_in(c, f"a_side{q}") for q in range(2)]
            a_proj = [sem_in(c, f"a_proj{q}") for q in range(2)]
            a_clamp = [sem_in(c, f"a_clamp{q}") for q in range(2)]
            a_exp = [sem_in(c, f"a_exp{q}") for q in range(2)]
            a_log = [sem_in(c, f"a_log{q}") for q in range(2)]
            a_soft = [sem_in(c, f"a_soft{q}") for q in range(2)]
            a_logit = sem_in(c, "a_logit")
            a_lrow = sem_in(c, "a_lrow")
            a_kept = sem_in(c, "a_kept")
            sp_out = [sem_in(c, f"sp_out{s}") for s in range(2)]
            lg_out = [sem_in(c, f"lg_out{s}") for s in range(2)]
            block = c.enter_context(nc.Block())
            v = nc.vector

            @block.sync
            def _(sp):
                sp.dma_start(w0_sb[:, :], w0).then_inc(a_const, 16)
                sp.dma_start(att_sb[:, :, :].rearrange("p q h -> p (q h)"), att).then_inc(a_const, 16)
                await_in_loop(sp, a_zero, 1)
                tables = ((msg0, D), (msg1, D + 1), (msg2, D + 2), (hop0, D), (hop1, D))
                for table, width in tables:
                    sp.dma_start(table.rearrange("(p a) f -> p (a f)", p=P).rearrange("p (w a) -> p w a", a=TILES),
                                 zeros[:, :].rearrange("p (o a) -> p o a", o=1).to_broadcast([P, width, TILES])).then_inc(zero_out, 16)

                def store(m, s, h, first):
                    await_in_loop(sp, a_soft[1], m + 1)
                    sp.dma_start(sp_j.rearrange("c b p e -> c p b e")[bass.ds(m, 1), :, :, :].rearrange("o p b e -> (o p) b e"),
                                 soft[1][s][:, :, :]).then_inc(sp_out[s], 16)
                    await_in_loop(sp, a_lrow, m + 1)
                    sp.dma_start(logits[:, bass.ds(m * CHUNK, CHUNK)], lrow[s][:, :]).then_inc(lg_out[s], 16)

                pipeline(sp, CHUNKS, [(store, 0)])
                await_in_loop(sp, zero_out, 16 * len(tables))
                for s in range(2):
                    await_in_loop(sp, sp_out[s], 16 * (CHUNKS // 2))
                    await_in_loop(sp, lg_out[s], 16 * (CHUNKS // 2))

            @block.gpsimd
            def _(pool):
                def ends(m, s, h, first):
                    await_in_loop(pool, a_index, m + 1)
                    if not first:
                        await_in_loop(pool, a_kept, m - 1)
                        await_in_loop(pool, a_turned[0], m - 1)
                    for k in range(K):
                        pool.indirect_dma_start(cat[s].bitcast(i32)[:, k, D:2 * D + 2], None, rec,
                                                bass.IndirectOffsetOnAxis(at_edge[s][:, k:k + 1], 0)).then_inc(rec_in[s], 16)
                    for k in range(K):
                        pool.indirect_dma_start(cat[s][:, k, 0:D], None, h0,
                                                bass.IndirectOffsetOnAxis(at_src[s][:, k:k + 1], 0)).then_inc(rec_in[s], 16)

                def other_end(m, s, h, first):
                    await_in_loop(pool, rec_in[s], h * (32 * K) + 32 * K)
                    if not first:
                        await_in_loop(pool, a_turned[1], m - 1)
                    for k in range(K):
                        pool.indirect_dma_start(hd[s][:, k, :], None, h0,
                                                bass.IndirectOffsetOnAxis(cat[s].bitcast(i32)[:, k, 2 * D:2 * D + 1], 0)).then_inc(hd_in[s], 16)

                pipeline(pool, CHUNKS, [(ends, 0), (other_end, 1)])

            @block.tensor
            def _(pe):
                pe.wait_ge(a_const, 32)

                def turn(m, s, h, first):
                    await_in_loop(pe, rec_in[s], h * (32 * K) + 32 * K)
                    if not (first and m == 0):
                        await_in_loop(pe, a_side[0], m)
                        await_in_loop(pe, a_edge_rows, m)
                    for k in range(K):
                        ins = nc.tensor.transpose(ps_in_side[0][:, k * P:(k + 1) * P], cat[s][:, k, 0:2 * D], eye[:, :])
                    ins.then_inc(a_turned[0], 1)
                    await_in_loop(pe, hd_in[s], h * (16 * K) + 16 * K)
                    if not (first and m == 0):
                        await_in_loop(pe, a_side[1], m)
                    for k in range(K):
                        ins = nc.tensor.transpose(ps_in_side[1][0:D, k * P:(k + 1) * P], hd[s][:, k, :], eye[:, :])
                    ins.then_inc(a_turned[1], 1)

                def project(m, s, h, first):
                    for q in range(2):
                        await_in_loop(pe, a_side[q], m + 1)
                        if q == 1:
                            await_in_loop(pe, a_edge_rows, m + 1)
                        if not (first and m == 0):
                            await_in_loop(pe, a_soft[q], m)
                        for b in range(2):
                            ins = nc.tensor.matmul(ps_side[q][:, b, :], w0_sb[:, b * P:(b + 1) * P], xside[q][:, :],
                                                   start=True, stop=True)
                        ins.then_inc(a_proj[q], 1)

                def logit(m, s, h, first):
                    await_in_loop(pe, a_soft[1], m + 1)
                    await_in_loop(pe, a_soft[0], m + 1)
                    if not (first and m == 0):
                        await_in_loop(pe, a_lrow, m)
                    for n in range(4):
                        ins = nc.tensor.matmul(ps_logit[:, :], att_sb[:, n, :], soft[n // 2][s][:, n % 2, :],
                                               start=(n == 0), stop=(n == 3))
                    ins.then_inc(a_logit, 1)

                pipeline(pe, CHUNKS, [(turn, 0), (project, 0), (logit, 1)])

            @block.scalar
            def _(act):
                nc.scalar.preload_act_table_set("natural_log_exp_and_others")

                def index(m, s, h, first):
                    if not first:
                        act.wait_ge(rec_in[s], h * (32 * K))
                    nc.scalar.copy(at_edge[s][:, :], edge_of[:, bass.ds(m * K, K)])
                    nc.scalar.copy(at_src[s][:, :], src_of[:, bass.ds(m * K, K)]).then_inc(a_index, 1)

                def sides(m, s, h, first):
                    act.wait_ge(a_turned[0], m + 1)
                    if not (first and m == 0):
                        act.wait_ge(a_proj[0], m)
                    nc.scalar.copy(xside[0][:, :], ps_in_side[0][:, :]).then_inc(a_side[0], 1)
                    if not (first and m == 0):
                        act.wait_ge(a_proj[1], m)
                    nc.scalar.copy(xside[1][D:2 * D, :], ps_in_side[0][D:2 * D, :]).then_inc(a_edge_rows, 1)

                def softplus(m, s, h, first):
                    for q in range(2):
                        act.wait_ge(a_clamp[q], m + 1)
                        nc.scalar.activation(expd[q][:, :, :], clamped[q][:, :, :], ACT.Exp).then_inc(a_exp[q], 1)
                        act.wait_ge(a_exp[q], m + 1)
                        if not (first and m == 0):
                            act.wait_ge(a_soft[q], m)
                        nc.scalar.activation(logd[q][:, :, :], expd[q][:, :, :], ACT.Ln, bias=1.0).then_inc(a_log[q], 1)

                def keep(m, s, h, first):
                    act.wait_ge(rec_in[s], h * (32 * K) + 32 * K)
                    act.wait_ge(hd_in[s], h * (16 * K) + 16 * K)
                    ends_of = cat[s].bitcast(i32)
                    nc.scalar.copy(dst_of[:, bass.ds(m * K, K)], ends_of[:, :, 2 * D])
                    nc.scalar.copy(type_of[:, bass.ds(m * K, K)], ends_of[:, :, 2 * D + 1]).then_inc(a_kept, 1)

                def logit_row(m, s, h, first):
                    act.wait_ge(a_logit, m + 1)
                    if not first:
                        act.wait_ge(lg_out[s], h * 16)
                    nc.scalar.copy(lrow[s][:, :], ps_logit[:, :]).then_inc(a_lrow, 1)

                pipeline(act, CHUNKS, [(index, 0), (keep, 1), (sides, 1), (softplus, 1), (logit_row, 2)])

            @block.vector
            def _(dve):
                v.memset(zeros[:, :], 0.0).then_inc(a_zero, 1)

                def side(m, s, h, first):
                    dve.wait_ge(a_turned[1], m + 1)
                    if not (first and m == 0):
                        dve.wait_ge(a_proj[1], m)
                    v.tensor_copy(xside[1][0:D, :], ps_in_side[1][0:D, :]).then_inc(a_side[1], 1)

                def softplus(m, s, h, first):
                    for q in range(2):
                        dve.wait_ge(a_proj[q], m + 1)
                        if not (first and m == 0):
                            dve.wait_ge(a_exp[q], m)
                        v.tensor_scalar(clamped[q][:, :, :], ps_side[q][:, :, :], CLAMP, None, ALU.min).then_inc(a_clamp[q], 1)
                    for q in range(2):
                        dve.wait_ge(a_log[q], m + 1)
                        if not first:
                            dve.wait_ge(a_logit, m - 1)
                            if q == 1:
                                dve.wait_ge(sp_out[s], h * 16)
                        v.tensor_tensor(soft[q][s][:, :, :], logd[q][:, :, :], ps_side[q][:, :, :], ALU.max).then_inc(a_soft[q], 1)

                pipeline(dve, CHUNKS, [(side, 0), (softplus, 0)])

        if "l0a" in debug:
            return

        with ExitStack() as c:
            c.enter_context(nc.cleanup_on_exit())
            def t(name):
                return sb_in(c, "m_" + name, [P, SEG_LEN])

            z, cont, contn, s1, s2, s3, s4 = (t(n) for n in ("z", "cont", "contn", "s1", "s2", "s3", "s4"))
            col = sb_in(c, "m_col", [P, 16])
            row = sb_in(c, "m_row", [1, 8, P])
            one = sb_in(c, "m_one", [1, 1])
            sh = sb_in(c, "m_sh", [P, P])
            gb = sb_in(c, "m_gb", [P, 2])
            trow = sb_in(c, "m_trow", [P, 4, P])
            ps_t = ps_in(c, "m_t", [P, 4, P])
            ps_s = ps_in(c, "m_s", [P, 512])
            ps_r = ps_in(c, "m_r", [1, 512])
            ps_b = ps_in(c, "m_b", [P, 512])
            m_in = sem_in(c, "m_in")
            m_types = sem_in(c, "m_types")
            m_trow = sem_in(c, "m_trow")
            m_out = sem_in(c, "m_out")
            m_masked = sem_in(c, "m_masked")
            m_first = sem_in(c, "m_first")
            m_dve = sem_in(c, "m_dve")
            m_to_act = sem_in(c, "m_to_act")
            m_from_act = sem_in(c, "m_from_act")
            m_to_pe = sem_in(c, "m_to_pe")
            m_from_pe = sem_in(c, "m_from_pe")
            m_done = sem_in(c, "m_done")
            block = c.enter_context(nc.Block())
            v = nc.vector
            PADS = N - (SEGS - 1) * SEG_LEN

            @block.sync
            def _(sp):
                sp.dma_start(z[:, :], logits.rearrange("h (c e) -> c h e", c=SEGS)).then_inc(m_in, 16)
                for i, tile in enumerate((cont, contn)):
                    sp.dma_start(tile[:, :], same_src[i:i + NPAD].rearrange("(c o e) -> c o e", c=SEGS, o=1).to_broadcast([SEGS, HEADS, SEG_LEN])).then_inc(m_in, 16)
                sp.dma_start(sh[:, :], samehead).then_inc(m_in, 16)
                sp.dma_start(gb[:, 0:1], gamma).then_inc(m_in, 16)
                sp.dma_start(gb[:, 1:2], beta).then_inc(m_in, 16)
                await_in_loop(sp, m_trow, 1)
                sp.dma_start(types_row[0:3 * P, :].rearrange("(j t) p -> t j p", j=3), trow[:, 0:3, :]).then_inc(m_out, 16)
                sp.dma_start(types_row[3 * P:TILES, :], trow[0:TILES - 3 * P, 3, :]).then_inc(m_out, 16)
                await_in_loop(sp, m_done, 1)
                sp.dma_start(weights.rearrange("h (c e) -> c h e", c=SEGS), z[:, :]).then_inc(m_out, 16)
                await_in_loop(sp, m_out, 48)

            @block.gpsimd
            def _(pool):
                pool.memset(one[:, :], 1.0).then_inc(m_types, 1)
                pool.wait_ge(m_first, 1)
                pool.affine_select(out=s1[:, PADS:SEG_LEN], in_=s1[:, PADS:SEG_LEN], compare_op=ALU.is_ge, fill=0.0,
                                   base=P - HEADS - 1, pattern=[[0, SEG_LEN - PADS]], channel_multiplier=-1).then_inc(m_masked, 1)
                pool.wait_ge(m_first, 2)
                pool.affine_select(out=s2[:, PADS:SEG_LEN], in_=s2[:, PADS:SEG_LEN], compare_op=ALU.is_ge, fill=0.0,
                                   base=P - HEADS - 1, pattern=[[0, SEG_LEN - PADS]], channel_multiplier=-1).then_inc(m_masked, 1)

            @block.tensor
            def _(pe):
                for j in range(4):
                    w = min(P, TILES - j * P)
                    ins = nc.tensor.transpose(ps_t[0:w, j, :], type_of[:, j * P:j * P + w], eye[:, :])
                ins.then_inc(m_from_pe, 1)
                pe.wait_ge(m_in, 96)
                for n in range(2):
                    pe.wait_ge(m_to_pe, n + 1)
                    nc.tensor.matmul(ps_s[:, n:n + 1], sh[:, :], col[:, n:n + 1], start=True, stop=True).then_inc(m_from_pe, 1)
                pe.wait_ge(m_types, 1)
                for n in range(4):
                    pe.wait_ge(m_to_pe, 2 * n + 3)
                    nc.tensor.transpose(ps_r[:, 0:P], col[:, 8:9], eye[:, :])
                    nc.tensor.transpose(ps_r[:, P:2 * P], col[:, 9:10], eye[:, :]).then_inc(m_from_pe, 1)
                    pe.wait_ge(m_to_pe, 2 * n + 4)
                    nc.tensor.matmul(ps_b[:, n:n + 1], row[:, 3, :], one[:, :], start=True, stop=True).then_inc(m_from_pe, 1)

            @block.scalar
            def _(act):
                n = [0]

                def do(o, i, f, **kw):
                    n[0] += 1
                    act.wait_ge(m_to_act, n[0])
                    nc.scalar.activation(o, i, f, **kw).then_inc(m_from_act, 1)

                act.wait_ge(m_from_pe, 1)
                nc.scalar.copy(trow[:, 0:3, :], ps_t[:, 0:3, :])
                nc.scalar.copy(trow[0:TILES - 3 * P, 3, :], ps_t[0:TILES - 3 * P, 3, :]).then_inc(m_trow, 1)
                do(s2[:, :], s1[:, :], ACT.Exp)
                do(s3[:, :], s2[:, :], ACT.Ln, bias=1.0)
                do(s3[:, :], s2[:, :], ACT.Square)
                do(col[:, 4:5], col[:, 3:4], ACT.Sqrt)
                do(s2[:, :], s1[:, :], ACT.Exp)
                do(s3[:, :], s2[:, :], ACT.Ln, bias=1.0)
                do(s3[:, :], s2[:, :], ACT.Exp)

            @block.vector
            def _(dve):
                cnt = {"v": 0, "a": 0, "p": 1, "pe": 0}

                def op(ins):
                    cnt["v"] += 1
                    ins.then_inc(m_dve, 1)
                    dve.wait_ge(m_dve, cnt["v"])

                def to_act(n=1):
                    for _ in range(n):
                        dve.sem_inc(m_to_act, 1)
                        cnt["a"] += 1
                        dve.wait_ge(m_from_act, cnt["a"])

                def to_pe():
                    dve.sem_inc(m_to_pe, 1)
                    cnt["p"] += 1
                    dve.wait_ge(m_from_pe, cnt["p"])

                dve.wait_ge(m_in, 96)
                dve.wait_ge(m_types, 1)

                def softplus():
                    op(v.tensor_scalar(s1[:, :], z[:, :], CLAMP, None, ALU.min))
                    to_act(2)
                    op(v.tensor_tensor(s1[:, :], s3[:, :], z[:, :], ALU.max))

                softplus()
                dve.sem_inc(m_first, 1)
                dve.wait_ge(m_masked, 1)
                op(v.tensor_reduce(col[:, 0:1], s1[:, :], AX, ALU.add))
                to_pe()
                op(v.tensor_scalar(col[:, 2:3], ps_s[:, 0:1], -1.0 / N, None, ALU.mult))
                op(v.tensor_scalar(s2[:, :], s1[:, :], col[:, 2:3], None, ALU.add))
                dve.sem_inc(m_first, 1)
                dve.wait_ge(m_masked, 2)
                to_act()
                op(v.tensor_reduce(col[:, 1:2], s3[:, :], AX, ALU.add))
                to_pe()
                op(v.tensor_scalar(col[:, 3:4], ps_s[:, 1:2], 1.0 / N, LN_EPS, ALU.mult, ALU.add))
                to_act()
                op(v.reciprocal(col[:, 5:6], col[:, 4:5]))
                op(v.tensor_tensor(col[:, 6:7], col[:, 5:6], gb[:, 0:1], ALU.mult))
                op(v.tensor_scalar(z[:, :], s2[:, :], col[:, 6:7], gb[:, 1:2], ALU.mult, ALU.add))
                softplus()

                def scan(o, keep, add, op1, n, reverse):
                    view = (lambda a: a[:, ::-1]) if reverse else (lambda a: a[:, :])
                    end = slice(0, 1) if reverse else slice(SEG_LEN - 1, SEG_LEN)
                    op(v.tensor_tensor_scan(view(o), view(keep), view(add), 0.0, ALU.mult, op1))
                    op(v.tensor_copy(col[:, 8:9], o[:, end]))
                    op(v.tensor_reduce(col[:, 9:10], keep[:, :], AX, ALU.min))
                    to_pe()
                    op(v.tensor_copy(row[:, 0:2, :].rearrange("p a b -> p (a b)"), ps_r[:, 0:2 * P]))
                    op(v.memset(row[:, 2:4, :], 0.0))
                    for h in range(HEADS):
                        def stretches(i, lo, hi, r=reverse):
                            a = row[:, i, :].rearrange("p (c h) -> p h c", h=HEADS)[:, h, lo:hi]
                            return a[:, ::-1] if r else a
                        op(v.tensor_tensor_scan(stretches(2, 0, SEGS), stretches(1, 0, SEGS), stretches(0, 0, SEGS), 0.0, ALU.mult, op1))
                        to, of = ((0, SEGS - 1), (1, SEGS)) if reverse else ((1, SEGS), (0, SEGS - 1))
                        op(v.tensor_copy(stretches(3, *to, r=False), stretches(2, *of, r=False)))
                    to_pe()
                    op(v.tensor_copy(col[:, 10:11], ps_b[:, n:n + 1]))
                    op(v.tensor_tensor_scan(view(o), view(keep), view(add), col[:, 10:11], ALU.mult, op1))

                scan(s2, cont, s1, ALU.max, 0, False)
                op(v.tensor_scalar(s3[:, :], contn[:, :], -1.0, 1.0, ALU.mult, ALU.add))
                op(v.tensor_tensor(s3[:, :], s3[:, :], s2[:, :], ALU.mult))
                scan(s4, contn, s3, ALU.add, 1, True)
                op(v.tensor_tensor(s2[:, :], s1[:, :], s4[:, :], ALU.subtract))
                to_act()
                scan(s2, cont, s3, ALU.add, 2, False)
                op(v.tensor_scalar(s1[:, :], contn[:, :], -1.0, 1.0, ALU.mult, ALU.add))
                op(v.tensor_tensor(s1[:, :], s1[:, :], s2[:, :], ALU.mult))
                scan(s4, contn, s1, ALU.add, 3, True)
                op(v.tensor_scalar(s4[:, :], s4[:, :], 1e-16, None, ALU.add))
                op(v.reciprocal(s2[:, :], s4[:, :]))
                op(v.scalar_tensor_tensor(z[:, :], s3[:, :], 1.0 / HEADS, s2[:, :], ALU.mult, ALU.mult))
                dve.sem_inc(m_done, 1)

        if "soft" in debug:
            return

        with ExitStack() as c:
            c.enter_context(nc.cleanup_on_exit())
            sj = [sb_in(c, f"sj{s}", [P, 2, CHUNK]) for s in range(2)]
            wr = [sb_in(c, f"wr{s}", [HEADS, CHUNK]) for s in range(2)]
            ct = [sb_in(c, f"ct{s}", [D, CHUNK]) for s in range(2)]
            wm = [sb_in(c, f"wm{s}", [P, 2, CHUNK]) for s in range(2)]
            run = [sb_in(c, f"c_run{s}", [D, CHUNK]) for s in range(2)]
            rows_sb = [sb_in(c, f"c_rows{s}", [P, K, D]) for s in range(2)]
            at_out = [sb_in(c, f"c_at_out{s}", [P, K], i32) for s in range(2)]
            hs_sb = sb_in(c, "hs_sb", [HEADS, 2, P])
            hsum_sb = sb_in(c, "hsum_sb", [P, D])
            ps_w = [ps_in(c, f"w{s}", [P, 2, CHUNK]) for s in range(2)]
            ps_m = [ps_in(c, f"m{s}", [D, CHUNK]) for s in range(2)]
            ps_back = [ps_in(c, f"c_back{s}", [P, CHUNK]) for s in range(2)]
            c_const = sem_in(c, "c_const")
            c_in = [sem_in(c, f"c_in{s}") for s in range(2)]
            c_spread = sem_in(c, "c_spread")
            c_weighed = sem_in(c, "c_weighed")
            c_msg = sem_in(c, "c_msg")
            c_run = sem_in(c, "c_run")
            c_back = sem_in(c, "c_back")
            c_rows = sem_in(c, "c_rows")
            c_out = [sem_in(c, f"c_out{s}") for s in range(2)]
            block = c.enter_context(nc.Block())
            v = nc.vector

            @block.sync
            def _(sp):
                sp.dma_start(hs_sb[:, :, :].rearrange("h b p -> h (b p)"), headsel).then_inc(c_const, 16)
                sp.dma_start(hsum_sb[:, :], headsum).then_inc(c_const, 16)

                def load(m, s, h, first):
                    if not first:
                        await_in_loop(sp, c_weighed, m - 1)
                        await_in_loop(sp, c_run, m - 1)
                    sp.dma_start(sj[s][:, :, :], sp_j.rearrange("c b p e -> c p b e")[bass.ds(m, 1), :, :, :].rearrange("o p b e -> (o p) b e")).then_inc(c_in[s], 16)
                    sp.dma_start(wr[s][:, :], weights[:, bass.ds(m * CHUNK, CHUNK)]).then_inc(c_in[s], 16)
                    sp.dma_start(ct[s][:, :], same_src[bass.ds(m * CHUNK, CHUNK)].rearrange("(o e) -> o e", o=1).to_broadcast([D, CHUNK])).then_inc(c_in[s], 16)

                pipeline(sp, CHUNKS, [(load, 0)])

            @block.tensor
            def _(pe):
                pe.wait_ge(c_const, 32)

                def spread(m, s, h, first):
                    await_in_loop(pe, c_in[s], h * 48 + 48)
                    if not first:
                        await_in_loop(pe, c_weighed, m - 1)
                    for b in range(2):
                        ins = nc.tensor.matmul(ps_w[s][:, b, :], hs_sb[:, b, :], wr[s][:, :], start=True, stop=True)
                    ins.then_inc(c_spread, 1)

                def join(m, s, h, first):
                    await_in_loop(pe, c_weighed, m + 1)
                    if not first:
                        await_in_loop(pe, c_run, m - 1)
                    for b in range(2):
                        ins = nc.tensor.matmul(ps_m[s][:, :], hsum_sb[:, :], wm[s][:, b, :], start=(b == 0), stop=(b == 1))
                    ins.then_inc(c_msg, 1)

                def turn_back(m, s, h, first):
                    await_in_loop(pe, c_run, m + 1)
                    if not first:
                        await_in_loop(pe, c_rows, m - 1)
                    for k in range(K):
                        ins = nc.tensor.transpose(ps_back[s][:, k * D:(k + 1) * D], run[s][:, k * P:(k + 1) * P], eye[0:D, 0:D])
                    ins.then_inc(c_back, 1)

                pipeline(pe, CHUNKS, [(spread, 0), (join, 1), (turn_back, 2)])

            @block.vector
            def _(dve):
                def weigh(m, s, h, first):
                    dve.wait_ge(c_spread, m + 1)
                    if not first:
                        dve.wait_ge(c_msg, m - 1)
                    v.tensor_tensor(wm[s][:, :, :], sj[s][:, :, :], ps_w[s][:, :, :], ALU.mult).then_inc(c_weighed, 1)

                def scan(m, s, h, first):
                    dve.wait_ge(c_msg, m + 1)
                    dve.wait_ge(c_in[s], h * 48 + 48)
                    if not first:
                        dve.wait_ge(c_back, m - 1)
                    if not (first and m == 0):
                        dve.wait_ge(c_run, m)
                    start = 0.0 if first and m == 0 else run[1 - s][:, CHUNK - 1:CHUNK]
                    v.tensor_tensor_scan(run[s][:, :], ct[s][:, :], ps_m[s][:, :], start, ALU.mult, ALU.add).then_inc(c_run, 1)

                pipeline(dve, CHUNKS, [(weigh, 0), (scan, 1)])

            @block.scalar
            def _(act):
                def rows(m, s, h, first):
                    act.wait_ge(c_back, m + 1)
                    if not first:
                        act.wait_ge(c_out[s], h * (16 * K))
                    nc.scalar.copy(at_out[s][:, :], out_src[:, bass.ds(m * K, K)])
                    nc.scalar.copy(rows_sb[s][:, :, :].rearrange("p k f -> p (k f)"), ps_back[s][:, 0:K * D]).then_inc(c_rows, 1)

                pipeline(act, CHUNKS, [(rows, 2)])

            @block.gpsimd
            def _(pool):
                def scatter(m, s, h, first):
                    await_in_loop(pool, c_rows, m + 1)
                    for k in range(K):
                        pool.indirect_dma_start(msg0, bass.IndirectOffsetOnAxis(at_out[s][:, k:k + 1], 0), rows_sb[s][:, k, :],
                                                None, bounds_check=NPAD - 1, oob_is_err=False).then_inc(c_out[s], 16)

                pipeline(pool, CHUNKS, [(scatter, 2)])
                for s in range(2):
                    pool.wait_ge(c_out[s], 16 * K * (CHUNKS // 2))

        node_pass("l0", x, x1, h1)
        if "l0" in debug:
            return

        seg_in = [sem(f"seg_in{s}") for s in range(2)]
        seg_flags = [sem(f"seg_flags{s}") for s in range(2)]
        seg_index = sem("seg_index")
        seg_turned = sem("seg_turned")
        seg_run = sem("seg_run")
        seg_back = sem("seg_back")
        seg_rows = sem("seg_rows")
        seg_out = [sem(f"seg_out{s}") for s in range(2)]
        seg_ones = sem("seg_ones")
        passes = [0]

        def sum_by_dst(name, table, target, width):
            base = passes[0] * CHUNKS
            half = passes[0] * 16 * (CHUNKS // 2)
            with ExitStack() as c:
                c.enter_context(nc.cleanup_on_exit())
                got = [sb_in(c, f"got_{name}{s}", [P, K, width]) for s in range(2)]
                at_in = [sb_in(c, f"at_in_{name}{s}", [P, K], i32) for s in range(2)]
                at_out = [sb_in(c, f"at_out_{name}{s}", [P, K], i32) for s in range(2)]
                ct = [sb_in(c, f"ct_{name}{s}", [80, CHUNK]) for s in range(2)]
                run = [sb_in(c, f"run_{name}{s}", [width, CHUNK]) for s in range(2)]
                rows_sb = [sb_in(c, f"rows_{name}{s}", [P, K, width]) for s in range(2)]
                ps_v = [ps_in(c, f"v_{name}{s}", [P, CHUNK]) for s in range(2)]
                ps_back = [ps_in(c, f"back_{name}{s}", [P, CHUNK]) for s in range(2)]
                block = c.enter_context(nc.Block())
                v = nc.vector

                @block.sync
                def _(sp):
                    def flags(m, s, h, first):
                        if not first:
                            await_in_loop(sp, seg_run, base + m - 1)
                        sp.dma_start(ct[s][:, :], same_dst[bass.ds(m * CHUNK, CHUNK)].rearrange("(o e) -> o e", o=1).to_broadcast([80, CHUNK])).then_inc(seg_flags[s], 16)

                    pipeline(sp, CHUNKS, [(flags, 0)])

                @block.gpsimd
                def _(pool):
                    if width > D:
                        for s in range(2):
                            pool.memset(got[s][:, :, :], 1.0).then_inc(seg_ones, 1)
                        pool.wait_ge(seg_ones, 2)

                    def gather(m, s, h, first):
                        await_in_loop(pool, seg_index, base + m + 1)
                        if not first:
                            await_in_loop(pool, seg_turned, base + m - 1)
                        for k in range(K):
                            pool.indirect_dma_start(got[s][:, k, 0:D], None, table,
                                                    bass.IndirectOffsetOnAxis(at_in[s][:, k:k + 1], 0)).then_inc(seg_in[s], 16)

                    def scatter(m, s, h, first):
                        await_in_loop(pool, seg_rows, base + m + 1)
                        for k in range(K):
                            pool.indirect_dma_start(target, bass.IndirectOffsetOnAxis(at_out[s][:, k:k + 1], 0), rows_sb[s][:, k, :],
                                                    None, bounds_check=NPAD - 1, oob_is_err=False).then_inc(seg_out[s], 16)

                    pipeline(pool, CHUNKS, [(gather, 0), (scatter, 2)])
                    for s in range(2):
                        pool.wait_ge(seg_out[s], K * half + 16 * K * (CHUNKS // 2))

                @block.tensor
                def _(pe):
                    def turn(m, s, h, first):
                        await_in_loop(pe, seg_in[s], h * (16 * K) + (K * half + 16 * K))
                        if not first:
                            await_in_loop(pe, seg_run, base + m - 1)
                        for k in range(K):
                            ins = nc.tensor.transpose(ps_v[s][0:width, k * P:(k + 1) * P], got[s][:, k, :], eye[:, :])
                        ins.then_inc(seg_turned, 1)

                    def turn_back(m, s, h, first):
                        await_in_loop(pe, seg_run, base + m + 1)
                        if not first:
                            await_in_loop(pe, seg_rows, base + m - 1)
                        for k in range(K):
                            ins = nc.tensor.transpose(ps_back[s][:, k * width:(k + 1) * width], run[s][:, k * P:(k + 1) * P],
                                                      eye[0:width, 0:width])
                        ins.then_inc(seg_back, 1)

                    pipeline(pe, CHUNKS, [(turn, 0), (turn_back, 1)])

                @block.vector
                def _(dve):
                    def scan(m, s, h, first):
                        dve.wait_ge(seg_turned, base + m + 1)
                        dve.wait_ge(seg_flags[s], h * 16 + (half + 16))
                        if not first:
                            dve.wait_ge(seg_back, base + m - 1)
                        if not (first and m == 0):
                            dve.wait_ge(seg_run, base + m)
                        start = 0.0 if first and m == 0 else run[1 - s][:, CHUNK - 1:CHUNK]
                        v.tensor_tensor_scan(run[s][:, :], ct[s][0:width, :], ps_v[s][0:width, :], start, ALU.mult,
                                             ALU.add).then_inc(seg_run, 1)

                    pipeline(dve, CHUNKS, [(scan, 0)])

                @block.scalar
                def _(act):
                    def index(m, s, h, first):
                        if not first:
                            act.wait_ge(seg_in[s], h * (16 * K) + K * half)
                        nc.scalar.copy(at_in[s][:, :], from_dst[:, bass.ds(m * K, K)]).then_inc(seg_index, 1)

                    def rows(m, s, h, first):
                        act.wait_ge(seg_back, base + m + 1)
                        if not first:
                            act.wait_ge(seg_out[s], h * (16 * K) + K * half)
                        nc.scalar.copy(at_out[s][:, :], out_dst[:, bass.ds(m * K, K)])
                        nc.scalar.copy(rows_sb[s][:, :, :].rearrange("p k f -> p (k f)"), ps_back[s][:, 0:K * width]).then_inc(seg_rows, 1)

                    pipeline(act, CHUNKS, [(index, 0), (rows, 1)])
            passes[0] += 1

        sum_by_dst("mean", h1, msg1, D + 1)
        node_pass("l1", x1, x2, h2)
        if "l1" in debug:
            return

        with ExitStack() as c:
            c.enter_context(nc.cleanup_on_exit())
            hs = [sb_in(c, f"hs{s}", [P, K, D]) for s in range(2)]
            hd = [sb_in(c, f"b_hd{s}", [P, K, D + 1]) for s in range(2)]
            at_src = [sb_in(c, f"b_at_src{s}", [P, K], i32) for s in range(2)]
            at_dst = [sb_in(c, f"b_at_dst{s}", [P, K], i32) for s in range(2)]
            at_out = [sb_in(c, f"b_at_out{s}", [P, K], i32) for s in range(2)]
            ct = [sb_in(c, f"b_ct{s}", [80, CHUNK]) for s in range(2)]
            ty = [sb_in(c, f"b_ty{s}", [D, CHUNK]) for s in range(2)]
            hot = sb_in(c, "hot", [D, CHUNK])
            gate = sb_in(c, "gate", [D, CHUNK])
            prod = sb_in(c, "prod", [D, CHUNK])
            pen = sb_in(c, "pen", [D + 1, CHUNK])
            top = [sb_in(c, f"top{s}", [D + 1, CHUNK + 1]) for s in range(2)]
            drop = sb_in(c, "drop", [D + 1, CHUNK])
            drop2 = sb_in(c, "drop2", [D + 1, CHUNK])
            less = sb_in(c, "less", [D + 1, CHUNK])
            decay = sb_in(c, "decay", [D + 1, CHUNK])
            grow = sb_in(c, "grow", [D + 1, CHUNK])
            val = sb_in(c, "val", [D + 1, CHUNK])
            run = [sb_in(c, f"b_run{s}", [D + 1, CHUNK]) for s in range(2)]
            rows_sb = [sb_in(c, f"b_rows{s}", [P, K, D + 2]) for s in range(2)]
            rel_sb = sb_in(c, "rel_sb", [D, D])
            ones = sb_in(c, "ones", [D, P])
            maxima = sb_in(c, "maxima", [P, CHUNKS])
            ps_g = ps_in(c, "g", [D, CHUNK])
            ps_t = ps_in(c, "b_t", [D + 1, CHUNK])
            ps_s = ps_in(c, "b_s", [P, CHUNK])
            ps_back = [ps_in(c, f"b_back{s}", [P, CHUNK]) for s in range(2)]
            b_const = sem_in(c, "b_const")
            b_in = [sem_in(c, f"b_in{s}") for s in range(2)]
            b_flags = [sem_in(c, f"b_flags{s}") for s in range(2)]
            b_index = sem_in(c, "b_index")
            names = ("hot", "pre", "turned", "gate", "prod", "score", "pen", "link", "top", "drop", "drop2", "less",
                     "decay", "grow", "val", "max", "run", "back", "rows")
            b = {n: sem_in(c, "b_" + n) for n in names}
            b_out = [sem_in(c, f"b_out{s}") for s in range(2)]
            block = c.enter_context(nc.Block())
            v = nc.vector

            @block.sync
            def _(sp):
                sp.dma_start(rel_sb[:, :], rel).then_inc(b_const, 16)

                def load(m, s, h, first):
                    if not first:
                        await_in_loop(sp, b["pen"], m - 1)
                        await_in_loop(sp, b["hot"], m - 1)
                    sp.dma_start(ct[s][:, :], same_src[bass.ds(m * CHUNK, CHUNK)].rearrange("(o e) -> o e", o=1).to_broadcast([80, CHUNK])).then_inc(b_flags[s], 16)
                    sp.dma_start(ty[s][:, :], types_row.rearrange("t p -> (t p)")[bass.ds(m * CHUNK, CHUNK)].rearrange("(o e) -> o e", o=1).to_broadcast([D, CHUNK])).then_inc(b_flags[s], 16)

                pipeline(sp, CHUNKS, [(load, 0)])

            @block.gpsimd
            def _(pool):
                for s in range(2):
                    pool.memset(hd[s][:, :, :], 1.0).then_inc(b_const, 1)
                    pool.memset(top[s][:, :], 0.0).then_inc(b_const, 1)
                pool.memset(ones[:, :], 1.0).then_inc(b_const, 1)
                pool.memset(maxima[:, :], -BIG).then_inc(b_const, 1)
                pool.wait_ge(b_const, 22)

                def gather(m, s, h, first):
                    await_in_loop(pool, b_index, m + 1)
                    if not first:
                        await_in_loop(pool, b["turned"], m - 1)
                    for k in range(K):
                        pool.indirect_dma_start(hs[s][:, k, :], None, h2,
                                                bass.IndirectOffsetOnAxis(at_src[s][:, k:k + 1], 0)).then_inc(b_in[s], 16)
                    for k in range(K):
                        pool.indirect_dma_start(hd[s][:, k, 0:D], None, h2,
                                                bass.IndirectOffsetOnAxis(at_dst[s][:, k:k + 1], 0)).then_inc(b_in[s], 16)

                def scatter(m, s, h, first):
                    await_in_loop(pool, b["rows"], m + 1)
                    for k in range(K):
                        pool.indirect_dma_start(msg2, bass.IndirectOffsetOnAxis(at_out[s][:, k:k + 1], 0), rows_sb[s][:, k, :],
                                                None, bounds_check=NPAD - 1, oob_is_err=False).then_inc(b_out[s], 16)

                pipeline(pool, CHUNKS, [(gather, 0), (scatter, 2)])
                for s in range(2):
                    pool.wait_ge(b_out[s], 16 * K * (CHUNKS // 2))

            @block.tensor
            def _(pe):
                pe.wait_ge(b_const, 22)

                def ends(m, s, h, first):
                    await_in_loop(pe, b["hot"], m + 1)
                    await_in_loop(pe, b_in[s], h * (32 * K) + 32 * K)
                    if not (first and m == 0):
                        await_in_loop(pe, b["gate"], m)
                        await_in_loop(pe, b["val"], m)
                    nc.tensor.matmul(ps_g[:, :], rel_sb[:, :], hot[:, :], start=True, stop=False)
                    for k in range(K):
                        ins = nc.tensor.matmul(ps_g[:, k * P:(k + 1) * P], hs[s][:, k, :], eye[:, :], start=False, stop=(k == K - 1))
                    ins.then_inc(b["pre"], 1)
                    for k in range(K):
                        ins = nc.tensor.transpose(ps_t[:, k * P:(k + 1) * P], hd[s][:, k, :], eye[:, :])
                    ins.then_inc(b["turned"], 1)

                def score(m, s, h, first):
                    await_in_loop(pe, b["prod"], m + 1)
                    if not (first and m == 0):
                        await_in_loop(pe, b["less"], m)
                        await_in_loop(pe, b["max"], m)
                    nc.tensor.matmul(ps_s[:, :], ones[:, :], prod[:, :], start=True, stop=True).then_inc(b["score"], 1)

                def turn_back(m, s, h, first):
                    await_in_loop(pe, b["run"], m + 1)
                    await_in_loop(pe, b["top"], m + 1)
                    if not first:
                        await_in_loop(pe, b["rows"], m - 1)
                    for k in range(K):
                        nc.tensor.transpose(ps_back[s][:, k * (D + 2):k * (D + 2) + D + 1], run[s][:, k * P:(k + 1) * P],
                                            eye[0:D + 1, 0:D + 1])
                        ins = nc.tensor.transpose(ps_back[s][:, k * (D + 2) + D + 1:(k + 1) * (D + 2)],
                                                  top[s][0:1, 1 + k * P:1 + (k + 1) * P], eye[0:1, 0:1])
                    ins.then_inc(b["back"], 1)

                pipeline(pe, CHUNKS, [(ends, 0), (score, 0), (turn_back, 1)])

            @block.vector
            def _(dve):
                dve.wait_ge(b_const, 22)

                def types(m, s, h, first):
                    dve.wait_ge(b_flags[s], h * 32 + 32)
                    if not (first and m == 0):
                        dve.wait_ge(b["pre"], m)
                    v.tensor_scalar(hot[:, :], ty[s][:, :], pid[0:D, 0:1], None, ALU.is_equal).then_inc(b["hot"], 1)

                def attend(m, s, h, first):
                    zero = first and m == 0
                    dve.wait_ge(b["gate"], m + 1)
                    dve.wait_ge(b["turned"], m + 1)
                    if not zero:
                        dve.wait_ge(b["score"], m)
                    v.tensor_tensor(prod[:, :], gate[:, :], ps_t[0:D, :], ALU.mult).then_inc(b["prod"], 1)
                    dve.wait_ge(b["pen"], m + 1)
                    dve.wait_ge(b["score"], m + 1)
                    if not first:
                        dve.wait_ge(b["back"], m - 1)
                    if not zero:
                        dve.wait_ge(b["top"], m)
                        dve.wait_ge(b["link"], m + 1 if False else m)
                    start = -BIG if zero else top[1 - s][:, CHUNK:CHUNK + 1]
                    v.tensor_tensor_scan(top[s][:, 1:CHUNK + 1], pen[:, :], ps_s[0:D + 1, :], start, ALU.add,
                                         ALU.max).then_inc(b["top"], 1)
                    dve.wait_ge(b["top"], m + 1)
                    v.tensor_tensor(less[:, :], ps_s[0:D + 1, :], top[s][:, 1:CHUNK + 1], ALU.subtract).then_inc(b["less"], 1)
                    dve.wait_ge(b["link"], m + 1)
                    v.tensor_tensor(drop[:, :], top[s][:, 0:CHUNK], top[s][:, 1:CHUNK + 1], ALU.subtract).then_inc(b["drop"], 1)
                    dve.wait_ge(b["drop"], m + 1)
                    if not zero:
                        dve.wait_ge(b["decay"], m)
                    v.tensor_tensor(drop2[:, :], drop[:, :], pen[:, :], ALU.add).then_inc(b["drop2"], 1)
                    real = LAST_REAL if isinstance(m, int) and m == CHUNKS - 1 else CHUNK
                    v.tensor_reduce(maxima[:, bass.ds(m, 1)], ps_s[:, 0:real], AX, ALU.max).then_inc(b["max"], 1)
                    dve.wait_ge(b["grow"], m + 1)
                    if not zero:
                        dve.wait_ge(b["run"], m)
                    v.tensor_tensor(val[:, :], grow[:, :], ps_t[:, :], ALU.mult).then_inc(b["val"], 1)
                    dve.wait_ge(b["val"], m + 1)
                    dve.wait_ge(b["decay"], m + 1)
                    start = 0.0 if zero else run[1 - s][:, CHUNK - 1:CHUNK]
                    v.tensor_tensor_scan(run[s][:, :], decay[:, :], val[:, :], start, ALU.mult, ALU.add).then_inc(b["run"], 1)

                pipeline(dve, CHUNKS, [(types, 0), (attend, 0)], peel_last=True)
                dve.wait_ge(b["max"], CHUNKS)
                v.tensor_reduce(gmax[:, :], maxima[:, :], AX, ALU.max).then_inc(b["max"], 1)
                dve.wait_ge(b["max"], CHUNKS + 1)

            @block.scalar
            def _(act):
                act.wait_ge(b_const, 22)

                def index(m, s, h, first):
                    if not first:
                        act.wait_ge(b_in[s], h * (32 * K))
                    nc.scalar.copy(at_src[s][:, :], src_of[:, bass.ds(m * K, K)])
                    nc.scalar.copy(at_dst[s][:, :], dst_of[:, bass.ds(m * K, K)]).then_inc(b_index, 1)

                def attend(m, s, h, first):
                    zero = first and m == 0
                    act.wait_ge(b_flags[s], h * 32 + 32)
                    if not zero:
                        act.wait_ge(b["drop2"], m)
                        act.wait_ge(b["top"], m)
                    nc.scalar.activation(pen[:, :], ct[s][0:D + 1, :], ACT.Copy, scale=BIG, bias=-BIG).then_inc(b["pen"], 1)
                    act.wait_ge(b["pre"], m + 1)
                    if not zero:
                        act.wait_ge(b["prod"], m)
                    nc.scalar.activation(gate[:, :], ps_g[:, :], ACT.Tanh).then_inc(b["gate"], 1)
                    if zero:
                        act.sem_inc(b["link"], 1)
                    else:
                        act.wait_ge(b["top"], m)
                        nc.scalar.copy(top[s][:, 0:1], top[1 - s][:, CHUNK:CHUNK + 1]).then_inc(b["link"], 1)
                    act.wait_ge(b["less"], m + 1)
                    if not zero:
                        act.wait_ge(b["val"], m)
                    nc.scalar.activation(grow[:, :], less[:, :], ACT.Exp).then_inc(b["grow"], 1)
                    act.wait_ge(b["drop2"], m + 1)
                    if not zero:
                        act.wait_ge(b["run"], m)
                    nc.scalar.activation(decay[:, :], drop2[:, :], ACT.Exp).then_inc(b["decay"], 1)

                def rows(m, s, h, first):
                    act.wait_ge(b["back"], m + 1)
                    if not first:
                        act.wait_ge(b_out[s], h * (16 * K))
                    nc.scalar.copy(at_out[s][:, :], out_src[:, bass.ds(m * K, K)])
                    nc.scalar.copy(rows_sb[s][:, :, :].rearrange("p k f -> p (k f)"), ps_back[s][:, 0:K * (D + 2)]).then_inc(b["rows"], 1)

                pipeline(act, CHUNKS, [(index, 0), (attend, 0), (rows, 1)])

        node_pass("l2", x2, x3, feat)
        if "l2" in debug:
            return

        sum_by_dst("hop0", g0, hop0, D)

        with ExitStack() as c:
            c.enter_context(nc.cleanup_on_exit())
            gi = [sb_in(c, f"gi{s}", [P, ROWS, D]) for s in range(2)]
            go = [sb_in(c, f"go{s}", [P, ROWS, D]) for s in range(2)]
            g_in = [sem_in(c, f"g_in{s}") for s in range(2)]
            g_scaled = sem_in(c, "g_scaled")
            g_out = [sem_in(c, f"g_out{s}") for s in range(2)]
            block = c.enter_context(nc.Block())

            @block.sync
            def _(sp):
                def load(m, s, h, first):
                    if not first:
                        await_in_loop(sp, g_scaled, m - 1)
                    sp.dma_start(gi[s][:, :, :].rearrange("p k (o f) -> p o (k f)", o=1), rows_of(hop0, m)).then_inc(g_in[s], 16)

                pipeline(sp, NCHUNKS, [(load, 0)])

            @block.scalar
            def _(act):
                def store(m, s, h, first):
                    act.wait_ge(g_scaled, m + 1)
                    act.dma_start(rows_of(g1, m), go[s][:, :, :].rearrange("p k (o f) -> p o (k f)", o=1)).then_inc(g_out[s], 16)

                pipeline(act, NCHUNKS, [(store, 0)])
                for s in range(2):
                    act.wait_ge(g_out[s], 16 * (NCHUNKS // 2))

            @block.vector
            def _(dve):
                def scale(m, s, h, first):
                    dve.wait_ge(g_in[s], h * 16 + 16)
                    if not first:
                        dve.wait_ge(g_out[s], h * 16)
                    nc.vector.tensor_tensor(go[s][:, :, :], gi[s][:, :, :],
                                            inv_deg2[:, bass.ds(m, 1), :].rearrange("p o k -> p k o").to_broadcast([P, ROWS, D]),
                                            ALU.mult).then_inc(g_scaled, 1)

                pipeline(dve, NCHUNKS, [(scale, 0)])

        sum_by_dst("hop1", g1, hop1, D)

        with ExitStack() as c:
            c.enter_context(nc.cleanup_on_exit())
            xi = [sb_in(c, f"o_xi{s}", [P, ROWS, D]) for s in range(2)]
            hi = [sb_in(c, f"o_hi{s}", [P, ROWS, D]) for s in range(2)]
            both = [sb_in(c, f"both{s}", [P, ROWS, 2 * D]) for s in range(2)]
            bt = [sb_in(c, f"bt{s}", [P, ROWS * P]) for s in range(2)]
            xb = [sb_in(c, f"o_xb{s}", [P, ROWS, D]) for s in range(2)]
            oo = [sb_in(c, f"o_oo{s}", [P, ROWS, D]) for s in range(2)]
            w3_sb = sb_in(c, "w3_sb", [P, D])
            bsum = sb_in(c, "bsum", [P, D])
            ps_bt = ps_in(c, "bt", [P, ROWS * P])
            ps_o = [ps_in(c, f"o{s}", [P, ROWS * D]) for s in range(2)]
            o_const = sem_in(c, "o_const")
            o_in = [sem_in(c, f"o_in{s}") for s in range(2)]
            o = {n: sem_in(c, "o_" + n) for n in ("scaled", "biased", "turned", "copied", "prod", "sum")}
            o_out = [sem_in(c, f"o_out{s}") for s in range(2)]
            block = c.enter_context(nc.Block())
            v = nc.vector

            @block.sync
            def _(sp):
                sp.dma_start(w3_sb[:, :], w3).then_inc(o_const, 16)
                sp.dma_start(b3_b[:, 0, :], b3.to_broadcast([P, D])).then_inc(o_const, 16)
                sp.dma_start(b3_b[:, 1, :], br3.to_broadcast([P, D])).then_inc(o_const, 16)

                def load(m, s, h, first):
                    if not first:
                        await_in_loop(sp, o["scaled"], m - 1)
                        await_in_loop(sp, o["biased"], m - 1)
                        await_in_loop(sp, o["turned"], m - 1)
                    sp.dma_start(hi[s][:, :, :].rearrange("p k (o f) -> p o (k f)", o=1), rows_of(hop1, m)).then_inc(o_in[s], 16)
                    sp.dma_start(xi[s][:, :, :].rearrange("p k (o f) -> p o (k f)", o=1), rows_of(x3, m)).then_inc(o_in[s], 16)
                    sp.dma_start(both[s][:, :, D:2 * D], feat.rearrange("(c p k) f -> c p k f", p=P, k=ROWS)[bass.ds(m, 1), :, :, :].rearrange("o p k f -> (o p) k f")).then_inc(o_in[s], 16)

                def store(m, s, h, first):
                    await_in_loop(sp, o["sum"], m + 1)
                    sp.dma_start(rows_of(out, m), oo[s][:, :, :].rearrange("p k (o f) -> p o (k f)", o=1)).then_inc(o_out[s], 16)

                pipeline(sp, NCHUNKS, [(load, 0), (store, 1)])
                for s in range(2):
                    await_in_loop(sp, o_out[s], 16 * (NCHUNKS // 2))

            @block.gpsimd
            def _(pool):
                pool.wait_ge(o_const, 48)
                pool.tensor_tensor(bsum[:, :], b3_b[:, 0, :], b3_b[:, 1, :], ALU.add).then_inc(o_const, 1)
                pool.wait_ge(o_const, 49)

                def bias(m, s, h, first):
                    await_in_loop(pool, o_in[s], h * 48 + 48)
                    if not first:
                        await_in_loop(pool, o["sum"], m - 1)
                    pool.tensor_tensor(xb[s][:, :, :], xi[s][:, :, :],
                                       bsum[:, :].rearrange("p (o f) -> p o f", o=1).to_broadcast([P, ROWS, D]), ALU.add).then_inc(o["biased"], 1)

                pipeline(pool, NCHUNKS, [(bias, 0)])

            @block.vector
            def _(dve):
                def scale(m, s, h, first):
                    dve.wait_ge(o_in[s], h * 48 + 48)
                    if not first:
                        dve.wait_ge(o["turned"], m - 1)
                    v.tensor_tensor(both[s][:, :, 0:D], hi[s][:, :, :],
                                    inv_deg[:, bass.ds(m, 1), :].rearrange("p o k -> p k o").to_broadcast([P, ROWS, D]),
                                    ALU.mult).then_inc(o["scaled"], 1)

                def add(m, s, h, first):
                    dve.wait_ge(o["prod"], m + 1)
                    dve.wait_ge(o["biased"], m + 1)
                    if not first:
                        dve.wait_ge(o_out[s], h * 16)
                    v.tensor_tensor(oo[s][:, :, :].rearrange("p k f -> p (k f)"), ps_o[s][:, :],
                                    xb[s][:, :, :].rearrange("p k f -> p (k f)"), ALU.add).then_inc(o["sum"], 1)

                pipeline(dve, NCHUNKS, [(scale, 0), (add, 1)])

            @block.scalar
            def _(act):
                def copy(m, s, h, first):
                    act.wait_ge(o["turned"], m + 1)
                    if not first:
                        act.wait_ge(o["prod"], m - 1)
                    nc.scalar.copy(bt[s][:, :], ps_bt[:, :]).then_inc(o["copied"], 1)

                pipeline(act, NCHUNKS, [(copy, 0)])

            @block.tensor
            def _(pe):
                pe.wait_ge(o_const, 48)

                def turn(m, s, h, first):
                    await_in_loop(pe, o_in[s], h * 48 + 48)
                    await_in_loop(pe, o["scaled"], m + 1)
                    if not (first and m == 0):
                        await_in_loop(pe, o["copied"], m)
                    for k in range(ROWS):
                        ins = nc.tensor.transpose(ps_bt[:, k * P:(k + 1) * P], both[s][:, k, :], eye[:, :])
                    ins.then_inc(o["turned"], 1)

                def project(m, s, h, first):
                    await_in_loop(pe, o["copied"], m + 1)
                    if not first:
                        await_in_loop(pe, o["sum"], m - 1)
                    for k in range(ROWS):
                        ins = nc.tensor.matmul(ps_o[s][:, k * D:(k + 1) * D], bt[s][:, k * P:(k + 1) * P], w3_sb[:, :],
                                               start=True, stop=True)
                    ins.then_inc(o["prod"], 1)

                pipeline(pe, NCHUNKS, [(turn, 0), (project, 0)])




_CONSTS = {}


def _layouts(a):
    import numpy as np

    f = np.float32
    def pad(t, n, fill):
        full = np.full((n,) + t.shape[1:], fill, t.dtype)
        full[:t.shape[0]] = t
        return full
    src, dst, typ = (np.asarray(a[k]).astype(np.int32) for k in ("src", "dst", "edge_type_64"))
    ea = np.ascontiguousarray(a["edge_attr_64"])
    rec = np.concatenate([pad(ea, NPAD, 0).view(np.int32), pad(dst, NPAD, N)[:, None], pad(typ, NPAD, 0)[:, None]], 1)
    att = np.asarray(a["L0_gnn_att"])
    att_sel = np.zeros((P, 4, HEADS), f)
    for side in range(2):
        for b in range(2):
            for hh in range(2):
                att_sel[hh * D:(hh + 1) * D, 2 * side + b, 2 * b + hh] = att[0, 2 * b + hh, side * D:(side + 1) * D]
    headsel = np.zeros((HEADS, 2, P), f)
    for h in range(HEADS):
        headsel[h, h // 2, (h % 2) * D:(h % 2 + 1) * D] = 1
    headsum = np.concatenate([np.eye(D, dtype=f)] * 2, 0)
    q = np.arange(P)
    samehead = (q[:, None] % HEADS == q[None] % HEADS).astype(f)
    w2 = np.zeros((P, P), f)
    for b in range(2):
        w2[b * D:(b + 1) * D, b * D:(b + 1) * D] = np.asarray(a["L2_gnn_W"]).T
    w3 = np.concatenate([np.asarray(a["L3_gnn_W"]).T, np.asarray(a["L3_gnn_Wr"]).T], 0)
    return {
        "x": pad(np.asarray(a["x"]), NPAD, 0), "rec": rec,
        "src": pad(src, SORT_N, N), "dst": pad(dst, SORT_N, N), "ident": np.eye(P, dtype=f),
        "w0": np.asarray(a["L0_gnn_W"]), "att": att_sel.reshape(P, 4 * HEADS), "bias0": np.asarray(a["L0_gnn_bias"])[None],
        "gamma": np.tile(np.asarray(a["L0_gnn_bn_gamma"]), SEGS)[:, None],
        "beta": np.tile(np.asarray(a["L0_gnn_bn_beta"]), SEGS)[:, None],
        "headsel": headsel.reshape(HEADS, 2 * P), "headsum": headsum, "samehead": samehead,
        "rel": np.asarray(a["L2_gnn_rel_embed"]), "w2": w2, "w3": w3,
        "b3": np.asarray(a["L3_gnn_b"])[None], "br3": np.asarray(a["L3_gnn_br"])[None],
    }


def kernel(**inputs):
    import numpy as _np
    import concourse.bacc as _bacc
    from concourse import mybir as _mybir
    from concourse.bass_utils import run_bass_kernel_spmd as _run

    nc = _bacc.Bacc("TRN2", target_bir_lowering=False, num_devices=1)
    arrays, args = {}, []
    for name, a in _layouts(inputs).items():
        a = _np.ascontiguousarray(a)
        arrays[f"in_{name}_dram"] = a
        args.append(nc.dram_tensor(f"in_{name}_dram", a.shape, _mybir.dt.from_np(a.dtype), kind="ExternalInput").ap())
    out = nc.dram_tensor("out_dram", (NPAD, D), _mybir.dt.float32, kind="ExternalOutput").ap()
    gnn_kernel(nc, *args, out)
    r = _run(nc, [arrays], core_ids=[0])
    return r.results[0]["out_dram"][:N]
```

```python
import concourse.bass as bass
from concourse import mybir
from contextlib import ExitStack

P = 128
D = 64
N = 50000
TILES = 392
NPAD = TILES * P
K = 4
CHUNK = K * P
CHUNKS = TILES // K
LAST_REAL = N - (CHUNKS - 1) * CHUNK
NS = 3
GS = 4
ROWS = 14
NCHUNKS = TILES // ROWS
SORT_N = 1 << 16
SORT_F = SORT_N // P
HEADS = 4
OOB = 200000.0
SPLIT = 32384
NEG_TOP = 0xFFFF - 0x80
POS_OFF = SPLIT - 0x80
BIG = 1e30
CLAMP = 30.0
LN_EPS = 1e-5
SEGS = 32
SEG_LEN = NPAD // SEGS

EDGE, SRC, OUT, DST = range(4)
D_SRC, D_OUT = range(2)

fp32 = mybir.dt.float32
bf16 = mybir.dt.bfloat16
i32 = mybir.dt.int32
u32 = mybir.dt.uint32
ALU = mybir.AluOpType
ACT = mybir.ActivationFunctionType
AX = mybir.AxisListType.X


def gnn_kernel(nc, x, rec, src, dst, ident, w0, att, bias0, gamma, beta, headsel, headsum, samehead,
               rel, w2, w3, b3, br3, out, debug=()):
    ctx = ExitStack()
    made = {}

    def dram(name, shape, dt=fp32):
        return nc.dram_tensor(name, shape, dt, kind="Internal").ap()

    h0 = dram("h0", (NPAD, D))
    h1 = dram("h1", (NPAD, D))
    h2 = dram("h2", (NPAD, D))
    x1 = dram("x1", (NPAD, D))
    x2 = dram("x2", (NPAD, D))
    x3 = dram("x3", (NPAD, D))
    feat = dram("feat", (NPAD, D))
    g0 = dram("g0", (NPAD, D))
    g1 = dram("g1", (NPAD, D))
    msg0 = dram("msg0", (NPAD, D))
    msg1 = dram("msg1", (NPAD, D + 1))
    msg2 = dram("msg2", (NPAD, D + 2))
    hop0 = dram("hop0", (NPAD, D))
    hop1 = dram("hop1", (NPAD, D))
    same_src = dram("same_src", (SORT_N,))
    same_dst = dram("same_dst", (SORT_N,))
    sp_j = dram("sp_j", (CHUNKS, 2, P, CHUNK))
    logits = dram("logits", (HEADS, NPAD))
    weights = dram("weights", (3, HEADS, NPAD), bf16)
    types_row = dram("types_row", (TILES, P))

    with ctx:
        def sb_in(c, name, shape, dt=fp32):
            return c.enter_context(nc.sbuf_tensor("sb_" + name, shape, dt))

        def ps_in(c, name, shape):
            return c.enter_context(nc.psum_tensor("ps_" + name, shape, fp32))

        def sem_in(c, name):
            return nc.alloc_semaphore(name=name)

        def sb(name, shape, dt=fp32):
            return sb_in(ctx, name, shape, dt)

        def sem(name):
            return ctx.enter_context(nc.semaphore(name))

        by_src = sb("by_src", [P, SORT_F, 4], i32)
        by_dst = sb("by_dst", [P, SORT_F, 2], i32)
        type_of = sb("type_of", [P, TILES])
        inv_deg = sb("inv_deg", [P, NCHUNKS, ROWS])
        eye = sb("eye", [P, P])
        pid = sb("pid", [P, 1])
        ready = sem("ready")

        def await_in_loop(eng, semaphore, value):
            eng.wait_ge(semaphore, value)
            eng.sem_inc(ready, 1)

        with ExitStack() as c:
            c.enter_context(nc.cleanup_on_exit())
            raw = [sb_in(c, "raw_src", [P, SORT_F], i32), sb_in(c, "raw_dst", [P, SORT_F], i32)]
            slot = sb_in(c, "slot", [P, SORT_F], i32)
            pidi = sb_in(c, "pidi", [P, 1], i32)
            signs_i = sb_in(c, "signs_i", [P, 8], i32)
            signs_t = sb_in(c, "signs_t", [P, 8], i32)
            signs = sb_in(c, "signs", [P, 8])
            key = [[sb_in(c, f"key{a}{b}", [P, SORT_F]) for b in range(2)] for a in range(2)]
            below = [sb_in(c, f"below{a}", [P, SORT_F]) for a in range(2)]
            work = [sb_in(c, f"work{a}", [P, SORT_F]) for a in range(2)]
            high = [sb_in(c, f"high{a}", [P, SORT_F], i32) for a in range(2)]
            node = [sb_in(c, f"node{a}", [P, SORT_F + 2]) for a in range(2)]
            same = [sb_in(c, f"same{a}", [P, SORT_F]) for a in range(2)]
            more = [sb_in(c, f"more{a}", [P, SORT_F]) for a in range(2)]
            dest = [sb_in(c, f"dest{a}", [P, SORT_F]) for a in range(2)]
            load_f = [sb_in(c, f"load_f{a}", [P, SORT_F]) for a in range(2)]
            turned = [ps_in(c, f"turned{a}", [P, 4, P]) for a in range(2)]
            final = [ps_in(c, f"final{n}", [P, 4, P]) for n in range(5)]
            loaded = sem_in(c, "loaded")
            counted = sem_in(c, "counted")
            chain = [sem_in(c, f"sort_chain{a}") for a in range(2)]
            signed = sem_in(c, "signed")
            handed = [sem_in(c, f"handed{a}") for a in range(2)]
            moved = [sem_in(c, f"moved{a}") for a in range(2)]
            back = [sem_in(c, f"back{a}") for a in range(2)]
            shifted = [sem_in(c, f"shifted{a}") for a in range(2)]
            flags_out = sem_in(c, "flags_out")
            decoded = [sem_in(c, f"decoded{a}") for a in range(2)]
            final_t = sem_in(c, "final_t")
            final_c = sem_in(c, "final_c")

            block = c.enter_context(nc.Block())
            FIRST_CROSS = 10
            TURNS = 2 * (17 - FIRST_CROSS)

            @block.sync
            def _(sp):
                sp.dma_start(raw[0][:, :], src.rearrange("(p f) -> p f", p=P)).then_inc(loaded, 16)
                sp.dma_start(raw[1][:, :], dst.rearrange("(p f) -> p f", p=P)).then_inc(loaded, 16)
                sp.dma_start(eye[:, :], ident).then_inc(loaded, 16)
                for a in range(2):
                    sp.wait_ge(decoded[a], 1)
                    sp.dma_start(node[a][1:P, 0:1], node[a][0:P - 1, SORT_F:SORT_F + 1]).then_inc(shifted[a], 16)
                    sp.dma_start(node[a][0:P - 1, SORT_F + 1:SORT_F + 2], node[a][1:P, 1:2]).then_inc(shifted[a], 16)
                for a, flags in enumerate((same_src, same_dst)):
                    sp.wait_ge(decoded[a], 2)
                    sp.dma_start(flags.rearrange("(p f) -> p f", p=P), same[a][:, :]).then_inc(flags_out, 16)
                sp.wait_ge(flags_out, 32)

            @block.gpsimd
            def _(pool):
                pool.iota(slot[:, :], pattern=[[1, SORT_F]], base=0, channel_multiplier=SORT_F).then_inc(counted, 1)
                pool.iota(pidi[:, :], pattern=[[0, 1]], base=0, channel_multiplier=1).then_inc(counted, 1)

            @block.vector
            def _(dve):
                v = nc.vector
                done = [0, 0]

                def link(a, ins):
                    done[a] += 1
                    ins.then_inc(chain[a], 1)

                def after(a):
                    if done[a]:
                        dve.wait_ge(chain[a], done[a])

                dve.wait_ge(counted, 2)
                v.tensor_copy(pid[:, :], pidi[:, :]).then_inc(signed, 1)
                v.tensor_scalar(signs_t[:, 0:1], pidi[:, :], 1, None, ALU.logical_shift_right).then_inc(signed, 1)
                dve.wait_ge(signed, 2)
                v.tensor_tensor(signs_t[:, 1:2], pidi[:, :], signs_t[:, 0:1], ALU.bitwise_xor).then_inc(signed, 1)
                dve.wait_ge(signed, 3)
                v.tensor_scalar(signs_i[:, 0:1], pidi[:, :], 1, None, ALU.bitwise_and).then_inc(signed, 1)
                for m in range(1, 8):
                    v.tensor_scalar(signs_i[:, m:m + 1], signs_t[:, 1:2], m - 1, 1, ALU.logical_shift_right,
                                    ALU.bitwise_and).then_inc(signed, 1)
                dve.wait_ge(signed, 11)
                v.tensor_scalar(signs[:, :], signs_i[:, :], -2.0, 1.0, ALU.mult, ALU.add).then_inc(signed, 1)
                dve.wait_ge(signed, 12)
                dve.wait_ge(loaded, 48)
                payload = [slot, raw[0]]
                for a in range(2):
                    link(a, v.tensor_scalar(below[a][:, :], raw[a][:, :], float(SPLIT), None, ALU.is_lt))
                    link(a, v.tensor_scalar(work[a][:, :], raw[a][:, :], -2.0, float(NEG_TOP + POS_OFF), ALU.mult, ALU.add))
                for a in range(2):
                    after(a)
                    link(a, v.tensor_tensor(work[a][:, :], work[a][:, :], below[a][:, :], ALU.mult))
                for a in range(2):
                    after(a)
                    link(a, v.scalar_tensor_tensor(high[a][:, :], raw[a][:, :], float(-POS_OFF), work[a][:, :],
                                                   ALU.add, ALU.add))
                for a in range(2):
                    after(a)
                    link(a, v.tensor_scalar(high[a][:, :], high[a][:, :], 16, None, ALU.logical_shift_left))
                for a in range(2):
                    after(a)
                    link(a, v.tensor_tensor(key[a][0].bitcast(i32)[:, :], high[a][:, :], payload[a][:, :], ALU.bitwise_or))

                def flip(a, b, lo_bit, lo, hi, w=2):
                    t = key[a][b][:, :].rearrange("p (g h l s) -> p g h l s", h=w, l=2, s=1 << lo_bit)[:, :, hi, lo, :]
                    link(a, v.tensor_scalar(t, t, -1.0, None, ALU.mult))

                at = [0, 0]
                turns = [0, 0]
                for a in range(2):
                    after(a)
                    flip(a, 0, 1, 1, 0)
                    flip(a, 0, 1, 1, 1)

                def stage(a, bit, last):
                    s, t = key[a][at[a]], key[a][1 - at[a]]
                    sv = s[:, :].rearrange("p (g two s) -> p g two s", two=2, s=1 << bit)
                    tv = t[:, :].rearrange("p (g two s) -> p g two s", two=2, s=1 << bit)
                    for side, op in ((0, ALU.min), (1, ALU.max)):
                        ins = v.tensor_tensor(tv[:, :, side, :], sv[:, :, 0, :], sv[:, :, 1, :], op)
                        if last:
                            ins.then_inc(handed[a], 1)
                        else:
                            link(a, ins)
                    at[a] = 1 - at[a]

                for k in range(1, 17):
                    if k >= FIRST_CROSS:
                        for bit in range(k - 1, 6, -1):
                            for a in range(2):
                                if bit == k - 1:
                                    dve.wait_ge(moved[a], turns[a] + 1)
                                    turns[a] += 1
                                    at[a] = 1 - at[a]
                                else:
                                    after(a)
                                stage(a, bit - 7, bit == 7)
                        low = 6
                    else:
                        low = k - 1
                    for bit in range(low, -1, -1):
                        for a in range(2):
                            if k >= FIRST_CROSS and bit == 6:
                                dve.wait_ge(moved[a], turns[a] + 1)
                                turns[a] += 1
                                at[a] = 1 - at[a]
                            else:
                                after(a)
                            stage(a, bit, False)
                    if k < 16:
                        for a in range(2):
                            after(a)
                            if k < 8:
                                flip(a, at[a], k, 1, 0)
                                flip(a, at[a], k, 0, 1)
                            else:
                                if k == 8:
                                    flip(a, at[a], 8, 1, 0, w=1)
                                    after(a)
                                ins = v.tensor_scalar(key[a][1 - at[a]][:, :], key[a][at[a]][:, :],
                                                      signs[:, k - 8:k - 7], None, ALU.mult)
                                at[a] = 1 - at[a]
                                if k + 1 >= FIRST_CROSS:
                                    ins.then_inc(handed[a], 2)
                                else:
                                    link(a, ins)
                for a in range(2):
                    after(a)
                    bits = key[a][at[a]].bitcast(i32)
                    link(a, v.tensor_scalar(high[a][:, :], bits[:, :], 16, None, ALU.logical_shift_right))
                    link(a, v.tensor_scalar(raw[a][:, :], bits[:, :], 0xFFFF, None, ALU.bitwise_and))
                    link(a, v.memset(node[a][:, :], -1.0))
                for a in range(2):
                    after(a)
                    link(a, v.tensor_scalar(below[a][:, :], high[a][:, :], 32768.0, None, ALU.is_ge))
                    link(a, v.tensor_scalar(work[a][:, :], high[a][:, :], -2.0, float(NEG_TOP - POS_OFF), ALU.mult, ALU.add))
                    link(a, v.tensor_copy(load_f[a][:, :], raw[a][:, :]))
                for a in range(2):
                    after(a)
                    link(a, v.tensor_tensor(work[a][:, :], work[a][:, :], below[a][:, :], ALU.mult))
                for a in range(2):
                    after(a)
                    v.scalar_tensor_tensor(node[a][:, 1:SORT_F + 1], high[a][:, :], float(POS_OFF), work[a][:, :],
                                           ALU.add, ALU.add).then_inc(decoded[a], 1)
                for a in range(2):
                    dve.wait_ge(decoded[a], 1)
                    dve.wait_ge(shifted[a], 32)
                    v.tensor_tensor(same[a][:, :], node[a][:, 1:SORT_F + 1], node[a][:, 0:SORT_F],
                                    ALU.is_equal).then_inc(decoded[a], 1)
                    link(a, v.tensor_tensor(more[a][:, :], node[a][:, 2:SORT_F + 2], node[a][:, 1:SORT_F + 1],
                                            ALU.is_equal))
                for a in range(2):
                    after(a)
                    v.scalar_tensor_tensor(dest[a][:, :], more[a][:, :], OOB, node[a][:, 1:SORT_F + 1],
                                           ALU.mult, ALU.add).then_inc(decoded[a], 1)

            FINALS = [(0, load_f[0], by_src[:, :, EDGE], 0), (0, node[0], by_src[:, :, SRC], 1),
                      (0, dest[0], by_src[:, :, OUT], 0), (1, load_f[1], by_dst[:, :, D_SRC], 0),
                      (1, dest[1], by_dst[:, :, D_OUT], 0)]

            @block.tensor
            def _(pe):
                pe.wait_ge(loaded, 48)
                pe.wait_ge(signed, 12)
                at = [0, 0]
                for k in range(1, 10):
                    at = [(b + k) % 2 for b in at]
                at = [(b + 2) % 2 for b in at]
                for k in range(FIRST_CROSS, 17):
                    for half in range(2):
                        n = 2 * (k - FIRST_CROSS) + half
                        for a in range(2):
                            pe.wait_ge(handed[a], 2 * n + 2)
                            if n:
                                pe.wait_ge(moved[a], n)
                            s = key[a][at[a]][:, :]
                            for j in range(4):
                                piece = s[:, j * P:(j + 1) * P] if half == 0 else \
                                    s.rearrange("p (q j) -> p j q", j=4)[:, j, :]
                                ins = nc.tensor.transpose(turned[a][:, j, :], piece, eye[:, :])
                            ins.then_inc(back[a], 1)
                            at[a] = 1 - at[a]
                            at[a] = (at[a] + (k - 7 if half == 0 else 7 + 1)) % 2
                for n, (a, source, _, off) in enumerate(FINALS):
                    pe.wait_ge(decoded[a], 3)
                    for j in range(4):
                        ins = nc.tensor.transpose(final[n][:, j, :], source[:, off + j * P:off + (j + 1) * P], eye[:, :])
                    ins.then_inc(final_t, 1)

            @block.scalar
            def _(act):
                at = [1, 1]
                for k in range(1, 10):
                    at = [(b + k) % 2 for b in at]
                at = [(b + 2) % 2 for b in at]
                for k in range(FIRST_CROSS, 17):
                    for half in range(2):
                        n = 2 * (k - FIRST_CROSS) + half
                        for a in range(2):
                            act.wait_ge(back[a], n + 1)
                            o = key[a][at[a]][:, :]
                            o = o.rearrange("p (q j) -> p j q", j=4) if half == 0 else \
                                o.rearrange("p (j q) -> p j q", j=4)
                            nc.scalar.copy(o, turned[a][:, :, :]).then_inc(moved[a], 1)
                            at[a] = 1 - at[a]
                            at[a] = (at[a] + (k - 7 if half == 0 else 7 + 1)) % 2
                for n, (_, _, target, _) in enumerate(FINALS):
                    act.wait_ge(final_t, n + 1)
                    nc.scalar.copy(target.rearrange("p (q j) -> p j q", j=4), final[n][:, :, :]).then_inc(final_c, 1)

        if "sort" in debug:
            return

        b3_b = sb("b3_b", [P, 2, D])
        gmax = sb("gmax", [P, 1])
        inv_deg2 = sb("inv_deg2", [P, NCHUNKS, ROWS])
        minus_half = sb("minus_half", [P, ROWS])

        def fresh(m, slots):
            return isinstance(m, int) and m < slots

        def pipeline(eng, count, parts, slots=2, peel_last=False):
            most = max(lag for _, lag in parts)
            low = (most + 2 * slots - 1) // slots * slots
            high = (count - 1 if peel_last else count) // slots * slots

            def straight(n):
                for f, lag in parts:
                    m = n - lag
                    if 0 <= m < count:
                        f(m, m % slots, m // slots, m < slots)

            for n in range(low):
                straight(n)
            with eng.Fori(low // slots, high // slots) as i:
                for r in range(slots):
                    for f, lag in parts:
                        s = (r - lag) % slots
                        f(i * slots + (r - lag), s, i + (r - lag - s) // slots, False)
            for n in range(high, count + most):
                straight(n)

        def times(s, slots):
            return (CHUNKS - s + slots - 1) // slots

        def rows_of(table, m, width=None):
            return table.rearrange("(c p k) f -> p c (k f)", p=P, k=ROWS)[:, bass.ds(m, 1), :]

        node_in = [sem(f"node_in{s}") for s in range(NS)]
        node_taken = sem("node_taken")
        node_x = sem("node_x")
        node_sum = sem("node_sum")
        node_cent = sem("node_cent")
        node_sq = sem("node_sq")
        node_var = sem("node_var")
        node_eps = sem("node_eps")
        node_rstd = sem("node_rstd")
        node_norm = sem("node_norm")
        node_h = sem("node_h")
        node_x_out = [sem(f"node_x_out{s}") for s in range(NS)]
        node_h_out = [sem(f"node_h_out{s}") for s in range(NS)]
        node_base = [0]
        in_base = [0] * NS
        x_out_base = [0] * NS
        h_out_base = [0] * NS

        def uses(s):
            return (NCHUNKS - s + NS - 1) // NS


        def node_pass(kind, x_in, x_new, h_new):
            base, ib, xb, hb = node_base[0], list(in_base), list(x_out_base), list(h_out_base)
            xbase = base - NCHUNKS
            with ExitStack() as c:
                c.enter_context(nc.cleanup_on_exit())
                xi = [sb_in(c, f"xi_{kind}{s}", [P, ROWS, D]) for s in range(NS)]
                width = {"first": 0, "l0": D, "l1": D + 1, "l2": D + 2}[kind]
                mi = [sb_in(c, f"mi_{kind}{s}", [P, ROWS, max(width, 1)]) for s in range(NS)]
                xn = xi if kind == "first" else [sb_in(c, f"xn_{kind}{s}", [P, ROWS, D]) for s in range(NS)]
                cent = [sb_in(c, f"cent_{kind}{s}", [P, ROWS, D]) for s in range(NS)]
                sq = [sb_in(c, f"sq_{kind}{s}", [P, ROWS, D]) for s in range(NS)]
                norm = [sb_in(c, f"norm_{kind}{s}", [P, ROWS, D]) for s in range(NS)]
                hn = [sb_in(c, f"hn_{kind}{s}", [P, ROWS, D]) for s in range(NS)]
                tmp = [sb_in(c, f"tmp_{kind}{s}", [P, ROWS, D]) for s in range(NS)]
                total = [sb_in(c, f"total_{kind}{s}", [P, ROWS]) for s in range(NS)]
                var = [sb_in(c, f"var_{kind}{s}", [P, ROWS]) for s in range(NS)]
                vare = [sb_in(c, f"vare_{kind}{s}", [P, ROWS]) for s in range(NS)]
                rstd = [sb_in(c, f"rstd_{kind}{s}", [P, ROWS]) for s in range(NS)]
                small = [sb_in(c, f"small_{kind}{s}", [P, 6, ROWS]) for s in range(NS)]
                fs = {n: sem_in(c, f"{kind}_{n}") for n in {
                    "first": (), "l0": (), "l1": ("clamped", "recip", "scaled", "inv"),
                    "l2": ("gap", "gap2", "expd", "den", "recip", "scaled", "y", "yt", "ytc", "z", "zs", "lrelu", "g",
                           *(f"h2_in{s}" for s in range(NS)), *(f"g_out{s}" for s in range(NS)))}[kind]}
                loads = 1 if kind == "first" else 2
                if kind == "l2":
                    hi = [sb_in(c, f"hi_{s}", [P, ROWS, D]) for s in range(NS)]
                    y = [sb_in(c, f"y_{s}", [P, ROWS, D]) for s in range(NS)]
                    yt = [sb_in(c, f"yt_{s}", [P, ROWS * D]) for s in range(NS)]
                    lr = [sb_in(c, f"lr_{s}", [P, ROWS, D]) for s in range(NS)]
                    gn = [sb_in(c, f"gn_{s}", [P, ROWS, D]) for s in range(NS)]
                    w2_sb = sb_in(c, "w2_sb", [P, P])
                    ps_yt = ps_in(c, "yt", [P, 1024])
                    ps_z = [ps_in(c, f"z{s}", [P, 1024]) for s in range(NS)]
                consts = sem_in(c, f"{kind}_consts")
                block = c.enter_context(nc.Block())
                v = nc.vector

                @block.sync
                def _(sp):
                    def load(m, s, h, first):
                        if not first:
                            await_in_loop(sp, node_cent, base + m + 1 - NS)
                            if loads == 2:
                                await_in_loop(sp, node_taken, xbase + m + 1 - NS)
                        sp.dma_start(xi[s][:, :, :].rearrange("p k (o f) -> p o (k f)", o=1), rows_of(x_in, m)).then_inc(node_in[s], 16)
                        if loads == 2:
                            table = {"l0": msg0, "l1": msg1, "l2": msg2}[kind]
                            sp.dma_start(mi[s][:, :, :].rearrange("p k (o f) -> p o (k f)", o=1), rows_of(table, m)).then_inc(node_in[s], 16)
                        if kind == "l2":
                            sp.dma_start(hi[s][:, :, :].rearrange("p k (o f) -> p o (k f)", o=1), rows_of(h2, m)).then_inc(fs[f"h2_in{s}"], 16)

                    def store_x(m, s, h, first):
                        await_in_loop(sp, node_x, xbase + m + 1)
                        sp.dma_start(rows_of(x_new, m), xn[s][:, :, :].rearrange("p k (o f) -> p o (k f)", o=1)).then_inc(node_x_out[s], 16)

                    def store_h(m, s, h, first):
                        await_in_loop(sp, node_h, base + m + 1)
                        sp.dma_start(rows_of(h_new, m), hn[s][:, :, :].rearrange("p k (o f) -> p o (k f)", o=1)).then_inc(node_h_out[s], 16)

                    def store_g(m, s, h, first):
                        await_in_loop(sp, fs["g"], m + 1)
                        sp.dma_start(rows_of(g0, m), gn[s][:, :, :].rearrange("p k (o f) -> p o (k f)", o=1)).then_inc(fs[f"g_out{s}"], 16)

                    if kind == "l2":
                        sp.dma_start(w2_sb[:, :], w2).then_inc(consts, 16)
                    parts = [(load, 0)]
                    if kind != "first":
                        parts = [(load, 0), (store_x, 2 if kind == "l2" else 1)]
                    parts.append((store_h, 3 if kind == "l2" else 2))
                    if kind == "l2":
                        parts.append((store_g, 3))
                    pipeline(sp, NCHUNKS, parts, NS)
                    for s in range(NS):
                        if kind != "first":
                            await_in_loop(sp, node_x_out[s], xb[s] + 16 * uses(s))
                        await_in_loop(sp, node_h_out[s], hb[s] + 16 * uses(s))
                        if kind == "l2":
                            await_in_loop(sp, fs[f"g_out{s}"], 16 * uses(s))

                @block.gpsimd
                def _(pool):
                    if kind == "first":
                        pool.memset(minus_half[:, :], -0.5).then_inc(consts, 1)
                        pool.wait_ge(consts, 1)

                    def inv(m, s, h, first):
                        await_in_loop(pool, fs["clamped"], m + 1)
                        pool.tensor_tensor(inv_deg[:, bass.ds(m, 1), :], small[s][:, 0:1, :],
                                           minus_half[:, :].rearrange("p (o k) -> p o k", o=1), ALU.pow).then_inc(fs["inv"], 1)

                    def norm_part(m, s, h, first):
                        await_in_loop(pool, node_eps, base + m + 1)
                        if not first:
                            await_in_loop(pool, node_norm, base + m + 1 - NS)
                        pool.tensor_tensor(rstd[s][:, :], vare[s][:, :], minus_half[:, :], ALU.pow).then_inc(node_rstd, 1)
                        await_in_loop(pool, node_rstd, base + m + 1)
                        if not first:
                            await_in_loop(pool, node_h, base + m + 1 - NS)
                        pool.tensor_tensor(norm[s][:, :, :], cent[s][:, :, :],
                                           rstd[s][:, :].rearrange("p (k o) -> p k o", o=1).to_broadcast([P, ROWS, D]),
                                           ALU.mult).then_inc(node_norm, 1)

                    def scale_g(m, s, h, first):
                        await_in_loop(pool, node_h, base + m + 1)
                        if not first:
                            await_in_loop(pool, fs[f"g_out{s}"], h * 16)
                        pool.tensor_tensor(gn[s][:, :, :], hn[s][:, :, :],
                                           inv_deg[:, bass.ds(m, 1), :].rearrange("p o k -> p k o").to_broadcast([P, ROWS, D]),
                                           ALU.mult).then_inc(fs["g"], 1)

                    parts = []
                    if kind == "l1":
                        parts.append((inv, 0))
                    parts.append((norm_part, 3 if kind == "l2" else 1))
                    if kind == "l2":
                        parts.append((scale_g, 3))
                    pipeline(pool, NCHUNKS, parts, NS)

                @block.vector
                def _(dve):
                    def front(m, s, h, first):
                        wb_in = h * (16 * loads) + (ib[s] + 16 * loads)
                        dve.wait_ge(node_in[s], wb_in)
                        if kind == "first":
                            return
                        if not first:
                            dve.wait_ge(node_x_out[s], h * 16 + xb[s])
                        if kind == "l0":
                            v.tensor_tensor(xn[s][:, :, :], xi[s][:, :, :], mi[s][:, :, :], ALU.add).then_inc(node_x, 1)
                            dve.wait_ge(node_x, xbase + m + 1)
                            dve.sem_inc(node_taken, 1)
                        if kind == "l1":
                            if not first:
                                dve.wait_ge(fs["inv"], m + 1 - NS)
                            v.tensor_scalar(small[s][:, 0, :], mi[s][:, :, D], 1.0, None, ALU.max).then_inc(fs["clamped"], 1)
                            dve.wait_ge(fs["clamped"], m + 1)
                            v.reciprocal(small[s][:, 1, :], small[s][:, 0, :]).then_inc(fs["recip"], 1)
                            dve.wait_ge(fs["recip"], m + 1)
                            v.tensor_tensor(tmp[s][:, :, :], mi[s][:, :, 0:D],
                                            small[s][:, 1, :].rearrange("p (k o) -> p k o", o=1).to_broadcast([P, ROWS, D]),
                                            ALU.mult).then_inc(fs["scaled"], 1)
                            dve.wait_ge(fs["scaled"], m + 1)
                            dve.sem_inc(node_taken, 1)
                            v.tensor_tensor(xn[s][:, :, :], tmp[s][:, :, :], xi[s][:, :, :], ALU.add).then_inc(node_x, 1)
                            dve.wait_ge(node_x, xbase + m + 1)
                        if kind == "l2":
                            v.tensor_scalar(small[s][:, 0, :], mi[s][:, :, D + 1], -1.0, gmax[:, 0:1], ALU.mult,
                                            ALU.add).then_inc(fs["gap"], 1)
                            dve.wait_ge(fs["gap"], m + 1)
                            v.tensor_scalar(small[s][:, 1, :], small[s][:, 0, :], 0.0, 80.0, ALU.max, ALU.min).then_inc(fs["gap2"], 1)
                            dve.wait_ge(fs["expd"], m + 1)
                            v.scalar_tensor_tensor(small[s][:, 3, :], small[s][:, 2, :], 1e-10, mi[s][:, :, D], ALU.mult,
                                                   ALU.add).then_inc(fs["den"], 1)
                            dve.wait_ge(fs["den"], m + 1)
                            v.reciprocal(small[s][:, 4, :], small[s][:, 3, :]).then_inc(fs["recip"], 1)
                            dve.wait_ge(fs["recip"], m + 1)
                            v.tensor_tensor(tmp[s][:, :, :], mi[s][:, :, 0:D],
                                            small[s][:, 4, :].rearrange("p (k o) -> p k o", o=1).to_broadcast([P, ROWS, D]),
                                            ALU.mult).then_inc(fs["scaled"], 1)
                            dve.wait_ge(fs["scaled"], m + 1)
                            dve.sem_inc(node_taken, 1)
                            dve.wait_ge(fs[f"h2_in{s}"], h * 16 + 16)
                            if not first:
                                dve.wait_ge(fs["yt"], m + 1 - NS)
                            v.tensor_tensor(y[s][:, :, :], tmp[s][:, :, :], hi[s][:, :, :], ALU.add).then_inc(fs["y"], 1)

                    def finish_x(m, s, h, first):
                        if kind == "l2":
                            dve.wait_ge(fs["zs"], m + 1)
                            v.tensor_tensor(lr[s][:, :, :].rearrange("p k f -> p (k f)"), ps_z[s][:, 0:ROWS * D],
                                            tmp[s][:, :, :].rearrange("p k f -> p (k f)"), ALU.max).then_inc(fs["lrelu"], 1)
                            dve.wait_ge(fs["lrelu"], m + 1)
                            v.tensor_tensor(xn[s][:, :, :], lr[s][:, :, :], xi[s][:, :, :], ALU.add).then_inc(node_x, 1)
                            dve.wait_ge(node_x, xbase + m + 1)

                    def center(m, s, h, first):
                        v.tensor_reduce(total[s][:, :], xn[s][:, :, :], AX, ALU.add).then_inc(node_sum, 1)
                        dve.wait_ge(node_sum, base + m + 1)
                        if not first:
                            dve.wait_ge(node_norm, base + m + 1 - NS)
                        v.scalar_tensor_tensor(cent[s][:, :, :], total[s][:, :].rearrange("p (k o) -> p k o", o=1).to_broadcast([P, ROWS, D]),
                                               -1.0 / D, xn[s][:, :, :], ALU.mult, ALU.add).then_inc(node_cent, 1)

                    def spread(m, s, h, first):
                        dve.wait_ge(node_sq, base + m + 1)
                        v.tensor_reduce(var[s][:, :], sq[s][:, :, :], AX, ALU.add).then_inc(node_var, 1)
                        dve.wait_ge(node_var, base + m + 1)
                        if not first:
                            dve.wait_ge(node_rstd, base + m + 1 - NS)
                        v.tensor_scalar(vare[s][:, :], var[s][:, :], 1.0 / D, LN_EPS, ALU.mult, ALU.add).then_inc(node_eps, 1)

                    if kind == "l2":
                        pipeline(dve, NCHUNKS, [(spread, 3), (finish_x, 2), (center, 2), (front, 0)], NS)
                    else:
                        pipeline(dve, NCHUNKS, [(spread, 1), (front, 0), (center, 0)], NS)
                    if kind == "l1":
                        dve.wait_ge(fs["inv"], NCHUNKS)
                        v.tensor_tensor(inv_deg2[:, :, :], inv_deg[:, :, :], inv_deg[:, :, :], ALU.mult).then_inc(consts, 1)
                        dve.wait_ge(consts, 1)

                @block.scalar
                def _(act):
                    def expd(m, s, h, first):
                        act.wait_ge(fs["gap2"], m + 1)
                        if not first:
                            act.wait_ge(fs["den"], m + 1 - NS)
                        nc.scalar.activation(small[s][:, 2, :], small[s][:, 1, :], ACT.Exp).then_inc(fs["expd"], 1)

                    def turn_y(m, s, h, first):
                        act.wait_ge(fs["yt"], m + 1)
                        if not first:
                            act.wait_ge(fs["z"], m + 1 - NS)
                        nc.scalar.copy(yt[s][:, :], ps_yt[:, 0:ROWS * D]).then_inc(fs["ytc"], 1)

                    def slope(m, s, h, first):
                        act.wait_ge(fs["z"], m + 1)
                        nc.scalar.activation(tmp[s][:, :, :].rearrange("p k f -> p (k f)"), ps_z[s][:, 0:ROWS * D], ACT.Copy,
                                             scale=0.2).then_inc(fs["zs"], 1)

                    def square(m, s, h, first):
                        act.wait_ge(node_cent, base + m + 1)
                        if not first:
                            act.wait_ge(node_var, base + m + 1 - NS)
                        nc.scalar.activation(sq[s][:, :, :], cent[s][:, :, :], ACT.Square).then_inc(node_sq, 1)

                    def relu(m, s, h, first):
                        act.wait_ge(node_norm, base + m + 1)
                        if not first:
                            act.wait_ge(node_h_out[s], h * 16 + hb[s])
                            if kind == "l2":
                                act.wait_ge(fs["g"], m + 1 - NS)
                        nc.scalar.activation(hn[s][:, :, :], norm[s][:, :, :], ACT.Relu).then_inc(node_h, 1)

                    if kind == "l2":
                        pipeline(act, NCHUNKS, [(expd, 0), (turn_y, 0), (square, 2), (slope, 1), (relu, 3)], NS)
                    else:
                        pipeline(act, NCHUNKS, [(square, 0), (relu, 1)], NS)

                if kind == "l2":
                    @block.tensor
                    def _(pe):
                        pe.wait_ge(consts, 16)

                        def turn(m, s, h, first):
                            await_in_loop(pe, fs["y"], m + 1)
                            if not (first and m == 0):
                                await_in_loop(pe, fs["ytc"], m)
                            for j in range(ROWS // 2):
                                ins = nc.tensor.transpose(ps_yt[:, j * P:(j + 1) * P],
                                                          y[s][:, 2 * j:2 * j + 2, :].rearrange("p k f -> p (k f)"), eye[:, :])
                            ins.then_inc(fs["yt"], 1)

                        def project(m, s, h, first):
                            await_in_loop(pe, fs["ytc"], m + 1)
                            if not first:
                                await_in_loop(pe, fs["lrelu"], m + 1 - NS)
                            for j in range(ROWS // 2):
                                ins = nc.tensor.matmul(ps_z[s][:, j * P:(j + 1) * P], yt[s][:, j * P:(j + 1) * P], w2_sb[:, :],
                                                       start=True, stop=True)
                            ins.then_inc(fs["z"], 1)

                        pipeline(pe, NCHUNKS, [(turn, 0), (project, 1)], NS)
            node_base[0] += NCHUNKS
            for s in range(NS):
                in_base[s] += 16 * loads * uses(s)
                if kind != "first":
                    x_out_base[s] += 16 * uses(s)
                h_out_base[s] += 16 * uses(s)

        node_pass("first", x, None, h0)
        if "first" in debug:
            return

        with ExitStack() as c:
            c.enter_context(nc.cleanup_on_exit())
            cat = [sb_in(c, f"cat{s}", [P, K, 2 * D + 2]) for s in range(GS)]
            hd = [sb_in(c, f"hd{s}", [P, K, D]) for s in range(GS)]
            at = [sb_in(c, f"at{s}", [P, K, 4], i32) for s in range(GS)]
            xsrc = sb_in(c, "xsrc", [P, CHUNK])
            xdst = [sb_in(c, f"xdst{s}", [P, CHUNK]) for s in range(GS)]
            bias_rep = sb_in(c, "bias_rep", [P, 8, D])
            clamped = [sb_in(c, f"clamped{q}", [P, 2, CHUNK]) for q in range(2)]
            expd = [sb_in(c, f"expd{q}", [P, 2, CHUNK]) for q in range(2)]
            logd = [sb_in(c, f"logd{q}", [P, 2, CHUNK]) for q in range(2)]
            soft = [[sb_in(c, f"soft{q}{s}", [P, 2, CHUNK]) for s in range(GS)] for q in range(2)]
            lrow = [sb_in(c, f"lrow{s}", [HEADS, CHUNK]) for s in range(GS)]
            w0_sb = sb_in(c, "w0_sb", [P, 2 * P])
            att_sb = sb_in(c, "att_sb", [P, 4, HEADS])
            zeros = sb_in(c, "zeros", [P, TILES])
            ps_in_side = [ps_in(c, f"in_side{q}", [P, CHUNK]) for q in range(2)]
            ps_side = [ps_in(c, f"side{q}", [P, 2, CHUNK]) for q in range(2)]
            ps_logit = ps_in(c, "logit", [HEADS, CHUNK])
            a_const = sem_in(c, "a_const")
            a_zero = sem_in(c, "a_zero")
            zero_out = sem_in(c, "zero_out")
            a_index = sem_in(c, "a_index")
            rec_in = [sem_in(c, f"rec_in{s}") for s in range(GS)]
            hd_in = [sem_in(c, f"hd_in{s}") for s in range(GS)]
            a_turned = [sem_in(c, f"a_turned{q}") for q in range(2)]
            a_edge_rows = sem_in(c, "a_edge_rows")
            a_side = [sem_in(c, f"a_side{q}") for q in range(2)]
            a_proj = [sem_in(c, f"a_proj{q}") for q in range(2)]
            a_clamp = [sem_in(c, f"a_clamp{q}") for q in range(2)]
            a_exp = [sem_in(c, f"a_exp{q}") for q in range(2)]
            a_log = [sem_in(c, f"a_log{q}") for q in range(2)]
            a_soft = [sem_in(c, f"a_soft{q}") for q in range(2)]
            a_logit = sem_in(c, "a_logit")
            a_lrow = sem_in(c, "a_lrow")
            a_kept = sem_in(c, "a_kept")
            sp_out = [sem_in(c, f"sp_out{s}") for s in range(GS)]
            lg_out = [sem_in(c, f"lg_out{s}") for s in range(GS)]
            block = c.enter_context(nc.Block())
            v = nc.vector

            @block.sync
            def _(sp):
                sp.dma_start(w0_sb[:, :], w0).then_inc(a_const, 16)
                sp.dma_start(att_sb[:, :, :].rearrange("p q h -> p (q h)"), att).then_inc(a_const, 16)
                await_in_loop(sp, a_zero, 1)
                sp.dma_start(bias_rep[:, :, :], bias0.rearrange("(a o) f -> a o f", o=1).to_broadcast([P, 8, D])).then_inc(a_const, 16)
                await_in_loop(sp, a_const, 48)
                sp.dma_start(msg0.rearrange("(p w a) f -> p w (a f)", p=P, a=8),
                             bias_rep[:, :, :].rearrange("p a (o f) -> p o (a f)", o=1).to_broadcast([P, TILES // 8, 8 * D])).then_inc(zero_out, 16)
                tables = ((msg1, D + 1), (msg2, D + 2), (hop0, D), (hop1, D))
                for table, width in tables:
                    sp.dma_start(table.rearrange("(p a) f -> p (a f)", p=P).rearrange("p (w a) -> p w a", a=TILES),
                                 zeros[:, :].rearrange("p (o a) -> p o a", o=1).to_broadcast([P, width, TILES])).then_inc(zero_out, 16)

                def store(m, s, h, first):
                    await_in_loop(sp, a_soft[1], m + 1)
                    sp.dma_start(sp_j.rearrange("c b p e -> c p b e")[bass.ds(m, 1), :, :, :].rearrange("o p b e -> (o p) b e"),
                                 soft[1][s][:, :, :]).then_inc(sp_out[s], 16)

                def store_row(m, s, h, first):
                    await_in_loop(sp, a_lrow, m + 1)
                    sp.dma_start(logits[:, bass.ds(m * CHUNK, CHUNK)], lrow[s][:, :]).then_inc(lg_out[s], 16)

                pipeline(sp, CHUNKS, [(store, 0), (store_row, 1)], GS)
                await_in_loop(sp, zero_out, 16 * (len(tables) + 1))
                for s in range(GS):
                    await_in_loop(sp, sp_out[s], 16 * times(s, GS))
                    await_in_loop(sp, lg_out[s], 16 * times(s, GS))

            @block.gpsimd
            def _(pool):
                def ends(m, s, h, first):
                    if not first:
                        await_in_loop(pool, rec_in[s], h * (32 * K))
                        await_in_loop(pool, a_kept, m + 1 - GS)
                        await_in_loop(pool, a_turned[0], m + 1 - GS)
                    pool.tensor_copy(at[s][:, :, 0:2], by_src[:, bass.ds(m * K, K), 0:2]).then_inc(a_index, 1)
                    await_in_loop(pool, a_index, m + 1)
                    for k in range(K):
                        pool.indirect_dma_start(cat[s].bitcast(i32)[:, k, D:2 * D + 2], None, rec,
                                                bass.IndirectOffsetOnAxis(at[s][:, k, EDGE:EDGE + 1], 0)).then_inc(rec_in[s], 16)
                    for k in range(K):
                        pool.indirect_dma_start(cat[s][:, k, 0:D], None, h0,
                                                bass.IndirectOffsetOnAxis(at[s][:, k, SRC:SRC + 1], 0)).then_inc(rec_in[s], 16)

                def other_end(m, s, h, first):
                    await_in_loop(pool, rec_in[s], h * (32 * K) + 32 * K)
                    if not first:
                        await_in_loop(pool, a_turned[1], m + 1 - GS)
                    for k in range(K):
                        pool.indirect_dma_start(hd[s][:, k, :], None, h0,
                                                bass.IndirectOffsetOnAxis(cat[s].bitcast(i32)[:, k, 2 * D:2 * D + 1], 0)).then_inc(hd_in[s], 16)

                pipeline(pool, CHUNKS, [(ends, 0), (other_end, 2)], GS)

            @block.tensor
            def _(pe):
                pe.wait_ge(a_const, 48)

                def turn(q):
                    def part(m, s, h, first):
                        if q == 0:
                            await_in_loop(pe, rec_in[s], h * (32 * K) + 32 * K)
                        else:
                            await_in_loop(pe, hd_in[s], h * (16 * K) + 16 * K)
                        if not fresh(m, 1):
                            await_in_loop(pe, a_side[q], m)
                            if q == 0:
                                await_in_loop(pe, a_edge_rows, m)
                        for k in range(K):
                            if q == 0:
                                ins = nc.tensor.transpose(ps_in_side[0][:, k * P:(k + 1) * P], cat[s][:, k, 0:2 * D], eye[:, :])
                            else:
                                ins = nc.tensor.transpose(ps_in_side[1][0:D, k * P:(k + 1) * P], hd[s][:, k, :], eye[:, :])
                        ins.then_inc(a_turned[q], 1)
                    return part

                def project(q):
                    def part(m, s, h, first):
                        await_in_loop(pe, a_side[q], m + 1)
                        if q == 1:
                            await_in_loop(pe, a_edge_rows, m + 1)
                        if not fresh(m, 1):
                            await_in_loop(pe, a_soft[q], m)
                        for b in range(2):
                            ins = nc.tensor.matmul(ps_side[q][:, b, :], w0_sb[:, b * P:(b + 1) * P],
                                                   (xsrc if q == 0 else xdst[s])[:, :], start=True, stop=True)
                        ins.then_inc(a_proj[q], 1)
                    return part

                def logit(m, s, h, first):
                    await_in_loop(pe, a_soft[1], m + 1)
                    await_in_loop(pe, a_soft[0], m + 1)
                    if not fresh(m, 1):
                        await_in_loop(pe, a_lrow, m)
                    for n in range(4):
                        ins = nc.tensor.matmul(ps_logit[:, :], att_sb[:, n, :], soft[n // 2][s][:, n % 2, :],
                                               start=(n == 0), stop=(n == 3))
                    ins.then_inc(a_logit, 1)

                pipeline(pe, CHUNKS, [(logit, 3), (turn(0), 0), (project(0), 0), (turn(1), 2), (project(1), 2)], GS)

            @block.scalar
            def _(act):
                nc.scalar.preload_act_table_set("natural_log_exp_and_others")

                def sides(m, s, h, first):
                    act.wait_ge(a_turned[0], m + 1)
                    if not fresh(m, 1):
                        act.wait_ge(a_proj[0], m)
                    nc.scalar.copy(xsrc[:, :], ps_in_side[0][:, :]).then_inc(a_side[0], 1)
                    if not first:
                        act.wait_ge(a_proj[1], m + 1 - GS)
                    nc.scalar.copy(xdst[s][D:2 * D, :], ps_in_side[0][D:2 * D, :]).then_inc(a_edge_rows, 1)

                def exp_log(q):
                    def part(m, s, h, first):
                        act.wait_ge(a_clamp[q], m + 1)
                        if not fresh(m, 1):
                            act.wait_ge(a_log[q], m)
                        nc.scalar.activation(expd[q][:, :, :], clamped[q][:, :, :], ACT.Exp).then_inc(a_exp[q], 1)
                        act.wait_ge(a_exp[q], m + 1)
                        if not fresh(m, 1):
                            act.wait_ge(a_soft[q], m)
                        nc.scalar.activation(logd[q][:, :, :], expd[q][:, :, :], ACT.Ln, bias=1.0).then_inc(a_log[q], 1)
                    return part

                def keep(m, s, h, first):
                    act.wait_ge(rec_in[s], h * (32 * K) + 32 * K)
                    act.wait_ge(hd_in[s], h * (16 * K) + 16 * K)
                    ends_of = cat[s].bitcast(i32)
                    nc.scalar.copy(by_src[:, bass.ds(m * K, K), DST], ends_of[:, :, 2 * D])
                    nc.scalar.copy(type_of[:, bass.ds(m * K, K)], ends_of[:, :, 2 * D + 1]).then_inc(a_kept, 1)

                def logit_row(m, s, h, first):
                    act.wait_ge(a_logit, m + 1)
                    if not first:
                        act.wait_ge(lg_out[s], h * 16)
                    nc.scalar.copy(lrow[s][:, :], ps_logit[:, :]).then_inc(a_lrow, 1)

                pipeline(act, CHUNKS, [(logit_row, 3), (sides, 0), (exp_log(0), 0), (keep, 2), (exp_log(1), 2)], GS)

            @block.vector
            def _(dve):
                v.memset(zeros[:, :], 0.0).then_inc(a_zero, 1)

                def side(m, s, h, first):
                    dve.wait_ge(a_turned[1], m + 1)
                    if not first:
                        dve.wait_ge(a_proj[1], m + 1 - GS)
                    v.tensor_copy(xdst[s][0:D, :], ps_in_side[1][0:D, :]).then_inc(a_side[1], 1)

                def clamp(q):
                    def part(m, s, h, first):
                        dve.wait_ge(a_proj[q], m + 1)
                        if not fresh(m, 1):
                            dve.wait_ge(a_exp[q], m)
                        v.tensor_scalar(clamped[q][:, :, :], ps_side[q][:, :, :], CLAMP, None, ALU.min).then_inc(a_clamp[q], 1)
                    return part

                def choose(q):
                    def part(m, s, h, first):
                        dve.wait_ge(a_log[q], m + 1)
                        if not first:
                            dve.wait_ge(a_logit, m + 1 - GS)
                            if q == 1:
                                dve.wait_ge(sp_out[s], h * 16)
                        v.tensor_tensor(soft[q][s][:, :, :], logd[q][:, :, :], ps_side[q][:, :, :], ALU.max).then_inc(a_soft[q], 1)
                    return part

                pipeline(dve, CHUNKS, [(clamp(0), 0), (choose(0), 0), (side, 2), (clamp(1), 2), (choose(1), 2)], GS)

        if "l0a" in debug:
            return

        with ExitStack() as c:
            c.enter_context(nc.cleanup_on_exit())
            def t(name):
                return sb_in(c, "m_" + name, [P, SEG_LEN])

            z, cont, contn, s1, s2, s3, s4 = (t(n) for n in ("z", "cont", "contn", "s1", "s2", "s3", "s4"))
            parts = [sb_in(c, f"m_part{i}", [P, SEG_LEN], bf16) for i in range(3)]
            col = sb_in(c, "m_col", [P, 16])
            row = sb_in(c, "m_row", [1, 8, P])
            one = sb_in(c, "m_one", [1, 1])
            sh = sb_in(c, "m_sh", [P, P])
            gb = sb_in(c, "m_gb", [P, 2])
            trow = sb_in(c, "m_trow", [P, 4, P])
            ps_t = ps_in(c, "m_t", [P, 4, P])
            ps_s = ps_in(c, "m_s", [P, 512])
            ps_r = ps_in(c, "m_r", [1, 512])
            ps_b = ps_in(c, "m_b", [P, 512])
            m_in = sem_in(c, "m_in")
            m_types = sem_in(c, "m_types")
            m_trow = sem_in(c, "m_trow")
            m_out = sem_in(c, "m_out")
            m_masked = sem_in(c, "m_masked")
            m_first = sem_in(c, "m_first")
            m_dve = sem_in(c, "m_dve")
            m_to_act = sem_in(c, "m_to_act")
            m_from_act = sem_in(c, "m_from_act")
            m_to_pe = sem_in(c, "m_to_pe")
            m_from_pe = sem_in(c, "m_from_pe")
            m_done = sem_in(c, "m_done")
            block = c.enter_context(nc.Block())
            v = nc.vector
            PADS = N - (SEGS - 1) * SEG_LEN

            @block.sync
            def _(sp):
                sp.dma_start(z[:, :], logits.rearrange("h (c e) -> c h e", c=SEGS)).then_inc(m_in, 16)
                for i, tile in enumerate((cont, contn)):
                    sp.dma_start(tile[:, :], same_src[i:i + NPAD].rearrange("(c o e) -> c o e", c=SEGS, o=1).to_broadcast([SEGS, HEADS, SEG_LEN])).then_inc(m_in, 16)
                sp.dma_start(sh[:, :], samehead).then_inc(m_in, 16)
                sp.dma_start(gb[:, 0:1], gamma).then_inc(m_in, 16)
                sp.dma_start(gb[:, 1:2], beta).then_inc(m_in, 16)
                await_in_loop(sp, m_trow, 1)
                sp.dma_start(types_row[0:3 * P, :].rearrange("(j t) p -> t j p", j=3), trow[:, 0:3, :]).then_inc(m_out, 16)
                sp.dma_start(types_row[3 * P:TILES, :], trow[0:TILES - 3 * P, 3, :]).then_inc(m_out, 16)
                await_in_loop(sp, m_done, 1)
                for i in range(3):
                    sp.dma_start(weights[i].rearrange("h (c e) -> c h e", c=SEGS), parts[i][:, :]).then_inc(m_out, 16)
                await_in_loop(sp, m_out, 80)

            @block.gpsimd
            def _(pool):
                pool.memset(one[:, :], 1.0).then_inc(m_types, 1)
                pool.wait_ge(m_first, 1)
                pool.affine_select(out=s1[:, PADS:SEG_LEN], in_=s1[:, PADS:SEG_LEN], compare_op=ALU.is_ge, fill=0.0,
                                   base=P - HEADS - 1, pattern=[[0, SEG_LEN - PADS]], channel_multiplier=-1).then_inc(m_masked, 1)
                pool.wait_ge(m_first, 2)
                pool.affine_select(out=s2[:, PADS:SEG_LEN], in_=s2[:, PADS:SEG_LEN], compare_op=ALU.is_ge, fill=0.0,
                                   base=P - HEADS - 1, pattern=[[0, SEG_LEN - PADS]], channel_multiplier=-1).then_inc(m_masked, 1)

            @block.tensor
            def _(pe):
                for j in range(4):
                    w = min(P, TILES - j * P)
                    ins = nc.tensor.transpose(ps_t[0:w, j, :], type_of[:, j * P:j * P + w], eye[:, :])
                ins.then_inc(m_from_pe, 1)
                pe.wait_ge(m_in, 96)
                for n in range(2):
                    pe.wait_ge(m_to_pe, n + 1)
                    nc.tensor.matmul(ps_s[:, n:n + 1], sh[:, :], col[:, n:n + 1], start=True, stop=True).then_inc(m_from_pe, 1)
                pe.wait_ge(m_types, 1)
                for n in range(4):
                    pe.wait_ge(m_to_pe, 2 * n + 3)
                    nc.tensor.transpose(ps_r[:, 0:P], col[:, 8:9], eye[:, :])
                    nc.tensor.transpose(ps_r[:, P:2 * P], col[:, 9:10], eye[:, :]).then_inc(m_from_pe, 1)
                    pe.wait_ge(m_to_pe, 2 * n + 4)
                    nc.tensor.matmul(ps_b[:, n:n + 1], row[:, 3, :], one[:, :], start=True, stop=True).then_inc(m_from_pe, 1)

            @block.scalar
            def _(act):
                n = [0]

                def do(o, i, f, **kw):
                    n[0] += 1
                    act.wait_ge(m_to_act, n[0])
                    nc.scalar.activation(o, i, f, **kw).then_inc(m_from_act, 1)

                act.wait_ge(m_from_pe, 1)
                nc.scalar.copy(trow[:, 0:3, :], ps_t[:, 0:3, :])
                nc.scalar.copy(trow[0:TILES - 3 * P, 3, :], ps_t[0:TILES - 3 * P, 3, :]).then_inc(m_trow, 1)
                do(s2[:, :], s1[:, :], ACT.Exp)
                do(s3[:, :], s2[:, :], ACT.Ln, bias=1.0)
                do(s3[:, :], s2[:, :], ACT.Square)
                do(col[:, 4:5], col[:, 3:4], ACT.Sqrt)
                do(s2[:, :], s1[:, :], ACT.Exp)
                do(s3[:, :], s2[:, :], ACT.Ln, bias=1.0)
                do(s3[:, :], s2[:, :], ACT.Exp)

            @block.vector
            def _(dve):
                cnt = {"v": 0, "a": 0, "p": 1, "pe": 0}

                def op(ins):
                    cnt["v"] += 1
                    ins.then_inc(m_dve, 1)
                    dve.wait_ge(m_dve, cnt["v"])

                def to_act(n=1):
                    for _ in range(n):
                        dve.sem_inc(m_to_act, 1)
                        cnt["a"] += 1
                        dve.wait_ge(m_from_act, cnt["a"])

                def to_pe():
                    dve.sem_inc(m_to_pe, 1)
                    cnt["p"] += 1
                    dve.wait_ge(m_from_pe, cnt["p"])

                dve.wait_ge(m_in, 96)
                dve.wait_ge(m_types, 1)

                def softplus():
                    op(v.tensor_scalar(s1[:, :], z[:, :], CLAMP, None, ALU.min))
                    to_act(2)
                    op(v.tensor_tensor(s1[:, :], s3[:, :], z[:, :], ALU.max))

                softplus()
                dve.sem_inc(m_first, 1)
                dve.wait_ge(m_masked, 1)
                op(v.tensor_reduce(col[:, 0:1], s1[:, :], AX, ALU.add))
                to_pe()
                op(v.tensor_scalar(col[:, 2:3], ps_s[:, 0:1], -1.0 / N, None, ALU.mult))
                op(v.tensor_scalar(s2[:, :], s1[:, :], col[:, 2:3], None, ALU.add))
                dve.sem_inc(m_first, 1)
                dve.wait_ge(m_masked, 2)
                to_act()
                op(v.tensor_reduce(col[:, 1:2], s3[:, :], AX, ALU.add))
                to_pe()
                op(v.tensor_scalar(col[:, 3:4], ps_s[:, 1:2], 1.0 / N, LN_EPS, ALU.mult, ALU.add))
                to_act()
                op(v.reciprocal(col[:, 5:6], col[:, 4:5]))
                op(v.tensor_tensor(col[:, 6:7], col[:, 5:6], gb[:, 0:1], ALU.mult))
                op(v.tensor_scalar(z[:, :], s2[:, :], col[:, 6:7], gb[:, 1:2], ALU.mult, ALU.add))
                softplus()

                def scan(o, keep, add, op1, n, reverse):
                    view = (lambda a: a[:, ::-1]) if reverse else (lambda a: a[:, :])
                    end = slice(0, 1) if reverse else slice(SEG_LEN - 1, SEG_LEN)
                    op(v.tensor_tensor_scan(view(o), view(keep), view(add), 0.0, ALU.mult, op1))
                    op(v.tensor_copy(col[:, 8:9], o[:, end]))
                    op(v.tensor_reduce(col[:, 9:10], keep[:, :], AX, ALU.min))
                    to_pe()
                    op(v.tensor_copy(row[:, 0:2, :].rearrange("p a b -> p (a b)"), ps_r[:, 0:2 * P]))
                    op(v.memset(row[:, 2:4, :], 0.0))
                    for h in range(HEADS):
                        def stretches(i, lo, hi, r=reverse):
                            a = row[:, i, :].rearrange("p (c h) -> p h c", h=HEADS)[:, h, lo:hi]
                            return a[:, ::-1] if r else a
                        op(v.tensor_tensor_scan(stretches(2, 0, SEGS), stretches(1, 0, SEGS), stretches(0, 0, SEGS), 0.0, ALU.mult, op1))
                        to, of = ((0, SEGS - 1), (1, SEGS)) if reverse else ((1, SEGS), (0, SEGS - 1))
                        op(v.tensor_copy(stretches(3, *to, r=False), stretches(2, *of, r=False)))
                    to_pe()
                    op(v.tensor_copy(col[:, 10:11], ps_b[:, n:n + 1]))
                    op(v.tensor_tensor_scan(view(o), view(keep), view(add), col[:, 10:11], ALU.mult, op1))

                scan(s2, cont, s1, ALU.max, 0, False)
                op(v.tensor_scalar(s3[:, :], contn[:, :], -1.0, 1.0, ALU.mult, ALU.add))
                op(v.tensor_tensor(s3[:, :], s3[:, :], s2[:, :], ALU.mult))
                scan(s4, contn, s3, ALU.add, 1, True)
                op(v.tensor_tensor(s2[:, :], s1[:, :], s4[:, :], ALU.subtract))
                to_act()
                scan(s2, cont, s3, ALU.add, 2, False)
                op(v.tensor_scalar(s1[:, :], contn[:, :], -1.0, 1.0, ALU.mult, ALU.add))
                op(v.tensor_tensor(s1[:, :], s1[:, :], s2[:, :], ALU.mult))
                scan(s4, contn, s1, ALU.add, 3, True)
                op(v.tensor_scalar(s4[:, :], s4[:, :], 1e-16, None, ALU.add))
                op(v.reciprocal(s2[:, :], s4[:, :]))
                op(v.scalar_tensor_tensor(z[:, :], s3[:, :], 1.0 / HEADS, s2[:, :], ALU.mult, ALU.mult))
                op(v.tensor_copy(parts[0][:, :], z[:, :]))
                op(v.tensor_tensor(s1[:, :], z[:, :], parts[0][:, :], ALU.subtract))
                op(v.tensor_copy(parts[1][:, :], s1[:, :]))
                op(v.tensor_tensor(s2[:, :], s1[:, :], parts[1][:, :], ALU.subtract))
                op(v.tensor_copy(parts[2][:, :], s2[:, :]))
                dve.sem_inc(m_done, 1)

        if "soft" in debug:
            return

        with ExitStack() as c:
            c.enter_context(nc.cleanup_on_exit())
            LS = 4
            sj = [sb_in(c, f"sj{s}", [P, 2, CHUNK]) for s in range(LS)]
            wr = [sb_in(c, f"wr{s}", [3 * HEADS, CHUNK], bf16) for s in range(LS)]
            ct = [sb_in(c, f"ct{s}", [D, CHUNK]) for s in range(LS)]
            biased = [sb_in(c, f"biased{s}", [D, CHUNK]) for s in range(2)]
            bias_col = sb_in(c, "bias_col", [D, 1])
            hs_f = sb_in(c, "hs_f", [3 * HEADS, 2, P])
            wm = [sb_in(c, f"wm{s}", [P, 2, CHUNK]) for s in range(2)]
            run = [sb_in(c, f"c_run{s}", [D, CHUNK]) for s in range(2)]
            rows_sb = [sb_in(c, f"c_rows{s}", [P, K, D]) for s in range(2)]
            at_out = [sb_in(c, f"c_at_out{s}", [P, K], i32) for s in range(2)]
            hs_sb = sb_in(c, "hs_sb", [3 * HEADS, 2, P], bf16)
            hsum_sb = sb_in(c, "hsum_sb", [P, D])
            ps_w = [ps_in(c, f"w{s}", [P, 2, CHUNK]) for s in range(2)]
            ps_m = [ps_in(c, f"m{s}", [D, CHUNK]) for s in range(2)]
            ps_back = [ps_in(c, f"c_back{s}", [P, CHUNK]) for s in range(2)]
            c_const = sem_in(c, "c_const")
            c_in = [sem_in(c, f"c_in{s}") for s in range(LS)]
            c_biased = sem_in(c, "c_biased")
            c_index = sem_in(c, "c_index")
            c_spread = sem_in(c, "c_spread")
            c_weighed = sem_in(c, "c_weighed")
            c_msg = sem_in(c, "c_msg")
            c_run = sem_in(c, "c_run")
            c_back = sem_in(c, "c_back")
            c_rows = sem_in(c, "c_rows")
            c_out = [sem_in(c, f"c_out{s}") for s in range(2)]
            block = c.enter_context(nc.Block())
            v = nc.vector

            @block.sync
            def _(sp):
                for i in range(3):
                    sp.dma_start(hs_f[i * HEADS:(i + 1) * HEADS, :, :].rearrange("h b p -> h (b p)"), headsel).then_inc(c_const, 16)
                sp.dma_start(hsum_sb[:, :], headsum).then_inc(c_const, 16)
                sp.dma_start(bias_col[:, :], bias0.rearrange("o f -> f o")).then_inc(c_const, 16)

                def load(m, s, h, first):
                    if not first:
                        await_in_loop(sp, c_run, m + 1 - LS)
                    sp.dma_start(sj[s][:, :, :], sp_j.rearrange("c b p e -> c p b e")[bass.ds(m, 1), :, :, :].rearrange("o p b e -> (o p) b e")).then_inc(c_in[s], 16)
                    sp.dma_start(wr[s][:, :], weights.rearrange("i h e -> (i h) e")[:, bass.ds(m * CHUNK, CHUNK)]).then_inc(c_in[s], 16)
                    sp.dma_start(ct[s][:, :], same_src[bass.ds(m * CHUNK, CHUNK)].rearrange("(o e) -> o e", o=1).to_broadcast([D, CHUNK])).then_inc(c_in[s], 16)

                pipeline(sp, CHUNKS, [(load, 0)], LS)

            @block.tensor
            def _(pe):
                pe.wait_ge(c_const, 81)

                def spread(m, s, h, first):
                    await_in_loop(pe, c_in[s], h * 48 + 48)
                    if not fresh(m, 2):
                        await_in_loop(pe, c_weighed, m - 1)
                    for b in range(2):
                        ins = nc.tensor.matmul(ps_w[s % 2][:, b, :], hs_sb[:, b, :], wr[s][:, :], start=True, stop=True)
                    ins.then_inc(c_spread, 1)

                def join(m, s, h, first):
                    await_in_loop(pe, c_weighed, m + 1)
                    if not fresh(m, 2):
                        await_in_loop(pe, c_run, m - 1)
                    for b in range(2):
                        ins = nc.tensor.matmul(ps_m[s % 2][:, :], hsum_sb[:, :], wm[s % 2][:, b, :], start=(b == 0), stop=(b == 1))
                    ins.then_inc(c_msg, 1)

                def turn_back(m, s, h, first):
                    await_in_loop(pe, c_biased, m + 1)
                    if not fresh(m, 2):
                        await_in_loop(pe, c_rows, m - 1)
                    for k in range(K):
                        ins = nc.tensor.transpose(ps_back[s % 2][:, k * D:(k + 1) * D], biased[s % 2][:, k * P:(k + 1) * P], eye[0:D, 0:D])
                    ins.then_inc(c_back, 1)

                pipeline(pe, CHUNKS, [(spread, 0), (join, 1), (turn_back, 3)], LS)

            @block.vector
            def _(dve):
                def weigh(m, s, h, first):
                    dve.wait_ge(c_spread, m + 1)
                    if not fresh(m, 2):
                        dve.wait_ge(c_msg, m - 1)
                    v.tensor_tensor(wm[s % 2][:, :, :], sj[s][:, :, :], ps_w[s % 2][:, :, :], ALU.mult).then_inc(c_weighed, 1)

                def scan(m, s, h, first):
                    dve.wait_ge(c_msg, m + 1)
                    dve.wait_ge(c_in[s], h * 48 + 48)
                    if not fresh(m, 2):
                        dve.wait_ge(c_biased, m - 1)
                    if not fresh(m, 1):
                        dve.wait_ge(c_run, m)
                    start = 0.0 if fresh(m, 1) else run[1 - s % 2][:, CHUNK - 1:CHUNK]
                    v.tensor_tensor_scan(run[s % 2][:, :], ct[s][:, :], ps_m[s % 2][:, :], start, ALU.mult, ALU.add).then_inc(c_run, 1)

                pipeline(dve, CHUNKS, [(weigh, 0), (scan, 1)], LS)

            @block.scalar
            def _(act):
                act.wait_ge(c_const, 80)
                nc.scalar.copy(hs_sb[:, :, :], hs_f[:, :, :]).then_inc(c_const, 1)

                def add_bias(m, s, h, first):
                    act.wait_ge(c_run, m + 1)
                    if not fresh(m, 2):
                        act.wait_ge(c_back, m - 1)
                    nc.scalar.activation(biased[s % 2][:, :], run[s % 2][:, :], ACT.Identity, bias=bias_col[:, 0:1]).then_inc(c_biased, 1)

                def rows(m, s, h, first):
                    act.wait_ge(c_back, m + 1)
                    if not fresh(m, 2):
                        act.wait_ge(c_out[s % 2], (h * 2 + s // 2) * (16 * K))
                    nc.scalar.copy(rows_sb[s % 2][:, :, :].rearrange("p k f -> p (k f)"), ps_back[s % 2][:, 0:K * D]).then_inc(c_rows, 1)

                pipeline(act, CHUNKS, [(add_bias, 1), (rows, 3)], LS)

            @block.gpsimd
            def _(pool):
                def scatter(m, s, h, first):
                    if not first:
                        await_in_loop(pool, c_out[s], h * (16 * K))
                    pool.tensor_copy(at_out[s][:, :], by_src[:, bass.ds(m * K, K), OUT]).then_inc(c_index, 1)
                    await_in_loop(pool, c_index, m + 1)
                    await_in_loop(pool, c_rows, m + 1)
                    for k in range(K):
                        pool.indirect_dma_start(msg0, bass.IndirectOffsetOnAxis(at_out[s][:, k:k + 1], 0), rows_sb[s][:, k, :],
                                                None, bounds_check=NPAD - 1, oob_is_err=False).then_inc(c_out[s], 16)

                pipeline(pool, CHUNKS, [(scatter, 2)])
                for s in range(2):
                    pool.wait_ge(c_out[s], 16 * K * (CHUNKS // 2))

        node_pass("l0", x, x1, h1)
        if "l0" in debug:
            return

        seg_in = [sem(f"seg_in{s}") for s in range(2)]
        seg_flags = [sem(f"seg_flags{s}") for s in range(2)]
        seg_index = sem("seg_index")
        seg_out_index = sem("seg_out_index")
        seg_turned = sem("seg_turned")
        seg_run = sem("seg_run")
        seg_back = sem("seg_back")
        seg_rows = sem("seg_rows")
        seg_out = [sem(f"seg_out{s}") for s in range(2)]
        seg_ones = sem("seg_ones")
        passes = [0]

        def sum_by_dst(name, table, target, width):
            base = passes[0] * CHUNKS
            half = passes[0] * 16 * (CHUNKS // 2)
            with ExitStack() as c:
                c.enter_context(nc.cleanup_on_exit())
                got = [sb_in(c, f"got_{name}{s}", [P, K, width]) for s in range(2)]
                at_in = [sb_in(c, f"at_in_{name}{s}", [P, K], i32) for s in range(2)]
                at_out = [sb_in(c, f"at_out_{name}{s}", [P, K], i32) for s in range(2)]
                ct = [sb_in(c, f"ct_{name}{s}", [80, CHUNK]) for s in range(2)]
                run = [sb_in(c, f"run_{name}{s}", [width, CHUNK]) for s in range(2)]
                rows_sb = [sb_in(c, f"rows_{name}{s}", [P, K, width]) for s in range(2)]
                ps_v = [ps_in(c, f"v_{name}{s}", [P, CHUNK]) for s in range(2)]
                ps_back = [ps_in(c, f"back_{name}{s}", [P, CHUNK]) for s in range(2)]
                block = c.enter_context(nc.Block())
                v = nc.vector

                @block.sync
                def _(sp):
                    def flags(m, s, h, first):
                        if not first:
                            await_in_loop(sp, seg_run, base + m - 1)
                        sp.dma_start(ct[s][:, :], same_dst[bass.ds(m * CHUNK, CHUNK)].rearrange("(o e) -> o e", o=1).to_broadcast([80, CHUNK])).then_inc(seg_flags[s], 16)

                    pipeline(sp, CHUNKS, [(flags, 0)])

                @block.gpsimd
                def _(pool):
                    if width > D:
                        for s in range(2):
                            pool.memset(got[s][:, :, :], 1.0).then_inc(seg_ones, 1)
                        pool.wait_ge(seg_ones, 2)

                    def gather(m, s, h, first):
                        if not first:
                            await_in_loop(pool, seg_in[s], h * (16 * K) + K * half)
                        pool.tensor_copy(at_in[s][:, :], by_dst[:, bass.ds(m * K, K), D_SRC]).then_inc(seg_index, 1)
                        await_in_loop(pool, seg_index, base + m + 1)
                        if not first:
                            await_in_loop(pool, seg_turned, base + m - 1)
                        for k in range(K):
                            pool.indirect_dma_start(got[s][:, k, 0:D], None, table,
                                                    bass.IndirectOffsetOnAxis(at_in[s][:, k:k + 1], 0)).then_inc(seg_in[s], 16)

                    def scatter(m, s, h, first):
                        if not first:
                            await_in_loop(pool, seg_out[s], h * (16 * K) + K * half)
                        pool.tensor_copy(at_out[s][:, :], by_dst[:, bass.ds(m * K, K), D_OUT]).then_inc(seg_out_index, 1)
                        await_in_loop(pool, seg_out_index, base + m + 1)
                        await_in_loop(pool, seg_rows, base + m + 1)
                        for k in range(K):
                            pool.indirect_dma_start(target, bass.IndirectOffsetOnAxis(at_out[s][:, k:k + 1], 0), rows_sb[s][:, k, :],
                                                    None, bounds_check=NPAD - 1, oob_is_err=False).then_inc(seg_out[s], 16)

                    pipeline(pool, CHUNKS, [(gather, 0), (scatter, 2)])
                    for s in range(2):
                        pool.wait_ge(seg_out[s], K * half + 16 * K * (CHUNKS // 2))

                @block.tensor
                def _(pe):
                    def turn(m, s, h, first):
                        await_in_loop(pe, seg_in[s], h * (16 * K) + (K * half + 16 * K))
                        if not first:
                            await_in_loop(pe, seg_run, base + m - 1)
                        for k in range(K):
                            ins = nc.tensor.transpose(ps_v[s][0:width, k * P:(k + 1) * P], got[s][:, k, :], eye[:, :])
                        ins.then_inc(seg_turned, 1)

                    def turn_back(m, s, h, first):
                        await_in_loop(pe, seg_run, base + m + 1)
                        if not first:
                            await_in_loop(pe, seg_rows, base + m - 1)
                        for k in range(K):
                            ins = nc.tensor.transpose(ps_back[s][:, k * width:(k + 1) * width], run[s][:, k * P:(k + 1) * P],
                                                      eye[0:width, 0:width])
                        ins.then_inc(seg_back, 1)

                    pipeline(pe, CHUNKS, [(turn, 0), (turn_back, 1)])

                @block.vector
                def _(dve):
                    def scan(m, s, h, first):
                        dve.wait_ge(seg_turned, base + m + 1)
                        dve.wait_ge(seg_flags[s], h * 16 + (half + 16))
                        if not first:
                            dve.wait_ge(seg_back, base + m - 1)
                        if not (first and m == 0):
                            dve.wait_ge(seg_run, base + m)
                        start = 0.0 if first and m == 0 else run[1 - s][:, CHUNK - 1:CHUNK]
                        v.tensor_tensor_scan(run[s][:, :], ct[s][0:width, :], ps_v[s][0:width, :], start, ALU.mult,
                                             ALU.add).then_inc(seg_run, 1)

                    pipeline(dve, CHUNKS, [(scan, 0)])

                @block.scalar
                def _(act):
                    def rows(m, s, h, first):
                        act.wait_ge(seg_back, base + m + 1)
                        if not first:
                            act.wait_ge(seg_out[s], h * (16 * K) + K * half)
                        nc.scalar.copy(rows_sb[s][:, :, :].rearrange("p k f -> p (k f)"), ps_back[s][:, 0:K * width]).then_inc(seg_rows, 1)

                    pipeline(act, CHUNKS, [(rows, 1)])
            passes[0] += 1

        sum_by_dst("mean", h1, msg1, D + 1)
        node_pass("l1", x1, x2, h2)
        if "l1" in debug:
            return

        with ExitStack() as c:
            c.enter_context(nc.cleanup_on_exit())
            hs = [sb_in(c, f"hs{s}", [P, K, D]) for s in range(GS)]
            hd = [sb_in(c, f"b_hd{s}", [P, K, D + 1]) for s in range(GS)]
            at = [sb_in(c, f"b_at{s}", [P, K, 4], i32) for s in range(GS)]
            at_out = [sb_in(c, f"b_at_out{s}", [P, K], i32) for s in range(GS)]
            ct = [sb_in(c, f"b_ct{s}", [80, CHUNK]) for s in range(GS)]
            ty = [sb_in(c, f"b_ty{s}", [D, CHUNK]) for s in range(GS)]
            hot = sb_in(c, "hot", [D, CHUNK])
            gate = sb_in(c, "gate", [D, CHUNK])
            prod = sb_in(c, "prod", [D, CHUNK])
            pen = sb_in(c, "pen", [D + 1, CHUNK])
            top = [sb_in(c, f"top{s}", [D + 1, CHUNK + 1]) for s in range(2)]
            drop = sb_in(c, "drop", [D + 1, CHUNK])
            drop2 = sb_in(c, "drop2", [D + 1, CHUNK])
            less = sb_in(c, "less", [D + 1, CHUNK])
            decay = sb_in(c, "decay", [D + 1, CHUNK])
            grow = sb_in(c, "grow", [D + 1, CHUNK])
            val = sb_in(c, "val", [D + 1, CHUNK])
            run = [sb_in(c, f"b_run{s}", [D + 1, CHUNK]) for s in range(2)]
            rows_sb = [sb_in(c, f"b_rows{s}", [P, K, D + 2]) for s in range(GS)]
            rel_sb = sb_in(c, "rel_sb", [D, D])
            ones = sb_in(c, "ones", [D, P])
            maxima = sb_in(c, "maxima", [P, CHUNKS])
            ps_g = ps_in(c, "g", [D, CHUNK])
            ps_t = [ps_in(c, f"b_t{s}", [D + 1, CHUNK]) for s in range(2)]
            ps_s = ps_in(c, "b_s", [P, CHUNK])
            ps_back = [ps_in(c, f"b_back{s}", [P, CHUNK]) for s in range(2)]
            b_const = sem_in(c, "b_const")
            b_in = [sem_in(c, f"b_in{s}") for s in range(GS)]
            b_flags = [sem_in(c, f"b_flags{s}") for s in range(GS)]
            b_index = sem_in(c, "b_index")
            b_out_index = sem_in(c, "b_out_index")
            names = ("hot", "pre", "turned", "gate", "prod", "score", "pen", "link", "top", "drop", "drop2", "less",
                     "decay", "grow", "val", "max", "run", "back", "rows")
            b = {n: sem_in(c, "b_" + n) for n in names}
            b_out = [sem_in(c, f"b_out{s}") for s in range(GS)]
            block = c.enter_context(nc.Block())
            v = nc.vector

            @block.sync
            def _(sp):
                sp.dma_start(rel_sb[:, :], rel).then_inc(b_const, 16)

                def load(m, s, h, first):
                    if not first:
                        await_in_loop(sp, b["pen"], m + 1 - GS)
                        await_in_loop(sp, b["hot"], m + 1 - GS)
                    sp.dma_start(ct[s][:, :], same_src[bass.ds(m * CHUNK, CHUNK)].rearrange("(o e) -> o e", o=1).to_broadcast([80, CHUNK])).then_inc(b_flags[s], 16)
                    sp.dma_start(ty[s][:, :], types_row.rearrange("t p -> (t p)")[bass.ds(m * CHUNK, CHUNK)].rearrange("(o e) -> o e", o=1).to_broadcast([D, CHUNK])).then_inc(b_flags[s], 16)

                pipeline(sp, CHUNKS, [(load, 0)], GS)

            @block.gpsimd
            def _(pool):
                for s in range(GS):
                    pool.memset(hd[s][:, :, :], 1.0).then_inc(b_const, 1)
                for s in range(2):
                    pool.memset(top[s][:, :], 0.0).then_inc(b_const, 1)
                pool.memset(ones[:, :], 1.0).then_inc(b_const, 1)
                pool.memset(maxima[:, :], -BIG).then_inc(b_const, 1)
                pool.wait_ge(b_const, 16 + GS + 4)

                def gather(m, s, h, first):
                    if not first:
                        await_in_loop(pool, b_in[s], h * (32 * K))
                    pool.tensor_copy(at[s][:, :, :], by_src[:, bass.ds(m * K, K), :]).then_inc(b_index, 1)
                    await_in_loop(pool, b_index, m + 1)
                    if not first:
                        await_in_loop(pool, b["turned"], m + 1 - GS)
                    for k in range(K):
                        pool.indirect_dma_start(hs[s][:, k, :], None, h2,
                                                bass.IndirectOffsetOnAxis(at[s][:, k, SRC:SRC + 1], 0)).then_inc(b_in[s], 16)
                    for k in range(K):
                        pool.indirect_dma_start(hd[s][:, k, 0:D], None, h2,
                                                bass.IndirectOffsetOnAxis(at[s][:, k, DST:DST + 1], 0)).then_inc(b_in[s], 16)

                def scatter(m, s, h, first):
                    if not first:
                        await_in_loop(pool, b_out[s], h * (16 * K))
                    pool.tensor_copy(at_out[s][:, :], by_src[:, bass.ds(m * K, K), OUT]).then_inc(b_out_index, 1)
                    await_in_loop(pool, b_out_index, m + 1)
                    await_in_loop(pool, b["rows"], m + 1)
                    for k in range(K):
                        pool.indirect_dma_start(msg2, bass.IndirectOffsetOnAxis(at_out[s][:, k:k + 1], 0), rows_sb[s][:, k, :],
                                                None, bounds_check=NPAD - 1, oob_is_err=False).then_inc(b_out[s], 16)

                pipeline(pool, CHUNKS, [(gather, 0), (scatter, 3)], GS)
                for s in range(GS):
                    pool.wait_ge(b_out[s], 16 * K * times(s, GS))

            @block.tensor
            def _(pe):
                pe.wait_ge(b_const, 16 + GS + 4)

                def ends(m, s, h, first):
                    await_in_loop(pe, b["hot"], m + 1)
                    await_in_loop(pe, b_in[s], h * (32 * K) + 32 * K)
                    if not (fresh(m, 1)):
                        await_in_loop(pe, b["gate"], m)
                    nc.tensor.matmul(ps_g[:, :], rel_sb[:, :], hot[:, :], start=True, stop=False)
                    for k in range(K):
                        ins = nc.tensor.matmul(ps_g[:, k * P:(k + 1) * P], hs[s][:, k, :], eye[:, :], start=False, stop=(k == K - 1))
                    ins.then_inc(b["pre"], 1)
                    if not fresh(m, 2):
                        await_in_loop(pe, b["val"], m - 1)
                    for k in range(K):
                        ins = nc.tensor.transpose(ps_t[s % 2][:, k * P:(k + 1) * P], hd[s][:, k, :], eye[:, :])
                    ins.then_inc(b["turned"], 1)

                def score(m, s, h, first):
                    await_in_loop(pe, b["prod"], m + 1)
                    if not (fresh(m, 1)):
                        await_in_loop(pe, b["less"], m)
                        await_in_loop(pe, b["max"], m)
                    nc.tensor.matmul(ps_s[:, :], ones[:, :], prod[:, :], start=True, stop=True).then_inc(b["score"], 1)

                def turn_back(m, s, h, first):
                    await_in_loop(pe, b["run"], m + 1)
                    await_in_loop(pe, b["top"], m + 1)
                    if not fresh(m, 2):
                        await_in_loop(pe, b["rows"], m - 1)
                    for k in range(K):
                        nc.tensor.transpose(ps_back[s % 2][:, k * (D + 2):k * (D + 2) + D + 1], run[s % 2][:, k * P:(k + 1) * P],
                                            eye[0:D + 1, 0:D + 1])
                        ins = nc.tensor.transpose(ps_back[s % 2][:, k * (D + 2) + D + 1:(k + 1) * (D + 2)],
                                                  top[s % 2][0:1, 1 + k * P:1 + (k + 1) * P], eye[0:1, 0:1])
                    ins.then_inc(b["back"], 1)

                pipeline(pe, CHUNKS, [(ends, 0), (turn_back, 2), (score, 0)], GS)

            @block.vector
            def _(dve):
                dve.wait_ge(b_const, 16 + GS + 4)

                def types(m, s, h, first):
                    dve.wait_ge(b_flags[s], h * 32 + 32)
                    if not (fresh(m, 1)):
                        dve.wait_ge(b["pre"], m)
                    v.tensor_scalar(hot[:, :], ty[s][:, :], pid[0:D, 0:1], None, ALU.is_equal).then_inc(b["hot"], 1)

                def gated(m, s, h, first):
                    zero = fresh(m, 1)
                    dve.wait_ge(b["gate"], m + 1)
                    dve.wait_ge(b["turned"], m + 1)
                    if not zero:
                        dve.wait_ge(b["score"], m)
                    v.tensor_tensor(prod[:, :], gate[:, :], ps_t[s % 2][0:D, :], ALU.mult).then_inc(b["prod"], 1)

                def attend(m, s, h, first):
                    zero = fresh(m, 1)
                    dve.wait_ge(b["pen"], m + 1)
                    dve.wait_ge(b["score"], m + 1)
                    if not fresh(m, 2):
                        dve.wait_ge(b["back"], m - 1)
                    if not zero:
                        dve.wait_ge(b["top"], m)
                        dve.wait_ge(b["link"], m)
                    start = -BIG if zero else top[(s + 1) % 2][:, CHUNK:CHUNK + 1]
                    v.tensor_tensor_scan(top[s % 2][:, 1:CHUNK + 1], pen[:, :], ps_s[0:D + 1, :], start, ALU.add,
                                         ALU.max).then_inc(b["top"], 1)
                    dve.wait_ge(b["top"], m + 1)
                    v.tensor_tensor(less[:, :], ps_s[0:D + 1, :], top[s % 2][:, 1:CHUNK + 1], ALU.subtract).then_inc(b["less"], 1)
                    dve.wait_ge(b["link"], m + 1)
                    v.tensor_tensor(drop[:, :], top[s % 2][:, 0:CHUNK], top[s % 2][:, 1:CHUNK + 1], ALU.subtract).then_inc(b["drop"], 1)
                    dve.wait_ge(b["drop"], m + 1)
                    if not zero:
                        dve.wait_ge(b["decay"], m)
                    v.tensor_tensor(drop2[:, :], drop[:, :], pen[:, :], ALU.add).then_inc(b["drop2"], 1)
                    real = LAST_REAL if isinstance(m, int) and m == CHUNKS - 1 else CHUNK
                    v.tensor_reduce(maxima[:, bass.ds(m, 1)], ps_s[:, 0:real], AX, ALU.max).then_inc(b["max"], 1)
                    dve.wait_ge(b["grow"], m + 1)
                    if not zero:
                        dve.wait_ge(b["run"], m)
                    v.tensor_tensor(val[:, :], grow[:, :], ps_t[s % 2][:, :], ALU.mult).then_inc(b["val"], 1)
                    dve.wait_ge(b["val"], m + 1)
                    dve.wait_ge(b["decay"], m + 1)
                    start = 0.0 if zero else run[(s + 1) % 2][:, CHUNK - 1:CHUNK]
                    v.tensor_tensor_scan(run[s % 2][:, :], decay[:, :], val[:, :], start, ALU.mult, ALU.add).then_inc(b["run"], 1)

                pipeline(dve, CHUNKS, [(types, 0), (attend, 1), (gated, 0)], GS, peel_last=True)
                dve.wait_ge(b["max"], CHUNKS)
                v.tensor_reduce(gmax[:, :], maxima[:, :], AX, ALU.max).then_inc(b["max"], 1)
                dve.wait_ge(b["max"], CHUNKS + 1)

            @block.scalar
            def _(act):
                act.wait_ge(b_const, 16 + GS + 4)

                def attend(m, s, h, first):
                    zero = fresh(m, 1)
                    act.wait_ge(b_flags[s], h * 32 + 32)
                    if not zero:
                        act.wait_ge(b["drop2"], m)
                        act.wait_ge(b["top"], m)
                    nc.scalar.activation(pen[:, :], ct[s][0:D + 1, :], ACT.Copy, scale=BIG, bias=-BIG).then_inc(b["pen"], 1)
                    if zero:
                        act.sem_inc(b["link"], 1)
                    else:
                        act.wait_ge(b["top"], m)
                        nc.scalar.copy(top[s % 2][:, 0:1], top[(s + 1) % 2][:, CHUNK:CHUNK + 1]).then_inc(b["link"], 1)
                    act.wait_ge(b["less"], m + 1)
                    if not zero:
                        act.wait_ge(b["val"], m)
                    nc.scalar.activation(grow[:, :], less[:, :], ACT.Exp).then_inc(b["grow"], 1)
                    act.wait_ge(b["drop2"], m + 1)
                    if not zero:
                        act.wait_ge(b["run"], m)
                    nc.scalar.activation(decay[:, :], drop2[:, :], ACT.Exp).then_inc(b["decay"], 1)

                def tanh(m, s, h, first):
                    act.wait_ge(b["pre"], m + 1)
                    if not fresh(m, 1):
                        act.wait_ge(b["prod"], m)
                    nc.scalar.activation(gate[:, :], ps_g[:, :], ACT.Tanh).then_inc(b["gate"], 1)

                def rows(m, s, h, first):
                    act.wait_ge(b["back"], m + 1)
                    if not first:
                        act.wait_ge(b_out[s], h * (16 * K))
                    nc.scalar.copy(rows_sb[s][:, :, :].rearrange("p k f -> p (k f)"), ps_back[s % 2][:, 0:K * (D + 2)]).then_inc(b["rows"], 1)

                pipeline(act, CHUNKS, [(rows, 2), (attend, 1), (tanh, 0)], GS)

        node_pass("l2", x2, x3, feat)
        if "l2" in debug:
            return

        sum_by_dst("hop0", g0, hop0, D)

        with ExitStack() as c:
            c.enter_context(nc.cleanup_on_exit())
            gi = [sb_in(c, f"gi{s}", [P, ROWS, D]) for s in range(2)]
            go = [sb_in(c, f"go{s}", [P, ROWS, D]) for s in range(2)]
            g_in = [sem_in(c, f"g_in{s}") for s in range(2)]
            g_scaled = sem_in(c, "g_scaled")
            g_out = [sem_in(c, f"g_out{s}") for s in range(2)]
            block = c.enter_context(nc.Block())

            @block.sync
            def _(sp):
                def load(m, s, h, first):
                    if not first:
                        await_in_loop(sp, g_scaled, m - 1)
                    sp.dma_start(gi[s][:, :, :].rearrange("p k (o f) -> p o (k f)", o=1), rows_of(hop0, m)).then_inc(g_in[s], 16)

                pipeline(sp, NCHUNKS, [(load, 0)])

            @block.scalar
            def _(act):
                def store(m, s, h, first):
                    act.wait_ge(g_scaled, m + 1)
                    act.dma_start(rows_of(g1, m), go[s][:, :, :].rearrange("p k (o f) -> p o (k f)", o=1)).then_inc(g_out[s], 16)

                pipeline(act, NCHUNKS, [(store, 0)])
                for s in range(2):
                    act.wait_ge(g_out[s], 16 * (NCHUNKS // 2))

            @block.vector
            def _(dve):
                def scale(m, s, h, first):
                    dve.wait_ge(g_in[s], h * 16 + 16)
                    if not first:
                        dve.wait_ge(g_out[s], h * 16)
                    nc.vector.tensor_tensor(go[s][:, :, :], gi[s][:, :, :],
                                            inv_deg2[:, bass.ds(m, 1), :].rearrange("p o k -> p k o").to_broadcast([P, ROWS, D]),
                                            ALU.mult).then_inc(g_scaled, 1)

                pipeline(dve, NCHUNKS, [(scale, 0)])

        sum_by_dst("hop1", g1, hop1, D)

        with ExitStack() as c:
            c.enter_context(nc.cleanup_on_exit())
            xi = [sb_in(c, f"o_xi{s}", [P, ROWS, D]) for s in range(2)]
            hi = [sb_in(c, f"o_hi{s}", [P, ROWS, D]) for s in range(2)]
            both = [sb_in(c, f"both{s}", [P, ROWS, 2 * D]) for s in range(2)]
            bt = [sb_in(c, f"bt{s}", [P, ROWS * P]) for s in range(2)]
            xb = [sb_in(c, f"o_xb{s}", [P, ROWS, D]) for s in range(2)]
            oo = [sb_in(c, f"o_oo{s}", [P, ROWS, D]) for s in range(2)]
            w3_sb = sb_in(c, "w3_sb", [P, D])
            bsum = sb_in(c, "bsum", [P, D])
            ps_bt = ps_in(c, "bt", [P, ROWS * P])
            ps_o = [ps_in(c, f"o{s}", [P, ROWS * D]) for s in range(2)]
            o_const = sem_in(c, "o_const")
            o_in = [sem_in(c, f"o_in{s}") for s in range(2)]
            o = {n: sem_in(c, "o_" + n) for n in ("scaled", "biased", "turned", "copied", "prod", "sum")}
            o_out = [sem_in(c, f"o_out{s}") for s in range(2)]
            block = c.enter_context(nc.Block())
            v = nc.vector

            @block.sync
            def _(sp):
                sp.dma_start(w3_sb[:, :], w3).then_inc(o_const, 16)
                sp.dma_start(b3_b[:, 0, :], b3.to_broadcast([P, D])).then_inc(o_const, 16)
                sp.dma_start(b3_b[:, 1, :], br3.to_broadcast([P, D])).then_inc(o_const, 16)

                def load(m, s, h, first):
                    if not first:
                        await_in_loop(sp, o["scaled"], m - 1)
                        await_in_loop(sp, o["biased"], m - 1)
                        await_in_loop(sp, o["turned"], m - 1)
                    sp.dma_start(hi[s][:, :, :].rearrange("p k (o f) -> p o (k f)", o=1), rows_of(hop1, m)).then_inc(o_in[s], 16)
                    sp.dma_start(xi[s][:, :, :].rearrange("p k (o f) -> p o (k f)", o=1), rows_of(x3, m)).then_inc(o_in[s], 16)
                    sp.dma_start(both[s][:, :, D:2 * D], feat.rearrange("(c p k) f -> c p k f", p=P, k=ROWS)[bass.ds(m, 1), :, :, :].rearrange("o p k f -> (o p) k f")).then_inc(o_in[s], 16)

                def store(m, s, h, first):
                    await_in_loop(sp, o["sum"], m + 1)
                    sp.dma_start(rows_of(out, m), oo[s][:, :, :].rearrange("p k (o f) -> p o (k f)", o=1)).then_inc(o_out[s], 16)

                pipeline(sp, NCHUNKS, [(load, 0), (store, 1)])
                for s in range(2):
                    await_in_loop(sp, o_out[s], 16 * (NCHUNKS // 2))

            @block.gpsimd
            def _(pool):
                pool.wait_ge(o_const, 48)
                pool.tensor_tensor(bsum[:, :], b3_b[:, 0, :], b3_b[:, 1, :], ALU.add).then_inc(o_const, 1)
                pool.wait_ge(o_const, 49)

                def bias(m, s, h, first):
                    await_in_loop(pool, o_in[s], h * 48 + 48)
                    if not first:
                        await_in_loop(pool, o["sum"], m - 1)
                    pool.tensor_tensor(xb[s][:, :, :], xi[s][:, :, :],
                                       bsum[:, :].rearrange("p (o f) -> p o f", o=1).to_broadcast([P, ROWS, D]), ALU.add).then_inc(o["biased"], 1)

                pipeline(pool, NCHUNKS, [(bias, 0)])

            @block.vector
            def _(dve):
                def scale(m, s, h, first):
                    dve.wait_ge(o_in[s], h * 48 + 48)
                    if not first:
                        dve.wait_ge(o["turned"], m - 1)
                    v.tensor_tensor(both[s][:, :, 0:D], hi[s][:, :, :],
                                    inv_deg[:, bass.ds(m, 1), :].rearrange("p o k -> p k o").to_broadcast([P, ROWS, D]),
                                    ALU.mult).then_inc(o["scaled"], 1)

                def add(m, s, h, first):
                    dve.wait_ge(o["prod"], m + 1)
                    dve.wait_ge(o["biased"], m + 1)
                    if not first:
                        dve.wait_ge(o_out[s], h * 16)
                    v.tensor_tensor(oo[s][:, :, :].rearrange("p k f -> p (k f)"), ps_o[s][:, :],
                                    xb[s][:, :, :].rearrange("p k f -> p (k f)"), ALU.add).then_inc(o["sum"], 1)

                pipeline(dve, NCHUNKS, [(scale, 0), (add, 1)])

            @block.scalar
            def _(act):
                def copy(m, s, h, first):
                    act.wait_ge(o["turned"], m + 1)
                    if not first:
                        act.wait_ge(o["prod"], m - 1)
                    nc.scalar.copy(bt[s][:, :], ps_bt[:, :]).then_inc(o["copied"], 1)

                pipeline(act, NCHUNKS, [(copy, 0)])

            @block.tensor
            def _(pe):
                pe.wait_ge(o_const, 48)

                def turn(m, s, h, first):
                    await_in_loop(pe, o_in[s], h * 48 + 48)
                    await_in_loop(pe, o["scaled"], m + 1)
                    if not (first and m == 0):
                        await_in_loop(pe, o["copied"], m)
                    for k in range(ROWS):
                        ins = nc.tensor.transpose(ps_bt[:, k * P:(k + 1) * P], both[s][:, k, :], eye[:, :])
                    ins.then_inc(o["turned"], 1)

                def project(m, s, h, first):
                    await_in_loop(pe, o["copied"], m + 1)
                    if not first:
                        await_in_loop(pe, o["sum"], m - 1)
                    for k in range(ROWS):
                        ins = nc.tensor.matmul(ps_o[s][:, k * D:(k + 1) * D], bt[s][:, k * P:(k + 1) * P], w3_sb[:, :],
                                               start=True, stop=True)
                    ins.then_inc(o["prod"], 1)

                pipeline(pe, NCHUNKS, [(turn, 0), (project, 0)])




_CONSTS = {}


def _layouts(a):
    import numpy as np

    f = np.float32
    def pad(t, n, fill):
        full = np.full((n,) + t.shape[1:], fill, t.dtype)
        full[:t.shape[0]] = t
        return full
    src, dst, typ = (np.asarray(a[k]).astype(np.int32) for k in ("src", "dst", "edge_type_64"))
    ea = np.ascontiguousarray(a["edge_attr_64"])
    rec = np.concatenate([pad(ea, NPAD, 0).view(np.int32), pad(dst, NPAD, N)[:, None], pad(typ, NPAD, 0)[:, None]], 1)
    att = np.asarray(a["L0_gnn_att"])
    att_sel = np.zeros((P, 4, HEADS), f)
    for side in range(2):
        for b in range(2):
            for hh in range(2):
                att_sel[hh * D:(hh + 1) * D, 2 * side + b, 2 * b + hh] = att[0, 2 * b + hh, side * D:(side + 1) * D]
    headsel = np.zeros((HEADS, 2, P), f)
    for h in range(HEADS):
        headsel[h, h // 2, (h % 2) * D:(h % 2 + 1) * D] = 1
    headsum = np.concatenate([np.eye(D, dtype=f)] * 2, 0)
    q = np.arange(P)
    samehead = (q[:, None] % HEADS == q[None] % HEADS).astype(f)
    w2 = np.zeros((P, P), f)
    for b in range(2):
        w2[b * D:(b + 1) * D, b * D:(b + 1) * D] = np.asarray(a["L2_gnn_W"]).T
    w3 = np.concatenate([np.asarray(a["L3_gnn_W"]).T, np.asarray(a["L3_gnn_Wr"]).T], 0)
    return {
        "x": pad(np.asarray(a["x"]), NPAD, 0), "rec": rec,
        "src": pad(src, SORT_N, N), "dst": pad(dst, SORT_N, N), "ident": np.eye(P, dtype=f),
        "w0": np.asarray(a["L0_gnn_W"]), "att": att_sel.reshape(P, 4 * HEADS), "bias0": np.asarray(a["L0_gnn_bias"])[None],
        "gamma": np.tile(np.asarray(a["L0_gnn_bn_gamma"]), SEGS)[:, None],
        "beta": np.tile(np.asarray(a["L0_gnn_bn_beta"]), SEGS)[:, None],
        "headsel": headsel.reshape(HEADS, 2 * P), "headsum": headsum, "samehead": samehead,
        "rel": np.asarray(a["L2_gnn_rel_embed"]), "w2": w2, "w3": w3,
        "b3": np.asarray(a["L3_gnn_b"])[None], "br3": np.asarray(a["L3_gnn_br"])[None],
    }


def kernel(**inputs):
    import numpy as _np
    import concourse.bacc as _bacc
    from concourse import mybir as _mybir
    from concourse.bass_utils import run_bass_kernel_spmd as _run

    nc = _bacc.Bacc("TRN2", target_bir_lowering=False, num_devices=1)
    arrays, args = {}, []
    for name, a in _layouts(inputs).items():
        a = _np.ascontiguousarray(a)
        arrays[f"in_{name}_dram"] = a
        args.append(nc.dram_tensor(f"in_{name}_dram", a.shape, _mybir.dt.from_np(a.dtype), kind="ExternalInput").ap())
    out = nc.dram_tensor("out_dram", (NPAD, D), _mybir.dt.float32, kind="ExternalOutput").ap()
    gnn_kernel(nc, *args, out)
    r = _run(nc, [arrays], core_ids=[0])
    return r.results[0]["out_dram"][:N]
```

```python
import concourse.bass as bass
from concourse import mybir
from contextlib import ExitStack

P = 128
D = 64
N = 50000
TILES = 392
NPAD = TILES * P
K = 4
CHUNK = K * P
CHUNKS = TILES // K
LAST_REAL = N - (CHUNKS - 1) * CHUNK
NS = 5
OS = 6
GS = 4
ROWS = 8
NCHUNKS = TILES // ROWS
SORT_N = 1 << 16
SORT_F = SORT_N // P
HEADS = 4
OOB = 200000.0
SPLIT = 32384
NEG_TOP = 0xFFFF - 0x80
POS_OFF = SPLIT - 0x80
BIG = 1e30
CLAMP = 30.0
LN_EPS = 1e-5
SEGS = 32
SEG_LEN = NPAD // SEGS

EDGE, SRC, OUT, DST = range(4)
D_SRC, D_OUT = range(2)

fp32 = mybir.dt.float32
bf16 = mybir.dt.bfloat16
i32 = mybir.dt.int32
u32 = mybir.dt.uint32
ALU = mybir.AluOpType
ACT = mybir.ActivationFunctionType
AX = mybir.AxisListType.X

def gnn_kernel(nc, x, rec, src, dst, ident, w0, att, bias0, gamma, beta, headsel, headsum, samehead,
               rel, w2, w3, b3, br3, out):
    ctx = ExitStack()

    def dram(name, shape, dt=fp32):
        return nc.dram_tensor(name, shape, dt, kind="Internal").ap()

    h0 = dram("h0", (NPAD, D))
    h1 = dram("h1", (NPAD, D))
    h2 = dram("h2", (NPAD, D))
    x1 = dram("x1", (NPAD, D))
    x2 = dram("x2", (NPAD, D))
    x3 = dram("x3", (NPAD, D))
    feat = dram("feat", (NPAD, D))
    g0 = dram("g0", (NPAD, D + 1))
    msg0 = dram("msg0", (NPAD, D))
    msg1 = dram("msg1", (NPAD, D + 2))
    msg2 = dram("msg2", (NPAD, D + 2))
    hop0 = dram("hop0", (NPAD + 1, D))
    hop1 = dram("hop1", (NPAD, D))
    same_src = dram("same_src", (SORT_N,))
    same_dst = dram("same_dst", (SORT_N,))
    sp_j = dram("sp_j", (CHUNKS, 2, P, CHUNK))
    logits = dram("logits", (HEADS, NPAD))
    weights = dram("weights", (3, HEADS, NPAD), bf16)
    types_row = dram("types_row", (TILES, P))

    with ctx:
        def sb_in(c, name, shape, dt=fp32):
            return c.enter_context(nc.sbuf_tensor("sb_" + name, shape, dt))

        def ps_in(c, name, shape):
            return c.enter_context(nc.psum_tensor("ps_" + name, shape, fp32))

        def sem_in(c, name):
            return nc.alloc_semaphore(name=name)

        def sb(name, shape, dt=fp32):
            return sb_in(ctx, name, shape, dt)

        def sem(name):
            return ctx.enter_context(nc.semaphore(name))

        by_src = sb("by_src", [P, SORT_F, 4], i32)
        by_dst = sb("by_dst", [P, SORT_F, 2], i32)
        type_of = sb("type_of", [P, TILES])
        inv_deg = sb("inv_deg", [P, NCHUNKS, ROWS])
        eye = sb("eye", [P, P])
        pid = sb("pid", [P, 1])
        ready = sem("ready")

        def await_in_loop(eng, semaphore, value):
            eng.wait_ge(semaphore, value)
            eng.sem_inc(ready, 1)

        with ExitStack() as c:
            c.enter_context(nc.cleanup_on_exit())
            raw = [sb_in(c, "raw_src", [P, SORT_F], i32), sb_in(c, "raw_dst", [P, SORT_F], i32)]
            slot = sb_in(c, "slot", [P, SORT_F], i32)
            pidi = sb_in(c, "pidi", [P, 1], i32)
            signs_i = sb_in(c, "signs_i", [P, 8], i32)
            signs_t = sb_in(c, "signs_t", [P, 8], i32)
            signs = sb_in(c, "signs", [P, 8])
            key = [[sb_in(c, f"key{a}{b}", [P, SORT_F]) for b in range(2)] for a in range(2)]
            below = [sb_in(c, f"below{a}", [P, SORT_F]) for a in range(2)]
            work = [sb_in(c, f"work{a}", [P, SORT_F]) for a in range(2)]
            high = [sb_in(c, f"high{a}", [P, SORT_F], i32) for a in range(2)]
            node = [sb_in(c, f"node{a}", [P, SORT_F + 2]) for a in range(2)]
            same = [sb_in(c, f"same{a}", [P, SORT_F]) for a in range(2)]
            more = [sb_in(c, f"more{a}", [P, SORT_F]) for a in range(2)]
            dest = [sb_in(c, f"dest{a}", [P, SORT_F]) for a in range(2)]
            load_f = [sb_in(c, f"load_f{a}", [P, SORT_F]) for a in range(2)]
            zeros = sb_in(c, "zeros", [P, TILES])
            bias_rep = sb_in(c, "bias_rep", [P, 8, D])
            turned = [ps_in(c, f"turned{a}", [P, 4, P]) for a in range(2)]
            final = [ps_in(c, f"final{n}", [P, 4, P]) for n in range(5)]
            loaded = sem_in(c, "loaded")
            counted = sem_in(c, "counted")
            chain = [sem_in(c, f"sort_chain{a}") for a in range(2)]
            signed = sem_in(c, "signed")
            handed = [sem_in(c, f"handed{a}") for a in range(2)]
            moved = [sem_in(c, f"moved{a}") for a in range(2)]
            back = [sem_in(c, f"back{a}") for a in range(2)]
            shifted = [sem_in(c, f"shifted{a}") for a in range(2)]
            flags_out = sem_in(c, "flags_out")
            zeroed = sem_in(c, "zeroed")
            bias_in = sem_in(c, "bias_in")
            empty_out = sem_in(c, "empty_out")
            decoded = [sem_in(c, f"decoded{a}") for a in range(2)]
            final_t = sem_in(c, "final_t")
            final_c = sem_in(c, "final_c")

            block = c.enter_context(nc.Block())
            FIRST_CROSS = 10
            TURNS = 2 * (17 - FIRST_CROSS)

            @block.sync
            def _(sp):
                sp.dma_start(raw[0][:, :], src.rearrange("(p f) -> p f", p=P)).then_inc(loaded, 16)
                sp.dma_start(raw[1][:, :], dst.rearrange("(p f) -> p f", p=P)).then_inc(loaded, 16)
                sp.dma_start(eye[:, :], ident).then_inc(loaded, 16)
                sp.dma_start(bias_rep[:, :, :], bias0.rearrange("(a o) f -> a o f", o=1).to_broadcast([P, 8, D])).then_inc(bias_in, 16)
                sp.wait_ge(bias_in, 16)
                sp.dma_start(msg0.rearrange("(p w a) f -> p w (a f)", p=P, a=8),
                             bias_rep[:, :, :].rearrange("p a (o f) -> p o (a f)", o=1).to_broadcast([P, TILES // 8, 8 * D])).then_inc(empty_out, 16)
                sp.wait_ge(zeroed, 1)
                sp.dma_start(hop0[0:1, :], zeros[0:1, 0:D]).then_inc(empty_out, 16)
                tables = ((msg1, D + 2), (msg2, D + 2), (hop1, D))
                for table, width in tables:
                    sp.dma_start(table.rearrange("(p a) f -> p (a f)", p=P).rearrange("p (w a) -> p w a", a=TILES),
                                 zeros[:, :].rearrange("p (o a) -> p o a", o=1).to_broadcast([P, width, TILES])).then_inc(empty_out, 16)
                for a in range(2):
                    sp.wait_ge(decoded[a], 1)
                    sp.dma_start(node[a][1:P, 0:1], node[a][0:P - 1, SORT_F:SORT_F + 1]).then_inc(shifted[a], 16)
                    sp.dma_start(node[a][0:P - 1, SORT_F + 1:SORT_F + 2], node[a][1:P, 1:2]).then_inc(shifted[a], 16)
                for a, flags in enumerate((same_src, same_dst)):
                    sp.wait_ge(decoded[a], 2)
                    sp.dma_start(flags.rearrange("(p f) -> p f", p=P), same[a][:, :]).then_inc(flags_out, 16)
                sp.wait_ge(flags_out, 32)
                sp.wait_ge(empty_out, 16 * (len(tables) + 2))

            @block.gpsimd
            def _(pool):
                pool.iota(slot[:, :], pattern=[[1, SORT_F]], base=0, channel_multiplier=SORT_F).then_inc(counted, 1)
                pool.iota(pidi[:, :], pattern=[[0, 1]], base=0, channel_multiplier=1).then_inc(counted, 1)
                pool.memset(zeros[:, :], 0.0).then_inc(zeroed, 1)

            @block.vector
            def _(dve):
                v = nc.vector
                done = [0, 0]

                def link(a, ins):
                    done[a] += 1
                    ins.then_inc(chain[a], 1)

                def after(a):
                    if done[a]:
                        dve.wait_ge(chain[a], done[a])

                dve.wait_ge(counted, 2)
                v.tensor_copy(pid[:, :], pidi[:, :]).then_inc(signed, 1)
                v.tensor_scalar(signs_t[:, 0:1], pidi[:, :], 1, None, ALU.logical_shift_right).then_inc(signed, 1)
                dve.wait_ge(signed, 2)
                v.tensor_tensor(signs_t[:, 1:2], pidi[:, :], signs_t[:, 0:1], ALU.bitwise_xor).then_inc(signed, 1)
                dve.wait_ge(signed, 3)
                v.tensor_scalar(signs_i[:, 0:1], pidi[:, :], 1, None, ALU.bitwise_and).then_inc(signed, 1)
                for m in range(1, 8):
                    v.tensor_scalar(signs_i[:, m:m + 1], signs_t[:, 1:2], m - 1, 1, ALU.logical_shift_right,
                                    ALU.bitwise_and).then_inc(signed, 1)
                dve.wait_ge(signed, 11)
                v.tensor_scalar(signs[:, :], signs_i[:, :], -2.0, 1.0, ALU.mult, ALU.add).then_inc(signed, 1)
                dve.wait_ge(signed, 12)
                dve.wait_ge(loaded, 48)
                payload = [slot, raw[0]]
                for a in range(2):
                    link(a, v.tensor_scalar(below[a][:, :], raw[a][:, :], float(SPLIT), None, ALU.is_lt))
                    link(a, v.tensor_scalar(work[a][:, :], raw[a][:, :], -2.0, float(NEG_TOP + POS_OFF), ALU.mult, ALU.add))
                for a in range(2):
                    after(a)
                    link(a, v.tensor_tensor(work[a][:, :], work[a][:, :], below[a][:, :], ALU.mult))
                for a in range(2):
                    after(a)
                    link(a, v.scalar_tensor_tensor(high[a][:, :], raw[a][:, :], float(-POS_OFF), work[a][:, :],
                                                   ALU.add, ALU.add))
                for a in range(2):
                    after(a)
                    link(a, v.tensor_scalar(high[a][:, :], high[a][:, :], 16, None, ALU.logical_shift_left))
                for a in range(2):
                    after(a)
                    link(a, v.tensor_tensor(key[a][0].bitcast(i32)[:, :], high[a][:, :], payload[a][:, :], ALU.bitwise_or))

                def flip(a, b, lo_bit, lo, hi, w=2):
                    t = key[a][b][:, :].rearrange("p (g h l s) -> p g h l s", h=w, l=2, s=1 << lo_bit)[:, :, hi, lo, :]
                    link(a, v.tensor_scalar(t, t, -1.0, None, ALU.mult))

                at = [0, 0]
                turns = [0, 0]
                for a in range(2):
                    after(a)
                    flip(a, 0, 1, 1, 0)
                    flip(a, 0, 1, 1, 1)

                def stage(a, bit, last):
                    s, t = key[a][at[a]], key[a][1 - at[a]]
                    sv = s[:, :].rearrange("p (g two s) -> p g two s", two=2, s=1 << bit)
                    tv = t[:, :].rearrange("p (g two s) -> p g two s", two=2, s=1 << bit)
                    for side, op in ((0, ALU.min), (1, ALU.max)):
                        ins = v.tensor_tensor(tv[:, :, side, :], sv[:, :, 0, :], sv[:, :, 1, :], op)
                        if last:
                            ins.then_inc(handed[a], 1)
                        else:
                            link(a, ins)
                    at[a] = 1 - at[a]

                for k in range(1, 17):
                    if k >= FIRST_CROSS:
                        for bit in range(k - 1, 6, -1):
                            for a in range(2):
                                if bit == k - 1:
                                    dve.wait_ge(moved[a], turns[a] + 1)
                                    turns[a] += 1
                                    at[a] = 1 - at[a]
                                else:
                                    after(a)
                                stage(a, bit - 7, bit == 7)
                        low = 6
                    else:
                        low = k - 1
                    for bit in range(low, -1, -1):
                        for a in range(2):
                            if k >= FIRST_CROSS and bit == 6:
                                dve.wait_ge(moved[a], turns[a] + 1)
                                turns[a] += 1
                                at[a] = 1 - at[a]
                            else:
                                after(a)
                            stage(a, bit, False)
                    if k < 16:
                        for a in range(2):
                            after(a)
                            if k < 8:
                                flip(a, at[a], k, 1, 0)
                                flip(a, at[a], k, 0, 1)
                            else:
                                if k == 8:
                                    flip(a, at[a], 8, 1, 0, w=1)
                                    after(a)
                                ins = v.tensor_scalar(key[a][1 - at[a]][:, :], key[a][at[a]][:, :],
                                                      signs[:, k - 8:k - 7], None, ALU.mult)
                                at[a] = 1 - at[a]
                                if k + 1 >= FIRST_CROSS:
                                    ins.then_inc(handed[a], 2)
                                else:
                                    link(a, ins)
                for a in range(2):
                    after(a)
                    bits = key[a][at[a]].bitcast(i32)
                    link(a, v.tensor_scalar(high[a][:, :], bits[:, :], 16, None, ALU.logical_shift_right))
                    link(a, v.tensor_scalar(raw[a][:, :], bits[:, :], 0xFFFF, None, ALU.bitwise_and))
                    link(a, v.memset(node[a][:, :], -1.0))
                for a in range(2):
                    after(a)
                    link(a, v.tensor_scalar(below[a][:, :], high[a][:, :], 32768.0, None, ALU.is_ge))
                    link(a, v.tensor_scalar(work[a][:, :], high[a][:, :], -2.0, float(NEG_TOP - POS_OFF), ALU.mult, ALU.add))
                    link(a, v.tensor_copy(load_f[a][:, :], raw[a][:, :]))
                for a in range(2):
                    after(a)
                    link(a, v.tensor_tensor(work[a][:, :], work[a][:, :], below[a][:, :], ALU.mult))
                for a in range(2):
                    after(a)
                    v.scalar_tensor_tensor(node[a][:, 1:SORT_F + 1], high[a][:, :], float(POS_OFF), work[a][:, :],
                                           ALU.add, ALU.add).then_inc(decoded[a], 1)
                for a in range(2):
                    dve.wait_ge(decoded[a], 1)
                    dve.wait_ge(shifted[a], 32)
                    v.tensor_tensor(same[a][:, :], node[a][:, 1:SORT_F + 1], node[a][:, 0:SORT_F],
                                    ALU.is_equal).then_inc(decoded[a], 1)
                    link(a, v.tensor_tensor(more[a][:, :], node[a][:, 2:SORT_F + 2], node[a][:, 1:SORT_F + 1],
                                            ALU.is_equal))
                for a in range(2):
                    after(a)
                    v.scalar_tensor_tensor(dest[a][:, :], more[a][:, :], OOB, node[a][:, 1:SORT_F + 1],
                                           ALU.mult, ALU.add).then_inc(decoded[a], 1)

            FINALS = [(0, load_f[0], by_src[:, :, EDGE], 0), (0, node[0], by_src[:, :, SRC], 1),
                      (0, dest[0], by_src[:, :, OUT], 0), (1, load_f[1], by_dst[:, :, D_SRC], 0),
                      (1, dest[1], by_dst[:, :, D_OUT], 0)]

            @block.tensor
            def _(pe):
                pe.wait_ge(loaded, 48)
                pe.wait_ge(signed, 12)
                at = [0, 0]
                for k in range(1, 10):
                    at = [(b + k) % 2 for b in at]
                at = [(b + 2) % 2 for b in at]
                for k in range(FIRST_CROSS, 17):
                    for half in range(2):
                        n = 2 * (k - FIRST_CROSS) + half
                        for a in range(2):
                            pe.wait_ge(handed[a], 2 * n + 2)
                            if n:
                                pe.wait_ge(moved[a], n)
                            s = key[a][at[a]][:, :]
                            for j in range(4):
                                piece = s[:, j * P:(j + 1) * P] if half == 0 else \
                                    s.rearrange("p (q j) -> p j q", j=4)[:, j, :]
                                ins = nc.tensor.transpose(turned[a][:, j, :], piece, eye[:, :])
                            ins.then_inc(back[a], 1)
                            at[a] = 1 - at[a]
                            at[a] = (at[a] + (k - 7 if half == 0 else 7 + 1)) % 2
                for n, (a, source, _, off) in enumerate(FINALS):
                    pe.wait_ge(decoded[a], 3)
                    for j in range(4):
                        ins = nc.tensor.transpose(final[n][:, j, :], source[:, off + j * P:off + (j + 1) * P], eye[:, :])
                    ins.then_inc(final_t, 1)

            @block.scalar
            def _(act):
                at = [1, 1]
                for k in range(1, 10):
                    at = [(b + k) % 2 for b in at]
                at = [(b + 2) % 2 for b in at]
                for k in range(FIRST_CROSS, 17):
                    for half in range(2):
                        n = 2 * (k - FIRST_CROSS) + half
                        for a in range(2):
                            act.wait_ge(back[a], n + 1)
                            o = key[a][at[a]][:, :]
                            o = o.rearrange("p (q j) -> p j q", j=4) if half == 0 else \
                                o.rearrange("p (j q) -> p j q", j=4)
                            nc.scalar.copy(o, turned[a][:, :, :]).then_inc(moved[a], 1)
                            at[a] = 1 - at[a]
                            at[a] = (at[a] + (k - 7 if half == 0 else 7 + 1)) % 2
                for n, (_, _, target, _) in enumerate(FINALS):
                    act.wait_ge(final_t, n + 1)
                    nc.scalar.copy(target.rearrange("p (q j) -> p j q", j=4), final[n][:, :, :]).then_inc(final_c, 1)

        b3_b = sb("b3_b", [P, 2, D])
        gmax = sb("gmax", [P, 1])
        degree = sb("degree", [P, NCHUNKS, ROWS])
        place_of = sb("place_of", [P, NCHUNKS, ROWS])
        sum_at = sb("sum_at", [P, TILES], i32)
        minus_half = sb("minus_half", [P, ROWS])

        def fresh(m, slots):
            return isinstance(m, int) and m < slots

        def pipeline(eng, count, parts, slots=2, peel_last=False):
            most = max(lag for _, lag in parts)
            low = (most + 2 * slots - 1) // slots * slots
            high = (count - 1 if peel_last else count) // slots * slots

            def straight(n):
                for f, lag in parts:
                    m = n - lag
                    if 0 <= m < count:
                        f(m, m % slots, m // slots, m < slots)

            for n in range(low):
                straight(n)
            with eng.Fori(low // slots, high // slots) as i:
                for r in range(slots):
                    for f, lag in parts:
                        s = (r - lag) % slots
                        f(i * slots + (r - lag), s, i + (r - lag - s) // slots, False)
            for n in range(high, count + most):
                straight(n)

        def times(s, slots):
            return (CHUNKS - s + slots - 1) // slots

        def rows_of(table, m, width=None):
            return table.rearrange("(c p k) f -> p c (k f)", p=P, k=ROWS)[:, bass.ds(m, 1), :]

        node_in = [sem(f"node_in{s}") for s in range(NS)]
        node_taken = sem("node_taken")
        node_x = sem("node_x")
        node_sum = sem("node_sum")
        node_cent = sem("node_cent")
        node_sq = sem("node_sq")
        node_var = sem("node_var")
        node_eps = sem("node_eps")
        node_rstd = sem("node_rstd")
        node_norm = sem("node_norm")
        node_h = sem("node_h")
        node_x_out = [sem(f"node_x_out{s}") for s in range(NS)]
        node_h_out = [sem(f"node_h_out{s}") for s in range(NS)]
        node_base = [0]
        in_base = [0] * NS
        x_out_base = [0] * NS
        h_out_base = [0] * NS

        def uses(s):
            return (NCHUNKS - s + NS - 1) // NS

        def node_pass(kind, x_in, x_new, h_new):
            base, ib, xb, hb = node_base[0], list(in_base), list(x_out_base), list(h_out_base)
            xbase = base - NCHUNKS
            with ExitStack() as c:
                c.enter_context(nc.cleanup_on_exit())
                xi = [sb_in(c, f"xi_{kind}{s}", [P, ROWS, D]) for s in range(NS)]
                width = {"first": 0, "l0": D, "l1": D + 2, "l2": D + 2}[kind]
                mi = [sb_in(c, f"mi_{kind}{s}", [P, ROWS, max(width, 1)]) for s in range(NS)]
                xn = xi if kind == "first" else [sb_in(c, f"xn_{kind}{s}", [P, ROWS, D]) for s in range(NS)]
                cent = [sb_in(c, f"cent_{kind}{s}", [P, ROWS, D]) for s in range(NS)]
                sq = [sb_in(c, f"sq_{kind}{s}", [P, ROWS, D]) for s in range(NS)]
                norm = [sb_in(c, f"norm_{kind}{s}", [P, ROWS, D]) for s in range(NS)]
                hn = [sb_in(c, f"hn_{kind}{s}", [P, ROWS, D]) for s in range(NS)]
                tmp = [sb_in(c, f"tmp_{kind}{s}", [P, ROWS, D]) for s in range(NS)]
                total = [sb_in(c, f"total_{kind}{s}", [P, ROWS]) for s in range(NS)]
                var = [sb_in(c, f"var_{kind}{s}", [P, ROWS]) for s in range(NS)]
                vare = [sb_in(c, f"vare_{kind}{s}", [P, ROWS]) for s in range(NS)]
                rstd = [sb_in(c, f"rstd_{kind}{s}", [P, ROWS]) for s in range(NS)]
                small = [sb_in(c, f"small_{kind}{s}", [P, 6, ROWS]) for s in range(NS)]
                fs = {n: sem_in(c, f"{kind}_{n}") for n in {
                    "first": (), "l0": (), "l1": ("clamped", "recip", "scaled"),
                    "l2": ("inv", "gap", "gap2", "expd", "den", "recip", "scaled", "y", "yt", "ytc", "z", "zs", "lrelu", "g",
                           *(f"h2_in{s}" for s in range(NS)), *(f"g_out{s}" for s in range(NS)))}[kind]}
                loads = 1 if kind == "first" else 2
                if kind == "l2":
                    hi = [sb_in(c, f"hi_{s}", [P, ROWS, D]) for s in range(NS)]
                    y = [sb_in(c, f"y_{s}", [P, ROWS, D]) for s in range(NS)]
                    yt = [sb_in(c, f"yt_{s}", [P, ROWS * D]) for s in range(NS)]
                    lr = [sb_in(c, f"lr_{s}", [P, ROWS, D]) for s in range(NS)]
                    gn = [sb_in(c, f"gn_{s}", [P, ROWS, D + 1]) for s in range(NS)]
                    w2_sb = sb_in(c, "w2_sb", [P, P])
                    ps_yt = ps_in(c, "yt", [P, ROWS * D])
                    ps_z = [ps_in(c, f"z{s}", [P, ROWS * D]) for s in range(NS)]
                consts = sem_in(c, f"{kind}_consts")
                block = c.enter_context(nc.Block())
                v = nc.vector

                @block.sync
                def _(sp):
                    def load(m, s, h, first):
                        if not first:
                            await_in_loop(sp, node_cent, base + m + 1 - NS)
                            if loads == 2:
                                await_in_loop(sp, node_taken, xbase + m + 1 - NS)
                        sp.dma_start(xi[s][:, :, :].rearrange("p k (o f) -> p o (k f)", o=1), rows_of(x_in, m)).then_inc(node_in[s], 16)
                        if loads == 2:
                            table = {"l0": msg0, "l1": msg1, "l2": msg2}[kind]
                            sp.dma_start(mi[s][:, :, :].rearrange("p k (o f) -> p o (k f)", o=1), rows_of(table, m)).then_inc(node_in[s], 16)
                        if kind == "l2":
                            sp.dma_start(hi[s][:, :, :].rearrange("p k (o f) -> p o (k f)", o=1), rows_of(h2, m)).then_inc(fs[f"h2_in{s}"], 16)

                    def store_x(m, s, h, first):
                        await_in_loop(sp, node_x, xbase + m + 1)
                        sp.dma_start(rows_of(x_new, m), xn[s][:, :, :].rearrange("p k (o f) -> p o (k f)", o=1)).then_inc(node_x_out[s], 16)

                    def store_h(m, s, h, first):
                        await_in_loop(sp, node_h, base + m + 1)
                        sp.dma_start(rows_of(h_new, m), hn[s][:, :, :].rearrange("p k (o f) -> p o (k f)", o=1)).then_inc(node_h_out[s], 16)

                    def store_g(m, s, h, first):
                        await_in_loop(sp, fs["g"], m + 1)
                        sp.dma_start(rows_of(g0, m), gn[s][:, :, :].rearrange("p k (o f) -> p o (k f)", o=1)).then_inc(fs[f"g_out{s}"], 16)

                    if kind == "l2":
                        sp.dma_start(w2_sb[:, :], w2).then_inc(consts, 16)
                    pipeline(sp, NCHUNKS, {"first": [(load, 0), (store_h, 6)],
                                           "l0": [(load, 0), (store_x, 3), (store_h, 6)],
                                           "l1": [(load, 0), (store_x, 3), (store_h, 6)],
                                           "l2": [(load, 0), (store_x, 5), (store_h, 7), (store_g, 8)]}[kind], NS)
                    for s in range(NS):
                        if kind != "first":
                            await_in_loop(sp, node_x_out[s], xb[s] + 16 * uses(s))
                        await_in_loop(sp, node_h_out[s], hb[s] + 16 * uses(s))
                        if kind == "l2":
                            await_in_loop(sp, fs[f"g_out{s}"], 16 * uses(s))

                @block.gpsimd
                def _(pool):
                    if kind == "first":
                        pool.memset(minus_half[:, :], -0.5).then_inc(consts, 1)
                        pool.wait_ge(consts, 1)

                    def inv(m, s, h, first):
                        pool.tensor_tensor(inv_deg[:, bass.ds(m, 1), :], degree[:, bass.ds(m, 1), :],
                                           minus_half[:, :].rearrange("p (o k) -> p o k", o=1), ALU.pow).then_inc(fs["inv"], 1)

                    def norm_part(m, s, h, first):
                        await_in_loop(pool, node_eps, base + m + 1)
                        if not first:
                            await_in_loop(pool, node_norm, base + m + 1 - NS)
                        pool.tensor_tensor(rstd[s][:, :], vare[s][:, :], minus_half[:, :], ALU.pow).then_inc(node_rstd, 1)
                        await_in_loop(pool, node_rstd, base + m + 1)
                        if not first:
                            await_in_loop(pool, node_h, base + m + 1 - NS)
                        pool.tensor_tensor(norm[s][:, :, :], cent[s][:, :, :],
                                           rstd[s][:, :].rearrange("p (k o) -> p k o", o=1).to_broadcast([P, ROWS, D]),
                                           ALU.mult).then_inc(node_norm, 1)

                    def scale_g(m, s, h, first):
                        await_in_loop(pool, node_h, base + m + 1)
                        await_in_loop(pool, fs["inv"], m + 1)
                        if not first:
                            await_in_loop(pool, fs[f"g_out{s}"], h * 16)
                        pool.tensor_tensor(gn[s][:, :, 0:D], hn[s][:, :, :],
                                           inv_deg[:, bass.ds(m, 1), :].rearrange("p o k -> p k o").to_broadcast([P, ROWS, D]),
                                           ALU.mult)
                        pool.tensor_copy(gn[s][:, :, D], place_of[:, bass.ds(m, 1), :].rearrange("p o k -> p (o k)")).then_inc(fs["g"], 1)

                    if kind == "l2":
                        pipeline(pool, NCHUNKS, [(inv, 0), (norm_part, 3), (scale_g, 4)], NS)
                    else:
                        pipeline(pool, NCHUNKS, [(norm_part, 2)], NS)

                @block.vector
                def _(dve):
                    def gap(m, s, h, first):
                        dve.wait_ge(node_in[s], h * (16 * loads) + (ib[s] + 16 * loads))
                        v.tensor_scalar(small[s][:, 0, :], mi[s][:, :, D + 1], -1.0, gmax[:, 0:1], ALU.mult,
                                        ALU.add).then_inc(fs["gap"], 1)
                        dve.wait_ge(fs["gap"], m + 1)
                        v.tensor_scalar(small[s][:, 1, :], small[s][:, 0, :], 0.0, 80.0, ALU.max, ALU.min).then_inc(fs["gap2"], 1)

                    def front(m, s, h, first):
                        wb_in = h * (16 * loads) + (ib[s] + 16 * loads)
                        dve.wait_ge(node_in[s], wb_in)
                        if kind == "first":
                            return
                        if not first:
                            dve.wait_ge(node_x_out[s], h * 16 + xb[s])
                        if kind == "l0":
                            v.tensor_tensor(xn[s][:, :, :], xi[s][:, :, :], mi[s][:, :, :], ALU.add).then_inc(node_x, 1)
                            dve.wait_ge(node_x, xbase + m + 1)
                            dve.sem_inc(node_taken, 1)
                        if kind == "l1":
                            v.tensor_copy(place_of[:, bass.ds(m, 1), :].rearrange("p o k -> p (o k)"), mi[s][:, :, D + 1])
                            v.tensor_scalar(degree[:, bass.ds(m, 1), :].rearrange("p o k -> p (o k)"), mi[s][:, :, D], 1.0, None, ALU.max)
                            v.tensor_scalar(small[s][:, 0, :], mi[s][:, :, D], 1.0, None, ALU.max).then_inc(fs["clamped"], 1)
                            dve.wait_ge(fs["clamped"], m + 1)
                            v.reciprocal(small[s][:, 1, :], small[s][:, 0, :]).then_inc(fs["recip"], 1)
                            dve.wait_ge(fs["recip"], m + 1)
                            v.tensor_tensor(tmp[s][:, :, :], mi[s][:, :, 0:D],
                                            small[s][:, 1, :].rearrange("p (k o) -> p k o", o=1).to_broadcast([P, ROWS, D]),
                                            ALU.mult).then_inc(fs["scaled"], 1)
                            dve.wait_ge(fs["scaled"], m + 1)
                            dve.sem_inc(node_taken, 1)
                            v.tensor_tensor(xn[s][:, :, :], tmp[s][:, :, :], xi[s][:, :, :], ALU.add).then_inc(node_x, 1)
                            dve.wait_ge(node_x, xbase + m + 1)
                        if kind == "l2":
                            dve.wait_ge(fs["expd"], m + 1)
                            v.scalar_tensor_tensor(small[s][:, 3, :], small[s][:, 2, :], 1e-10, mi[s][:, :, D], ALU.mult,
                                                   ALU.add).then_inc(fs["den"], 1)
                            dve.wait_ge(fs["den"], m + 1)
                            v.reciprocal(small[s][:, 4, :], small[s][:, 3, :]).then_inc(fs["recip"], 1)
                            dve.wait_ge(fs["recip"], m + 1)
                            v.tensor_tensor(tmp[s][:, :, :], mi[s][:, :, 0:D],
                                            small[s][:, 4, :].rearrange("p (k o) -> p k o", o=1).to_broadcast([P, ROWS, D]),
                                            ALU.mult).then_inc(fs["scaled"], 1)
                            dve.wait_ge(fs["scaled"], m + 1)
                            dve.sem_inc(node_taken, 1)
                            dve.wait_ge(fs[f"h2_in{s}"], h * 16 + 16)
                            if not first:
                                dve.wait_ge(fs["yt"], m + 1 - NS)
                            v.tensor_tensor(y[s][:, :, :], tmp[s][:, :, :], hi[s][:, :, :], ALU.add).then_inc(fs["y"], 1)

                    def finish_x(m, s, h, first):
                        if kind == "l2":
                            dve.wait_ge(fs["zs"], m + 1)
                            v.tensor_tensor(lr[s][:, :, :].rearrange("p k f -> p (k f)"), ps_z[s][:, 0:ROWS * D],
                                            tmp[s][:, :, :].rearrange("p k f -> p (k f)"), ALU.max).then_inc(fs["lrelu"], 1)
                            dve.wait_ge(fs["lrelu"], m + 1)
                            v.tensor_tensor(xn[s][:, :, :], lr[s][:, :, :], xi[s][:, :, :], ALU.add).then_inc(node_x, 1)
                            dve.wait_ge(node_x, xbase + m + 1)

                    def center(m, s, h, first):
                        v.tensor_reduce(total[s][:, :], xn[s][:, :, :], AX, ALU.add).then_inc(node_sum, 1)
                        dve.wait_ge(node_sum, base + m + 1)
                        if not first:
                            dve.wait_ge(node_norm, base + m + 1 - NS)
                        v.scalar_tensor_tensor(cent[s][:, :, :], total[s][:, :].rearrange("p (k o) -> p k o", o=1).to_broadcast([P, ROWS, D]),
                                               -1.0 / D, xn[s][:, :, :], ALU.mult, ALU.add).then_inc(node_cent, 1)

                    def spread(m, s, h, first):
                        dve.wait_ge(node_sq, base + m + 1)
                        v.tensor_reduce(var[s][:, :], sq[s][:, :, :], AX, ALU.add).then_inc(node_var, 1)
                        dve.wait_ge(node_var, base + m + 1)
                        if not first:
                            dve.wait_ge(node_rstd, base + m + 1 - NS)
                        v.tensor_scalar(vare[s][:, :], var[s][:, :], 1.0 / D, LN_EPS, ALU.mult, ALU.add).then_inc(node_eps, 1)

                    if kind == "l2":
                        pipeline(dve, NCHUNKS, [(gap, 0), (finish_x, 2), (center, 2), (spread, 3), (front, 0)], NS)
                    else:
                        pipeline(dve, NCHUNKS, [(spread, 2), (front, 0), (center, 0)], NS)

                @block.scalar
                def _(act):
                    def expd(m, s, h, first):
                        act.wait_ge(fs["gap2"], m + 1)
                        if not first:
                            act.wait_ge(fs["den"], m + 1 - NS)
                        nc.scalar.activation(small[s][:, 2, :], small[s][:, 1, :], ACT.Exp).then_inc(fs["expd"], 1)

                    def turn_y(m, s, h, first):
                        act.wait_ge(fs["yt"], m + 1)
                        if not first:
                            act.wait_ge(fs["z"], m + 1 - NS)
                        nc.scalar.copy(yt[s][:, :], ps_yt[:, 0:ROWS * D]).then_inc(fs["ytc"], 1)

                    def slope(m, s, h, first):
                        act.wait_ge(fs["z"], m + 1)
                        nc.scalar.activation(tmp[s][:, :, :].rearrange("p k f -> p (k f)"), ps_z[s][:, 0:ROWS * D], ACT.Copy,
                                             scale=0.2).then_inc(fs["zs"], 1)

                    def square(m, s, h, first):
                        act.wait_ge(node_cent, base + m + 1)
                        if not first:
                            act.wait_ge(node_var, base + m + 1 - NS)
                        nc.scalar.activation(sq[s][:, :, :], cent[s][:, :, :], ACT.Square).then_inc(node_sq, 1)

                    def relu(m, s, h, first):
                        act.wait_ge(node_norm, base + m + 1)
                        if not first:
                            act.wait_ge(node_h_out[s], h * 16 + hb[s])
                            if kind == "l2":
                                act.wait_ge(fs["g"], m + 1 - NS)
                        nc.scalar.activation(hn[s][:, :, :], norm[s][:, :, :], ACT.Relu).then_inc(node_h, 1)

                    if kind == "l2":
                        pipeline(act, NCHUNKS, [(expd, 0), (slope, 1), (square, 2), (relu, 4), (turn_y, 0)], NS)
                    else:
                        pipeline(act, NCHUNKS, [(relu, 3), (square, 0)], NS)

                if kind == "l2":
                    @block.tensor
                    def _(pe):
                        pe.wait_ge(consts, 16)

                        def turn(m, s, h, first):
                            await_in_loop(pe, fs["y"], m + 1)
                            if not (first and m == 0):
                                await_in_loop(pe, fs["ytc"], m)
                            for j in range(ROWS // 2):
                                ins = nc.tensor.transpose(ps_yt[:, j * P:(j + 1) * P],
                                                          y[s][:, 2 * j:2 * j + 2, :].rearrange("p k f -> p (k f)"), eye[:, :])
                            ins.then_inc(fs["yt"], 1)

                        def project(m, s, h, first):
                            await_in_loop(pe, fs["ytc"], m + 1)
                            if not first:
                                await_in_loop(pe, fs["lrelu"], m + 1 - NS)
                            for j in range(ROWS // 2):
                                ins = nc.tensor.matmul(ps_z[s][:, j * P:(j + 1) * P], yt[s][:, j * P:(j + 1) * P], w2_sb[:, :],
                                                       start=True, stop=True)
                            ins.then_inc(fs["z"], 1)

                        pipeline(pe, NCHUNKS, [(turn, 0), (project, 0)], NS)
            node_base[0] += NCHUNKS
            for s in range(NS):
                in_base[s] += 16 * loads * uses(s)
                if kind != "first":
                    x_out_base[s] += 16 * uses(s)
                h_out_base[s] += 16 * uses(s)

        node_pass("first", x, None, h0)
        with ExitStack() as c:
            c.enter_context(nc.cleanup_on_exit())
            cat = [sb_in(c, f"cat{s}", [P, K, 2 * D + 2]) for s in range(GS)]
            hd = [sb_in(c, f"hd{s}", [P, K, D]) for s in range(GS)]
            at = [sb_in(c, f"at{s}", [P, K, 4], i32) for s in range(GS)]
            xsrc = sb_in(c, "xsrc", [P, CHUNK])
            xdst = [sb_in(c, f"xdst{s}", [P, CHUNK]) for s in range(GS)]
            clamped = [sb_in(c, f"clamped{q}", [P, 2, CHUNK]) for q in range(2)]
            expd = [sb_in(c, f"expd{q}", [P, 2, CHUNK]) for q in range(2)]
            logd = [sb_in(c, f"logd{q}", [P, 2, CHUNK]) for q in range(2)]
            soft = [[sb_in(c, f"soft{q}{s}", [P, 2, CHUNK]) for s in range(GS)] for q in range(2)]
            lrow = [sb_in(c, f"lrow{s}", [HEADS, CHUNK]) for s in range(GS)]
            w0_sb = sb_in(c, "w0_sb", [P, 2 * P])
            att_sb = sb_in(c, "att_sb", [P, 4, HEADS])
            ps_in_side = [ps_in(c, f"in_side{q}", [P, CHUNK]) for q in range(2)]
            ps_side = [ps_in(c, f"side{q}", [P, 2, CHUNK]) for q in range(2)]
            ps_logit = ps_in(c, "logit", [HEADS, CHUNK])
            a_const = sem_in(c, "a_const")
            a_index = sem_in(c, "a_index")
            rec_in = [sem_in(c, f"rec_in{s}") for s in range(GS)]
            hd_in = [sem_in(c, f"hd_in{s}") for s in range(GS)]
            a_turned = [sem_in(c, f"a_turned{q}") for q in range(2)]
            a_edge_rows = sem_in(c, "a_edge_rows")
            a_side = [sem_in(c, f"a_side{q}") for q in range(2)]
            a_proj = [sem_in(c, f"a_proj{q}") for q in range(2)]
            a_clamp = [sem_in(c, f"a_clamp{q}") for q in range(2)]
            a_exp = [sem_in(c, f"a_exp{q}") for q in range(2)]
            a_log = [sem_in(c, f"a_log{q}") for q in range(2)]
            a_soft = [sem_in(c, f"a_soft{q}") for q in range(2)]
            a_logit = sem_in(c, "a_logit")
            a_lrow = sem_in(c, "a_lrow")
            a_kept = sem_in(c, "a_kept")
            sp_out = [sem_in(c, f"sp_out{s}") for s in range(GS)]
            lg_out = [sem_in(c, f"lg_out{s}") for s in range(GS)]
            block = c.enter_context(nc.Block())
            v = nc.vector

            @block.sync
            def _(sp):
                sp.dma_start(w0_sb[:, :], w0).then_inc(a_const, 16)
                sp.dma_start(att_sb[:, :, :].rearrange("p q h -> p (q h)"), att).then_inc(a_const, 16)

                def store(m, s, h, first):
                    await_in_loop(sp, a_soft[1], m + 1)
                    sp.dma_start(sp_j.rearrange("c b p e -> c p b e")[bass.ds(m, 1), :, :, :].rearrange("o p b e -> (o p) b e"),
                                 soft[1][s][:, :, :]).then_inc(sp_out[s], 16)

                def store_row(m, s, h, first):
                    await_in_loop(sp, a_lrow, m + 1)
                    sp.dma_start(logits[:, bass.ds(m * CHUNK, CHUNK)], lrow[s][:, :]).then_inc(lg_out[s], 16)

                pipeline(sp, CHUNKS, [(store, 0), (store_row, 2)], GS)
                for s in range(GS):
                    await_in_loop(sp, sp_out[s], 16 * times(s, GS))
                    await_in_loop(sp, lg_out[s], 16 * times(s, GS))

            @block.gpsimd
            def _(pool):
                def number(m, s, h, first):
                    if not first:
                        await_in_loop(pool, rec_in[s], h * (32 * K))
                    pool.tensor_copy(at[s][:, :, 0:2], by_src[:, bass.ds(m * K, K), 0:2]).then_inc(a_index, 1)

                def ends(m, s, h, first):
                    await_in_loop(pool, a_index, m + 1)
                    if not first:
                        await_in_loop(pool, a_kept, m + 1 - GS)
                        await_in_loop(pool, a_turned[0], m + 1 - GS)
                    for k in range(K):
                        pool.indirect_dma_start(cat[s].bitcast(i32)[:, k, D:2 * D + 2], None, rec,
                                                bass.IndirectOffsetOnAxis(at[s][:, k, EDGE:EDGE + 1], 0)).then_inc(rec_in[s], 16)
                    for k in range(K):
                        pool.indirect_dma_start(cat[s][:, k, 0:D], None, h0,
                                                bass.IndirectOffsetOnAxis(at[s][:, k, SRC:SRC + 1], 0)).then_inc(rec_in[s], 16)

                def other_end(m, s, h, first):
                    await_in_loop(pool, rec_in[s], h * (32 * K) + 32 * K)
                    if not first:
                        await_in_loop(pool, a_turned[1], m + 1 - GS)
                    for k in range(K):
                        pool.indirect_dma_start(hd[s][:, k, :], None, h0,
                                                bass.IndirectOffsetOnAxis(cat[s].bitcast(i32)[:, k, 2 * D:2 * D + 1], 0)).then_inc(hd_in[s], 16)

                pipeline(pool, CHUNKS, [(number, 0), (ends, 1), (other_end, 3)], GS)

            @block.tensor
            def _(pe):
                pe.wait_ge(a_const, 32)

                def turn(q):
                    def part(m, s, h, first):
                        if q == 0:
                            await_in_loop(pe, rec_in[s], h * (32 * K) + 32 * K)
                        else:
                            await_in_loop(pe, hd_in[s], h * (16 * K) + 16 * K)
                        if not fresh(m, 1):
                            await_in_loop(pe, a_side[q], m)
                            if q == 0:
                                await_in_loop(pe, a_edge_rows, m)
                        for k in range(K):
                            if q == 0:
                                ins = nc.tensor.transpose(ps_in_side[0][:, k * P:(k + 1) * P], cat[s][:, k, 0:2 * D], eye[:, :])
                            else:
                                ins = nc.tensor.transpose(ps_in_side[1][0:D, k * P:(k + 1) * P], hd[s][:, k, :], eye[:, :])
                        ins.then_inc(a_turned[q], 1)
                    return part

                def project(q):
                    def part(m, s, h, first):
                        await_in_loop(pe, a_side[q], m + 1)
                        if q == 1:
                            await_in_loop(pe, a_edge_rows, m + 1)
                        if not fresh(m, 1):
                            await_in_loop(pe, a_soft[q], m)
                        for b in range(2):
                            ins = nc.tensor.matmul(ps_side[q][:, b, :], w0_sb[:, b * P:(b + 1) * P],
                                                   (xsrc if q == 0 else xdst[s])[:, :], start=True, stop=True)
                        ins.then_inc(a_proj[q], 1)
                    return part

                def logit(m, s, h, first):
                    await_in_loop(pe, a_soft[1], m + 1)
                    await_in_loop(pe, a_soft[0], m + 1)
                    if not fresh(m, 1):
                        await_in_loop(pe, a_lrow, m)
                    for n in range(4):
                        ins = nc.tensor.matmul(ps_logit[:, :], att_sb[:, n, :], soft[n // 2][s][:, n % 2, :],
                                               start=(n == 0), stop=(n == 3))
                    ins.then_inc(a_logit, 1)

                pipeline(pe, CHUNKS, [(project(0), 1), (turn(0), 0), (project(1), 3), (turn(1), 2), (logit, 4)], GS)

            @block.scalar
            def _(act):
                nc.scalar.preload_act_table_set("natural_log_exp_and_others")

                def sides(m, s, h, first):
                    act.wait_ge(a_turned[0], m + 1)
                    if not fresh(m, 1):
                        act.wait_ge(a_proj[0], m)
                    nc.scalar.copy(xsrc[:, :], ps_in_side[0][:, :]).then_inc(a_side[0], 1)
                    if not first:
                        act.wait_ge(a_proj[1], m + 1 - GS)
                    nc.scalar.copy(xdst[s][D:2 * D, :], ps_in_side[0][D:2 * D, :]).then_inc(a_edge_rows, 1)

                def exp_log(q):
                    def part(m, s, h, first):
                        act.wait_ge(a_clamp[q], m + 1)
                        if not fresh(m, 1):
                            act.wait_ge(a_log[q], m)
                        nc.scalar.activation(expd[q][:, :, :], clamped[q][:, :, :], ACT.Exp).then_inc(a_exp[q], 1)
                        act.wait_ge(a_exp[q], m + 1)
                        if not fresh(m, 1):
                            act.wait_ge(a_soft[q], m)
                        nc.scalar.activation(logd[q][:, :, :], expd[q][:, :, :], ACT.Ln, bias=1.0).then_inc(a_log[q], 1)
                    return part

                def keep(m, s, h, first):
                    act.wait_ge(rec_in[s], h * (32 * K) + 32 * K)
                    act.wait_ge(hd_in[s], h * (16 * K) + 16 * K)
                    ends_of = cat[s].bitcast(i32)
                    nc.scalar.copy(by_src[:, bass.ds(m * K, K), DST], ends_of[:, :, 2 * D])
                    nc.scalar.copy(type_of[:, bass.ds(m * K, K)], ends_of[:, :, 2 * D + 1]).then_inc(a_kept, 1)

                def logit_row(m, s, h, first):
                    act.wait_ge(a_logit, m + 1)
                    if not first:
                        act.wait_ge(lg_out[s], h * 16)
                    nc.scalar.copy(lrow[s][:, :], ps_logit[:, :]).then_inc(a_lrow, 1)

                pipeline(act, CHUNKS, [(logit_row, 5), (exp_log(0), 1), (sides, 0), (exp_log(1), 3), (keep, 2)], GS)

            @block.vector
            def _(dve):
                def side(m, s, h, first):
                    dve.wait_ge(a_turned[1], m + 1)
                    if not first:
                        dve.wait_ge(a_proj[1], m + 1 - GS)
                    v.tensor_copy(xdst[s][0:D, :], ps_in_side[1][0:D, :]).then_inc(a_side[1], 1)

                def clamp(q):
                    def part(m, s, h, first):
                        dve.wait_ge(a_proj[q], m + 1)
                        if not fresh(m, 1):
                            dve.wait_ge(a_exp[q], m)
                        v.tensor_scalar(clamped[q][:, :, :], ps_side[q][:, :, :], CLAMP, None, ALU.min).then_inc(a_clamp[q], 1)
                    return part

                def choose(q):
                    def part(m, s, h, first):
                        dve.wait_ge(a_log[q], m + 1)
                        if not first:
                            dve.wait_ge(a_logit, m + 1 - GS)
                            if q == 1:
                                dve.wait_ge(sp_out[s], h * 16)
                        v.tensor_tensor(soft[q][s][:, :, :], logd[q][:, :, :], ps_side[q][:, :, :], ALU.max).then_inc(a_soft[q], 1)
                    return part

                pipeline(dve, CHUNKS, [(clamp(0), 1), (choose(0), 1), (clamp(1), 3), (choose(1), 3), (side, 2)], GS)

        with ExitStack() as c:
            c.enter_context(nc.cleanup_on_exit())
            def t(name):
                return sb_in(c, "m_" + name, [P, SEG_LEN])

            z, cont, contn, s1, s2, s3, s4 = (t(n) for n in ("z", "cont", "contn", "s1", "s2", "s3", "s4"))
            parts = [sb_in(c, f"m_part{i}", [P, SEG_LEN], bf16) for i in range(3)]
            col = sb_in(c, "m_col", [P, 16])
            row = sb_in(c, "m_row", [1, 8, P])
            one = sb_in(c, "m_one", [1, 1])
            sh = sb_in(c, "m_sh", [P, P])
            gb = sb_in(c, "m_gb", [P, 2])
            trow = sb_in(c, "m_trow", [P, 4, P])
            ps_t = ps_in(c, "m_t", [P, 4, P])
            ps_s = ps_in(c, "m_s", [P, 512])
            ps_r = ps_in(c, "m_r", [1, 512])
            ps_b = ps_in(c, "m_b", [P, 512])
            m_in = sem_in(c, "m_in")
            m_types = sem_in(c, "m_types")
            m_trow = sem_in(c, "m_trow")
            m_out = sem_in(c, "m_out")
            m_masked = sem_in(c, "m_masked")
            m_first = sem_in(c, "m_first")
            m_dve = sem_in(c, "m_dve")
            m_to_act = sem_in(c, "m_to_act")
            m_from_act = sem_in(c, "m_from_act")
            m_to_pe = sem_in(c, "m_to_pe")
            m_from_pe = sem_in(c, "m_from_pe")
            m_done = sem_in(c, "m_done")
            block = c.enter_context(nc.Block())
            v = nc.vector
            PADS = N - (SEGS - 1) * SEG_LEN

            @block.sync
            def _(sp):
                sp.dma_start(z[:, :], logits.rearrange("h (c e) -> c h e", c=SEGS)).then_inc(m_in, 16)
                for i, tile in enumerate((cont, contn)):
                    sp.dma_start(tile[:, :], same_src[i:i + NPAD].rearrange("(c o e) -> c o e", c=SEGS, o=1).to_broadcast([SEGS, HEADS, SEG_LEN])).then_inc(m_in, 16)
                sp.dma_start(sh[:, :], samehead).then_inc(m_in, 16)
                sp.dma_start(gb[:, 0:1], gamma).then_inc(m_in, 16)
                sp.dma_start(gb[:, 1:2], beta).then_inc(m_in, 16)
                await_in_loop(sp, m_trow, 1)
                sp.dma_start(types_row[0:3 * P, :].rearrange("(j t) p -> t j p", j=3), trow[:, 0:3, :]).then_inc(m_out, 16)
                sp.dma_start(types_row[3 * P:TILES, :], trow[0:TILES - 3 * P, 3, :]).then_inc(m_out, 16)
                await_in_loop(sp, m_done, 1)
                for i in range(3):
                    sp.dma_start(weights[i].rearrange("h (c e) -> c h e", c=SEGS), parts[i][:, :]).then_inc(m_out, 16)
                await_in_loop(sp, m_out, 80)

            @block.gpsimd
            def _(pool):
                pool.memset(one[:, :], 1.0).then_inc(m_types, 1)
                pool.wait_ge(m_first, 1)
                pool.affine_select(out=s1[:, PADS:SEG_LEN], in_=s1[:, PADS:SEG_LEN], compare_op=ALU.is_ge, fill=0.0,
                                   base=P - HEADS - 1, pattern=[[0, SEG_LEN - PADS]], channel_multiplier=-1).then_inc(m_masked, 1)
                pool.wait_ge(m_first, 2)
                pool.affine_select(out=s2[:, PADS:SEG_LEN], in_=s2[:, PADS:SEG_LEN], compare_op=ALU.is_ge, fill=0.0,
                                   base=P - HEADS - 1, pattern=[[0, SEG_LEN - PADS]], channel_multiplier=-1).then_inc(m_masked, 1)

            @block.tensor
            def _(pe):
                for j in range(4):
                    w = min(P, TILES - j * P)
                    ins = nc.tensor.transpose(ps_t[0:w, j, :], type_of[:, j * P:j * P + w], eye[:, :])
                ins.then_inc(m_from_pe, 1)
                pe.wait_ge(m_in, 96)
                for n in range(2):
                    pe.wait_ge(m_to_pe, n + 1)
                    nc.tensor.matmul(ps_s[:, n:n + 1], sh[:, :], col[:, n:n + 1], start=True, stop=True).then_inc(m_from_pe, 1)
                pe.wait_ge(m_types, 1)
                for n in range(4):
                    pe.wait_ge(m_to_pe, 2 * n + 3)
                    nc.tensor.transpose(ps_r[:, 0:P], col[:, 8:9], eye[:, :])
                    nc.tensor.transpose(ps_r[:, P:2 * P], col[:, 9:10], eye[:, :]).then_inc(m_from_pe, 1)
                    pe.wait_ge(m_to_pe, 2 * n + 4)
                    nc.tensor.matmul(ps_b[:, n:n + 1], row[:, 3, :], one[:, :], start=True, stop=True).then_inc(m_from_pe, 1)

            @block.scalar
            def _(act):
                n = [0]

                def do(o, i, f, **kw):
                    n[0] += 1
                    act.wait_ge(m_to_act, n[0])
                    nc.scalar.activation(o, i, f, **kw).then_inc(m_from_act, 1)

                act.wait_ge(m_from_pe, 1)
                nc.scalar.copy(trow[:, 0:3, :], ps_t[:, 0:3, :])
                nc.scalar.copy(trow[0:TILES - 3 * P, 3, :], ps_t[0:TILES - 3 * P, 3, :]).then_inc(m_trow, 1)
                do(s2[:, :], s1[:, :], ACT.Exp)
                do(s3[:, :], s2[:, :], ACT.Ln, bias=1.0)
                do(s3[:, :], s2[:, :], ACT.Square)
                do(col[:, 4:5], col[:, 3:4], ACT.Sqrt)
                do(s2[:, :], s1[:, :], ACT.Exp)
                do(s3[:, :], s2[:, :], ACT.Ln, bias=1.0)
                do(s3[:, :], s2[:, :], ACT.Exp)

            @block.vector
            def _(dve):
                cnt = {"v": 0, "a": 0, "p": 1, "pe": 0}

                def op(ins):
                    cnt["v"] += 1
                    ins.then_inc(m_dve, 1)
                    dve.wait_ge(m_dve, cnt["v"])

                def to_act(n=1):
                    for _ in range(n):
                        dve.sem_inc(m_to_act, 1)
                        cnt["a"] += 1
                        dve.wait_ge(m_from_act, cnt["a"])

                def to_pe():
                    dve.sem_inc(m_to_pe, 1)
                    cnt["p"] += 1
                    dve.wait_ge(m_from_pe, cnt["p"])

                dve.wait_ge(m_in, 96)
                dve.wait_ge(m_types, 1)

                def softplus():
                    op(v.tensor_scalar(s1[:, :], z[:, :], CLAMP, None, ALU.min))
                    to_act(2)
                    op(v.tensor_tensor(s1[:, :], s3[:, :], z[:, :], ALU.max))

                softplus()
                dve.sem_inc(m_first, 1)
                dve.wait_ge(m_masked, 1)
                op(v.tensor_reduce(col[:, 0:1], s1[:, :], AX, ALU.add))
                to_pe()
                op(v.tensor_scalar(col[:, 2:3], ps_s[:, 0:1], -1.0 / N, None, ALU.mult))
                op(v.tensor_scalar(s2[:, :], s1[:, :], col[:, 2:3], None, ALU.add))
                dve.sem_inc(m_first, 1)
                dve.wait_ge(m_masked, 2)
                to_act()
                op(v.tensor_reduce(col[:, 1:2], s3[:, :], AX, ALU.add))
                to_pe()
                op(v.tensor_scalar(col[:, 3:4], ps_s[:, 1:2], 1.0 / N, LN_EPS, ALU.mult, ALU.add))
                to_act()
                op(v.reciprocal(col[:, 5:6], col[:, 4:5]))
                op(v.tensor_tensor(col[:, 6:7], col[:, 5:6], gb[:, 0:1], ALU.mult))
                op(v.tensor_scalar(z[:, :], s2[:, :], col[:, 6:7], gb[:, 1:2], ALU.mult, ALU.add))
                softplus()

                def scan(o, keep, add, op1, n, reverse):
                    view = (lambda a: a[:, ::-1]) if reverse else (lambda a: a[:, :])
                    end = slice(0, 1) if reverse else slice(SEG_LEN - 1, SEG_LEN)
                    op(v.tensor_tensor_scan(view(o), view(keep), view(add), 0.0, ALU.mult, op1))
                    op(v.tensor_copy(col[:, 8:9], o[:, end]))
                    op(v.tensor_reduce(col[:, 9:10], keep[:, :], AX, ALU.min))
                    to_pe()
                    op(v.tensor_copy(row[:, 0:2, :].rearrange("p a b -> p (a b)"), ps_r[:, 0:2 * P]))
                    op(v.memset(row[:, 2:4, :], 0.0))
                    for h in range(HEADS):
                        def stretches(i, lo, hi, r=reverse):
                            a = row[:, i, :].rearrange("p (c h) -> p h c", h=HEADS)[:, h, lo:hi]
                            return a[:, ::-1] if r else a
                        op(v.tensor_tensor_scan(stretches(2, 0, SEGS), stretches(1, 0, SEGS), stretches(0, 0, SEGS), 0.0, ALU.mult, op1))
                        to, of = ((0, SEGS - 1), (1, SEGS)) if reverse else ((1, SEGS), (0, SEGS - 1))
                        op(v.tensor_copy(stretches(3, *to, r=False), stretches(2, *of, r=False)))
                    to_pe()
                    op(v.tensor_copy(col[:, 10:11], ps_b[:, n:n + 1]))
                    op(v.tensor_tensor_scan(view(o), view(keep), view(add), col[:, 10:11], ALU.mult, op1))

                scan(s2, cont, s1, ALU.max, 0, False)
                op(v.tensor_scalar(s3[:, :], contn[:, :], -1.0, 1.0, ALU.mult, ALU.add))
                op(v.tensor_tensor(s3[:, :], s3[:, :], s2[:, :], ALU.mult))
                scan(s4, contn, s3, ALU.add, 1, True)
                op(v.tensor_tensor(s2[:, :], s1[:, :], s4[:, :], ALU.subtract))
                to_act()
                scan(s2, cont, s3, ALU.add, 2, False)
                op(v.tensor_scalar(s1[:, :], contn[:, :], -1.0, 1.0, ALU.mult, ALU.add))
                op(v.tensor_tensor(s1[:, :], s1[:, :], s2[:, :], ALU.mult))
                scan(s4, contn, s1, ALU.add, 3, True)
                op(v.tensor_scalar(s4[:, :], s4[:, :], 1e-16, None, ALU.add))
                op(v.reciprocal(s2[:, :], s4[:, :]))
                op(v.scalar_tensor_tensor(z[:, :], s3[:, :], 1.0 / HEADS, s2[:, :], ALU.mult, ALU.mult))
                op(v.tensor_copy(parts[0][:, :], z[:, :]))
                op(v.tensor_tensor(s1[:, :], z[:, :], parts[0][:, :], ALU.subtract))
                op(v.tensor_copy(parts[1][:, :], s1[:, :]))
                op(v.tensor_tensor(s2[:, :], s1[:, :], parts[1][:, :], ALU.subtract))
                op(v.tensor_copy(parts[2][:, :], s2[:, :]))
                dve.sem_inc(m_done, 1)

        with ExitStack() as c:
            c.enter_context(nc.cleanup_on_exit())
            LS = 4
            sj = [sb_in(c, f"sj{s}", [P, 2, CHUNK]) for s in range(LS)]
            wr = [sb_in(c, f"wr{s}", [3 * HEADS, CHUNK], bf16) for s in range(LS)]
            ct = [sb_in(c, f"ct{s}", [D, CHUNK]) for s in range(LS)]
            biased = [sb_in(c, f"biased{s}", [D, CHUNK]) for s in range(2)]
            bias_col = sb_in(c, "bias_col", [D, 1])
            hs_f = sb_in(c, "hs_f", [3 * HEADS, 2, P])
            wm = [sb_in(c, f"wm{s}", [P, 2, CHUNK]) for s in range(2)]
            run = [sb_in(c, f"c_run{s}", [D, CHUNK]) for s in range(2)]
            rows_sb = [sb_in(c, f"c_rows{s}", [P, K, D]) for s in range(LS)]
            at_out = [sb_in(c, f"c_at_out{s}", [P, K], i32) for s in range(LS)]
            hs_sb = sb_in(c, "hs_sb", [3 * HEADS, 2, P], bf16)
            hsum_sb = sb_in(c, "hsum_sb", [P, D])
            ps_w = [ps_in(c, f"w{s}", [P, 2, CHUNK]) for s in range(2)]
            ps_m = [ps_in(c, f"m{s}", [D, CHUNK]) for s in range(2)]
            ps_back = [ps_in(c, f"c_back{s}", [P, CHUNK]) for s in range(2)]
            c_const = sem_in(c, "c_const")
            c_in = [sem_in(c, f"c_in{s}") for s in range(LS)]
            c_biased = sem_in(c, "c_biased")
            c_index = sem_in(c, "c_index")
            c_spread = sem_in(c, "c_spread")
            c_weighed = sem_in(c, "c_weighed")
            c_msg = sem_in(c, "c_msg")
            c_run = sem_in(c, "c_run")
            c_back = sem_in(c, "c_back")
            c_rows = sem_in(c, "c_rows")
            c_out = [sem_in(c, f"c_out{s}") for s in range(LS)]
            block = c.enter_context(nc.Block())
            v = nc.vector

            @block.sync
            def _(sp):
                for i in range(3):
                    sp.dma_start(hs_f[i * HEADS:(i + 1) * HEADS, :, :].rearrange("h b p -> h (b p)"), headsel).then_inc(c_const, 16)
                sp.dma_start(hsum_sb[:, :], headsum).then_inc(c_const, 16)
                sp.dma_start(bias_col[:, :], bias0.rearrange("o f -> f o")).then_inc(c_const, 16)

                def load(m, s, h, first):
                    if not first:
                        await_in_loop(sp, c_run, m + 1 - LS)
                    sp.dma_start(sj[s][:, :, :], sp_j.rearrange("c b p e -> c p b e")[bass.ds(m, 1), :, :, :].rearrange("o p b e -> (o p) b e")).then_inc(c_in[s], 16)
                    sp.dma_start(wr[s][:, :], weights.rearrange("i h e -> (i h) e")[:, bass.ds(m * CHUNK, CHUNK)]).then_inc(c_in[s], 16)
                    sp.dma_start(ct[s][:, :], same_src[bass.ds(m * CHUNK, CHUNK)].rearrange("(o e) -> o e", o=1).to_broadcast([D, CHUNK])).then_inc(c_in[s], 16)

                pipeline(sp, CHUNKS, [(load, 0)], LS)

            @block.tensor
            def _(pe):
                pe.wait_ge(c_const, 81)

                def spread(m, s, h, first):
                    await_in_loop(pe, c_in[s], h * 48 + 48)
                    if not fresh(m, 2):
                        await_in_loop(pe, c_weighed, m - 1)
                    for b in range(2):
                        ins = nc.tensor.matmul(ps_w[s % 2][:, b, :], hs_sb[:, b, :], wr[s][:, :], start=True, stop=True)
                    ins.then_inc(c_spread, 1)

                def join(m, s, h, first):
                    await_in_loop(pe, c_weighed, m + 1)
                    if not fresh(m, 2):
                        await_in_loop(pe, c_run, m - 1)
                    for b in range(2):
                        ins = nc.tensor.matmul(ps_m[s % 2][:, :], hsum_sb[:, :], wm[s % 2][:, b, :], start=(b == 0), stop=(b == 1))
                    ins.then_inc(c_msg, 1)

                def turn_back(m, s, h, first):
                    await_in_loop(pe, c_biased, m + 1)
                    if not fresh(m, 2):
                        await_in_loop(pe, c_rows, m - 1)
                    for k in range(K):
                        ins = nc.tensor.transpose(ps_back[s % 2][:, k * D:(k + 1) * D], biased[s % 2][:, k * P:(k + 1) * P], eye[0:D, 0:D])
                    ins.then_inc(c_back, 1)

                pipeline(pe, CHUNKS, [(spread, 0), (join, 1), (turn_back, 3)], LS)

            @block.vector
            def _(dve):
                def weigh(m, s, h, first):
                    dve.wait_ge(c_spread, m + 1)
                    if not fresh(m, 2):
                        dve.wait_ge(c_msg, m - 1)
                    v.tensor_tensor(wm[s % 2][:, :, :], sj[s][:, :, :], ps_w[s % 2][:, :, :], ALU.mult).then_inc(c_weighed, 1)

                def scan(m, s, h, first):
                    dve.wait_ge(c_msg, m + 1)
                    dve.wait_ge(c_in[s], h * 48 + 48)
                    if not fresh(m, 2):
                        dve.wait_ge(c_biased, m - 1)
                    if not fresh(m, 1):
                        dve.wait_ge(c_run, m)
                    start = 0.0 if fresh(m, 1) else run[1 - s % 2][:, CHUNK - 1:CHUNK]
                    v.tensor_tensor_scan(run[s % 2][:, :], ct[s][:, :], ps_m[s % 2][:, :], start, ALU.mult, ALU.add).then_inc(c_run, 1)

                pipeline(dve, CHUNKS, [(weigh, 0), (scan, 1)], LS)

            @block.scalar
            def _(act):
                act.wait_ge(c_const, 80)
                nc.scalar.copy(hs_sb[:, :, :], hs_f[:, :, :]).then_inc(c_const, 1)

                def add_bias(m, s, h, first):
                    act.wait_ge(c_run, m + 1)
                    if not fresh(m, 2):
                        act.wait_ge(c_back, m - 1)
                    nc.scalar.activation(biased[s % 2][:, :], run[s % 2][:, :], ACT.Identity, bias=bias_col[:, 0:1]).then_inc(c_biased, 1)

                def rows(m, s, h, first):
                    act.wait_ge(c_back, m + 1)
                    if not first:
                        act.wait_ge(c_out[s], h * (16 * K))
                    nc.scalar.copy(rows_sb[s][:, :, :].rearrange("p k f -> p (k f)"), ps_back[s % 2][:, 0:K * D]).then_inc(c_rows, 1)

                pipeline(act, CHUNKS, [(add_bias, 1), (rows, 3)], LS)

            @block.gpsimd
            def _(pool):
                def number_out(m, s, h, first):
                    if not first:
                        await_in_loop(pool, c_out[s], h * (16 * K))
                    pool.tensor_copy(at_out[s][:, :], by_src[:, bass.ds(m * K, K), OUT]).then_inc(c_index, 1)

                def scatter(m, s, h, first):
                    await_in_loop(pool, c_index, m + 1)
                    await_in_loop(pool, c_rows, m + 1)
                    for k in range(K):
                        pool.indirect_dma_start(msg0, bass.IndirectOffsetOnAxis(at_out[s][:, k:k + 1], 0), rows_sb[s][:, k, :],
                                                None, bounds_check=NPAD - 1, oob_is_err=False).then_inc(c_out[s], 16)

                pipeline(pool, CHUNKS, [(number_out, 0), (scatter, 1)], LS)
                for s in range(LS):
                    pool.wait_ge(c_out[s], 16 * K * times(s, LS))

        node_pass("l0", x, x1, h1)
        def sum_by_dst(name, table, target):
            count = {"mean": D, "hop0": D + 1, "hop1": None}[name]
            width = D if name == "hop1" else count + 1
            read = D + 1 if name == "hop0" else D
            wide = {"mean": D + 2, "hop0": D, "hop1": D}[name]
            with ExitStack() as c:
                c.enter_context(nc.cleanup_on_exit())
                got = [sb_in(c, f"got_{name}{s}", [P, K, width]) for s in range(GS)]
                at_in = [sb_in(c, f"at_in_{name}{s}", [P, K], i32) for s in range(GS)]
                at_out = [sb_in(c, f"at_out_{name}{s}", [P, K], i32) for s in range(GS)]
                ct = [sb_in(c, f"ct_{name}{s}", [80, CHUNK]) for s in range(GS)]
                run = [sb_in(c, f"run_{name}{s}", [width, CHUNK]) for s in range(2)]
                rows_sb = [sb_in(c, f"rows_{name}{s}", [P, K, wide]) for s in range(GS)]
                place = sb_in(c, f"place_{name}", [P, TILES], i32)
                over = sb_in(c, f"over_{name}", [P, K, 1])
                ps_v = [ps_in(c, f"v_{name}{s}", [P, CHUNK]) for s in range(2)]
                ps_back = [ps_in(c, f"back_{name}{s}", [P, CHUNK]) for s in range(2)]
                s_once = sem_in(c, f"{name}_once")
                s_index = sem_in(c, f"{name}_index")
                s_out_index = sem_in(c, f"{name}_out_index")
                s_in = [sem_in(c, f"{name}_in{s}") for s in range(GS)]
                s_flags = [sem_in(c, f"{name}_flags{s}") for s in range(GS)]
                s_turned = sem_in(c, f"{name}_turned")
                s_kept = sem_in(c, f"{name}_kept")
                s_run = sem_in(c, f"{name}_run")
                s_back = sem_in(c, f"{name}_back")
                s_over = sem_in(c, f"{name}_over")
                s_rows = sem_in(c, f"{name}_rows")
                s_out = [sem_in(c, f"{name}_out{s}") for s in range(GS)]
                out_once = 16 if name == "hop0" else 16 * K
                block = c.enter_context(nc.Block())
                v = nc.vector

                @block.sync
                def _(sp):
                    def flags(m, s, h, first):
                        if not first:
                            await_in_loop(sp, s_run, m + 1 - GS)
                        sp.dma_start(ct[s][:, :], same_dst[bass.ds(m * CHUNK, CHUNK)].rearrange("(o e) -> o e", o=1).to_broadcast([80, CHUNK])).then_inc(s_flags[s], 16)

                    def store(m, s, h, first):
                        await_in_loop(sp, s_rows, m + 1)
                        sp.dma_start(target[bass.ds(m * CHUNK + 1, CHUNK), :].rearrange("(k p) f -> p k f", p=P),
                                     rows_sb[s][:, :, :]).then_inc(s_out[s], 16)

                    if name == "hop0":
                        pipeline(sp, CHUNKS, [(flags, 0), (store, 2)], GS)
                        for s in range(GS):
                            await_in_loop(sp, s_out[s], 16 * times(s, GS))
                    else:
                        pipeline(sp, CHUNKS, [(flags, 0)], GS)

                @block.gpsimd
                def _(pool):
                    if name == "mean":
                        pool.iota(place[:, :], pattern=[[P, TILES]], base=1, channel_multiplier=1).then_inc(s_once, 1)
                    if count:
                        for s in range(GS):
                            pool.memset(got[s][:, :, :], 1.0).then_inc(s_once, 1)
                        pool.wait_ge(s_once, GS)

                    def number(m, s, h, first):
                        if not first:
                            await_in_loop(pool, s_in[s], h * (16 * K))
                        numbers = sum_at[:, bass.ds(m * K, K)] if name == "hop1" else by_dst[:, bass.ds(m * K, K), D_SRC]
                        pool.tensor_copy(at_in[s][:, :], numbers).then_inc(s_index, 1)

                    def gather(m, s, h, first):
                        await_in_loop(pool, s_index, m + 1)
                        if not first:
                            await_in_loop(pool, s_turned, m + 1 - GS)
                            if name == "hop0":
                                await_in_loop(pool, s_kept, m + 1 - GS)
                        for k in range(K):
                            pool.indirect_dma_start(got[s][:, k, 0:read], None, table,
                                                    bass.IndirectOffsetOnAxis(at_in[s][:, k:k + 1], 0)).then_inc(s_in[s], 16)

                    def number_out(m, s, h, first):
                        if not first:
                            await_in_loop(pool, s_out[s], h * (16 * K))
                        pool.tensor_copy(at_out[s][:, :], by_dst[:, bass.ds(m * K, K), D_OUT]).then_inc(s_out_index, 1)

                    def scatter(m, s, h, first):
                        await_in_loop(pool, s_out_index, m + 1)
                        await_in_loop(pool, s_rows, m + 1)
                        for k in range(K):
                            pool.indirect_dma_start(target, bass.IndirectOffsetOnAxis(at_out[s][:, k:k + 1], 0), rows_sb[s][:, k, :],
                                                    None, bounds_check=NPAD - 1, oob_is_err=False).then_inc(s_out[s], 16)

                    if name == "hop0":
                        pipeline(pool, CHUNKS, [(number, 0), (gather, 1)], GS)
                    else:
                        pipeline(pool, CHUNKS, [(number, 0), (number_out, 3), (gather, 1), (scatter, 4)], GS)
                        for s in range(GS):
                            pool.wait_ge(s_out[s], 16 * K * times(s, GS))

                @block.tensor
                def _(pe):
                    if count:
                        pe.wait_ge(s_once, GS)

                    def turn(m, s, h, first):
                        await_in_loop(pe, s_in[s], h * (16 * K) + 16 * K)
                        if not fresh(m, 2):
                            await_in_loop(pe, s_run, m - 1)
                        for k in range(K):
                            ins = nc.tensor.transpose(ps_v[s % 2][0:width, k * P:(k + 1) * P], got[s][:, k, :], eye[:, :])
                        ins.then_inc(s_turned, 1)

                    def turn_back(m, s, h, first):
                        await_in_loop(pe, s_run, m + 1)
                        if not fresh(m, 2):
                            await_in_loop(pe, s_rows, m - 1)
                        for k in range(K):
                            ins = nc.tensor.transpose(ps_back[s % 2][:, k * width:(k + 1) * width], run[s % 2][:, k * P:(k + 1) * P],
                                                      eye[0:width, 0:width])
                        ins.then_inc(s_back, 1)

                    pipeline(pe, CHUNKS, [(turn, 0), (turn_back, 1)], GS)

                @block.vector
                def _(dve):
                    def scan(m, s, h, first):
                        dve.wait_ge(s_turned, m + 1)
                        dve.wait_ge(s_flags[s], h * 16 + 16)
                        if not fresh(m, 2):
                            dve.wait_ge(s_back, m - 1)
                        if not fresh(m, 1):
                            dve.wait_ge(s_run, m)
                        start = 0.0 if fresh(m, 1) else run[(s + 1) % 2][:, CHUNK - 1:CHUNK]
                        v.tensor_tensor_scan(run[s % 2][:, :], ct[s][0:width, :], ps_v[s % 2][0:width, :], start, ALU.mult,
                                             ALU.add).then_inc(s_run, 1)

                    def divide(m, s, h, first):
                        dve.wait_ge(s_back, m + 1)
                        if not fresh(m, 1):
                            dve.wait_ge(s_rows, m)
                        sums = ps_back[s % 2][:, 0:K * width].rearrange("p (k f) -> p k f", f=width)
                        v.reciprocal(over[:, :, :], sums[:, :, count:count + 1]).then_inc(s_over, 1)
                        dve.wait_ge(s_over, m + 1)
                        if not first:
                            dve.wait_ge(s_out[s], h * out_once)
                        v.tensor_tensor(rows_sb[s][:, :, :], sums[:, :, 0:D], over[:, :, :].to_broadcast([P, K, D]),
                                        ALU.mult).then_inc(s_rows, 1)

                    if name == "hop0":
                        pipeline(dve, CHUNKS, [(scan, 0), (divide, 1)], GS)
                    else:
                        pipeline(dve, CHUNKS, [(scan, 0)], GS)

                @block.scalar
                def _(act):
                    def rows(m, s, h, first):
                        act.wait_ge(s_back, m + 1)
                        if not first:
                            act.wait_ge(s_out[s], h * out_once)
                        if name == "mean":
                            nc.scalar.copy(rows_sb[s][:, :, D + 1], place[:, bass.ds(m * K, K)])
                        nc.scalar.copy(rows_sb[s][:, :, 0:width], ps_back[s % 2][:, 0:K * width].rearrange("p (k f) -> p k f", f=width)).then_inc(s_rows, 1)

                    def keep(m, s, h, first):
                        act.wait_ge(s_in[s], h * (16 * K) + 16 * K)
                        nc.scalar.copy(sum_at[:, bass.ds(m * K, K)], got[s][:, :, D]).then_inc(s_kept, 1)

                    if name == "mean":
                        act.wait_ge(s_once, GS + 1)
                    pipeline(act, CHUNKS, [(keep, 0)] if name == "hop0" else [(rows, 1)], GS)

        sum_by_dst("mean", h1, msg1)
        node_pass("l1", x1, x2, h2)
        with ExitStack() as c:
            c.enter_context(nc.cleanup_on_exit())
            hs = [sb_in(c, f"hs{s}", [P, K, D]) for s in range(GS)]
            hd = [sb_in(c, f"b_hd{s}", [P, K, D + 1]) for s in range(GS)]
            at = [sb_in(c, f"b_at{s}", [P, K, 4], i32) for s in range(GS)]
            at_out = [sb_in(c, f"b_at_out{s}", [P, K], i32) for s in range(GS)]
            ct = [sb_in(c, f"b_ct{s}", [80, CHUNK]) for s in range(GS)]
            ty = [sb_in(c, f"b_ty{s}", [D, CHUNK]) for s in range(GS)]
            hot = sb_in(c, "hot", [D, CHUNK])
            gate = sb_in(c, "gate", [D, CHUNK])
            prod = sb_in(c, "prod", [D, CHUNK])
            pen = sb_in(c, "pen", [D + 1, CHUNK])
            top = [sb_in(c, f"top{s}", [D + 1, CHUNK + 1]) for s in range(2)]
            drop = sb_in(c, "drop", [D + 1, CHUNK])
            drop2 = sb_in(c, "drop2", [D + 1, CHUNK])
            less = sb_in(c, "less", [D + 1, CHUNK])
            decay = sb_in(c, "decay", [D + 1, CHUNK])
            grow = sb_in(c, "grow", [D + 1, CHUNK])
            val = sb_in(c, "val", [D + 1, CHUNK])
            run = [sb_in(c, f"b_run{s}", [D + 1, CHUNK]) for s in range(2)]
            rows_sb = [sb_in(c, f"b_rows{s}", [P, K, D + 2]) for s in range(GS)]
            rel_sb = sb_in(c, "rel_sb", [D, D])
            ones = sb_in(c, "ones", [D, P])
            maxima = sb_in(c, "maxima", [P, CHUNKS])
            ps_g = ps_in(c, "g", [D, CHUNK])
            ps_t = [ps_in(c, f"b_t{s}", [D + 1, CHUNK]) for s in range(2)]
            ps_s = ps_in(c, "b_s", [P, CHUNK])
            ps_back = [ps_in(c, f"b_back{s}", [P, CHUNK]) for s in range(2)]
            b_const = sem_in(c, "b_const")
            b_in = [sem_in(c, f"b_in{s}") for s in range(GS)]
            b_flags = [sem_in(c, f"b_flags{s}") for s in range(GS)]
            b_index = sem_in(c, "b_index")
            b_out_index = sem_in(c, "b_out_index")
            names = ("hot", "pre", "turned", "gate", "prod", "score", "pen", "link", "top", "drop", "drop2", "less",
                     "decay", "grow", "val", "max", "run", "back", "rows")
            b = {n: sem_in(c, "b_" + n) for n in names}
            b_out = [sem_in(c, f"b_out{s}") for s in range(GS)]
            block = c.enter_context(nc.Block())
            v = nc.vector

            @block.sync
            def _(sp):
                sp.dma_start(rel_sb[:, :], rel).then_inc(b_const, 16)

                def load(m, s, h, first):
                    if not first:
                        await_in_loop(sp, b["pen"], m + 1 - GS)
                        await_in_loop(sp, b["hot"], m + 1 - GS)
                    sp.dma_start(ct[s][:, :], same_src[bass.ds(m * CHUNK, CHUNK)].rearrange("(o e) -> o e", o=1).to_broadcast([80, CHUNK])).then_inc(b_flags[s], 16)
                    sp.dma_start(ty[s][:, :], types_row.rearrange("t p -> (t p)")[bass.ds(m * CHUNK, CHUNK)].rearrange("(o e) -> o e", o=1).to_broadcast([D, CHUNK])).then_inc(b_flags[s], 16)

                pipeline(sp, CHUNKS, [(load, 0)], GS)

            @block.gpsimd
            def _(pool):
                for s in range(GS):
                    pool.memset(hd[s][:, :, :], 1.0).then_inc(b_const, 1)
                for s in range(2):
                    pool.memset(top[s][:, :], 0.0).then_inc(b_const, 1)
                pool.memset(ones[:, :], 1.0).then_inc(b_const, 1)
                pool.memset(maxima[:, :], -BIG).then_inc(b_const, 1)
                pool.wait_ge(b_const, 16 + GS + 4)

                def number(m, s, h, first):
                    if not first:
                        await_in_loop(pool, b_in[s], h * (32 * K))
                    pool.tensor_copy(at[s][:, :, :], by_src[:, bass.ds(m * K, K), :]).then_inc(b_index, 1)

                def gather(m, s, h, first):
                    await_in_loop(pool, b_index, m + 1)
                    if not first:
                        await_in_loop(pool, b["turned"], m + 1 - GS)
                    for k in range(K):
                        pool.indirect_dma_start(hs[s][:, k, :], None, h2,
                                                bass.IndirectOffsetOnAxis(at[s][:, k, SRC:SRC + 1], 0)).then_inc(b_in[s], 16)
                    for k in range(K):
                        pool.indirect_dma_start(hd[s][:, k, 0:D], None, h2,
                                                bass.IndirectOffsetOnAxis(at[s][:, k, DST:DST + 1], 0)).then_inc(b_in[s], 16)

                def number_out(m, s, h, first):
                    if not first:
                        await_in_loop(pool, b_out[s], h * (16 * K))
                    pool.tensor_copy(at_out[s][:, :], by_src[:, bass.ds(m * K, K), OUT]).then_inc(b_out_index, 1)

                def scatter(m, s, h, first):
                    await_in_loop(pool, b_out_index, m + 1)
                    await_in_loop(pool, b["rows"], m + 1)
                    for k in range(K):
                        pool.indirect_dma_start(msg2, bass.IndirectOffsetOnAxis(at_out[s][:, k:k + 1], 0), rows_sb[s][:, k, :],
                                                None, bounds_check=NPAD - 1, oob_is_err=False).then_inc(b_out[s], 16)

                pipeline(pool, CHUNKS, [(number, 0), (number_out, 4), (gather, 1), (scatter, 5)], GS)
                for s in range(GS):
                    pool.wait_ge(b_out[s], 16 * K * times(s, GS))

            @block.tensor
            def _(pe):
                pe.wait_ge(b_const, 16 + GS + 4)

                def ends(m, s, h, first):
                    await_in_loop(pe, b["hot"], m + 1)
                    await_in_loop(pe, b_in[s], h * (32 * K) + 32 * K)
                    if not (fresh(m, 1)):
                        await_in_loop(pe, b["gate"], m)
                    nc.tensor.matmul(ps_g[:, :], rel_sb[:, :], hot[:, :], start=True, stop=False)
                    for k in range(K):
                        ins = nc.tensor.matmul(ps_g[:, k * P:(k + 1) * P], hs[s][:, k, :], eye[:, :], start=False, stop=(k == K - 1))
                    ins.then_inc(b["pre"], 1)
                    if not fresh(m, 2):
                        await_in_loop(pe, b["val"], m - 1)
                    for k in range(K):
                        ins = nc.tensor.transpose(ps_t[s % 2][:, k * P:(k + 1) * P], hd[s][:, k, :], eye[:, :])
                    ins.then_inc(b["turned"], 1)

                def score(m, s, h, first):
                    await_in_loop(pe, b["prod"], m + 1)
                    if not (fresh(m, 1)):
                        await_in_loop(pe, b["less"], m)
                        await_in_loop(pe, b["max"], m)
                    nc.tensor.matmul(ps_s[:, :], ones[:, :], prod[:, :], start=True, stop=True).then_inc(b["score"], 1)

                def turn_back(m, s, h, first):
                    await_in_loop(pe, b["run"], m + 1)
                    await_in_loop(pe, b["top"], m + 1)
                    if not fresh(m, 2):
                        await_in_loop(pe, b["rows"], m - 1)
                    for k in range(K):
                        nc.tensor.transpose(ps_back[s % 2][:, k * (D + 2):k * (D + 2) + D + 1], run[s % 2][:, k * P:(k + 1) * P],
                                            eye[0:D + 1, 0:D + 1])
                        ins = nc.tensor.transpose(ps_back[s % 2][:, k * (D + 2) + D + 1:(k + 1) * (D + 2)],
                                                  top[s % 2][0:1, 1 + k * P:1 + (k + 1) * P], eye[0:1, 0:1])
                    ins.then_inc(b["back"], 1)

                pipeline(pe, CHUNKS, [(turn_back, 2), (ends, 0), (score, 0)], GS)

            @block.vector
            def _(dve):
                dve.wait_ge(b_const, 16 + GS + 4)

                def types(m, s, h, first):
                    dve.wait_ge(b_flags[s], h * 32 + 32)
                    if not (fresh(m, 1)):
                        dve.wait_ge(b["pre"], m)
                    v.tensor_scalar(hot[:, :], ty[s][:, :], pid[0:D, 0:1], None, ALU.is_equal).then_inc(b["hot"], 1)

                def gated(m, s, h, first):
                    zero = fresh(m, 1)
                    dve.wait_ge(b["gate"], m + 1)
                    dve.wait_ge(b["turned"], m + 1)
                    if not zero:
                        dve.wait_ge(b["score"], m)
                    v.tensor_tensor(prod[:, :], gate[:, :], ps_t[s % 2][0:D, :], ALU.mult).then_inc(b["prod"], 1)

                def attend(m, s, h, first):
                    zero = fresh(m, 1)
                    dve.wait_ge(b["pen"], m + 1)
                    dve.wait_ge(b["score"], m + 1)
                    if not fresh(m, 2):
                        dve.wait_ge(b["back"], m - 1)
                    if not zero:
                        dve.wait_ge(b["top"], m)
                        dve.wait_ge(b["link"], m)
                    start = -BIG if zero else top[(s + 1) % 2][:, CHUNK:CHUNK + 1]
                    v.tensor_tensor_scan(top[s % 2][:, 1:CHUNK + 1], pen[:, :], ps_s[0:D + 1, :], start, ALU.add,
                                         ALU.max).then_inc(b["top"], 1)
                    dve.wait_ge(b["top"], m + 1)
                    v.tensor_tensor(less[:, :], ps_s[0:D + 1, :], top[s % 2][:, 1:CHUNK + 1], ALU.subtract).then_inc(b["less"], 1)
                    dve.wait_ge(b["link"], m + 1)
                    v.tensor_tensor(drop[:, :], top[s % 2][:, 0:CHUNK], top[s % 2][:, 1:CHUNK + 1], ALU.subtract).then_inc(b["drop"], 1)
                    dve.wait_ge(b["drop"], m + 1)
                    if not zero:
                        dve.wait_ge(b["decay"], m)
                    v.tensor_tensor(drop2[:, :], drop[:, :], pen[:, :], ALU.add).then_inc(b["drop2"], 1)
                    real = LAST_REAL if isinstance(m, int) and m == CHUNKS - 1 else CHUNK
                    v.tensor_reduce(maxima[:, bass.ds(m, 1)], ps_s[:, 0:real], AX, ALU.max).then_inc(b["max"], 1)
                    dve.wait_ge(b["grow"], m + 1)
                    if not zero:
                        dve.wait_ge(b["run"], m)
                    v.tensor_tensor(val[:, :], grow[:, :], ps_t[s % 2][:, :], ALU.mult).then_inc(b["val"], 1)
                    dve.wait_ge(b["val"], m + 1)
                    dve.wait_ge(b["decay"], m + 1)
                    start = 0.0 if zero else run[(s + 1) % 2][:, CHUNK - 1:CHUNK]
                    v.tensor_tensor_scan(run[s % 2][:, :], decay[:, :], val[:, :], start, ALU.mult, ALU.add).then_inc(b["run"], 1)

                pipeline(dve, CHUNKS, [(types, 0), (attend, 1), (gated, 0)], GS, peel_last=True)
                dve.wait_ge(b["max"], CHUNKS)
                v.tensor_reduce(gmax[:, :], maxima[:, :], AX, ALU.max).then_inc(b["max"], 1)
                dve.wait_ge(b["max"], CHUNKS + 1)

            @block.scalar
            def _(act):
                act.wait_ge(b_const, 16 + GS + 4)

                def attend(m, s, h, first):
                    zero = fresh(m, 1)
                    act.wait_ge(b_flags[s], h * 32 + 32)
                    if not zero:
                        act.wait_ge(b["drop2"], m)
                        act.wait_ge(b["top"], m)
                    nc.scalar.activation(pen[:, :], ct[s][0:D + 1, :], ACT.Copy, scale=BIG, bias=-BIG).then_inc(b["pen"], 1)
                    if zero:
                        act.sem_inc(b["link"], 1)
                    else:
                        act.wait_ge(b["top"], m)
                        nc.scalar.copy(top[s % 2][:, 0:1], top[(s + 1) % 2][:, CHUNK:CHUNK + 1]).then_inc(b["link"], 1)
                    act.wait_ge(b["less"], m + 1)
                    if not zero:
                        act.wait_ge(b["val"], m)
                    nc.scalar.activation(grow[:, :], less[:, :], ACT.Exp).then_inc(b["grow"], 1)
                    act.wait_ge(b["drop2"], m + 1)
                    if not zero:
                        act.wait_ge(b["run"], m)
                    nc.scalar.activation(decay[:, :], drop2[:, :], ACT.Exp).then_inc(b["decay"], 1)

                def tanh(m, s, h, first):
                    act.wait_ge(b["pre"], m + 1)
                    if not fresh(m, 1):
                        act.wait_ge(b["prod"], m)
                    nc.scalar.activation(gate[:, :], ps_g[:, :], ACT.Tanh).then_inc(b["gate"], 1)

                def rows(m, s, h, first):
                    act.wait_ge(b["back"], m + 1)
                    if not first:
                        act.wait_ge(b_out[s], h * (16 * K))
                    nc.scalar.copy(rows_sb[s][:, :, :].rearrange("p k f -> p (k f)"), ps_back[s % 2][:, 0:K * (D + 2)]).then_inc(b["rows"], 1)

                pipeline(act, CHUNKS, [(rows, 2), (attend, 1), (tanh, 0)], GS)

        node_pass("l2", x2, x3, feat)
        sum_by_dst("hop0", g0, hop0)
        sum_by_dst("hop1", hop0, hop1)

        with ExitStack() as c:
            c.enter_context(nc.cleanup_on_exit())
            xi = [sb_in(c, f"o_xi{s}", [P, ROWS, D]) for s in range(OS)]
            hi = [sb_in(c, f"o_hi{s}", [P, ROWS, D]) for s in range(OS)]
            both = [sb_in(c, f"both{s}", [P, ROWS, 2 * D]) for s in range(OS)]
            bt = [sb_in(c, f"bt{s}", [P, ROWS * P]) for s in range(OS)]
            xb = [sb_in(c, f"o_xb{s}", [P, ROWS, D]) for s in range(OS)]
            oo = [sb_in(c, f"o_oo{s}", [P, ROWS, D]) for s in range(OS)]
            w3_sb = sb_in(c, "w3_sb", [P, D])
            bsum = sb_in(c, "bsum", [P, D])
            ps_bt = [ps_in(c, f"bt{s}", [P, ROWS * P]) for s in range(2)]
            ps_o = [ps_in(c, f"o{s}", [P, ROWS * D]) for s in range(2)]
            o_const = sem_in(c, "o_const")
            o_in = [sem_in(c, f"o_in{s}") for s in range(OS)]
            o = {n: sem_in(c, "o_" + n) for n in ("scaled", "biased", "turned", "copied", "prod", "sum")}
            o_out = [sem_in(c, f"o_out{s}") for s in range(OS)]
            block = c.enter_context(nc.Block())
            v = nc.vector

            @block.sync
            def _(sp):
                sp.dma_start(w3_sb[:, :], w3).then_inc(o_const, 16)
                sp.dma_start(b3_b[:, 0, :], b3.to_broadcast([P, D])).then_inc(o_const, 16)
                sp.dma_start(b3_b[:, 1, :], br3.to_broadcast([P, D])).then_inc(o_const, 16)

                def load(m, s, h, first):
                    if not first:
                        await_in_loop(sp, o["scaled"], m + 1 - OS)
                        await_in_loop(sp, o["biased"], m + 1 - OS)
                        await_in_loop(sp, o["turned"], m + 1 - OS)
                    sp.dma_start(hi[s][:, :, :].rearrange("p k (o f) -> p o (k f)", o=1), rows_of(hop1, m)).then_inc(o_in[s], 16)
                    sp.dma_start(xi[s][:, :, :].rearrange("p k (o f) -> p o (k f)", o=1), rows_of(x3, m)).then_inc(o_in[s], 16)
                    sp.dma_start(both[s][:, :, D:2 * D], feat.rearrange("(c p k) f -> c p k f", p=P, k=ROWS)[bass.ds(m, 1), :, :, :].rearrange("o p k f -> (o p) k f")).then_inc(o_in[s], 16)

                def store(m, s, h, first):
                    await_in_loop(sp, o["sum"], m + 1)
                    sp.dma_start(rows_of(out, m), oo[s][:, :, :].rearrange("p k (o f) -> p o (k f)", o=1)).then_inc(o_out[s], 16)

                pipeline(sp, NCHUNKS, [(load, 0), (store, 5)], OS)
                for s in range(OS):
                    await_in_loop(sp, o_out[s], 16 * ((NCHUNKS - s + OS - 1) // OS))

            @block.gpsimd
            def _(pool):
                pool.wait_ge(o_const, 48)
                pool.tensor_tensor(bsum[:, :], b3_b[:, 0, :], b3_b[:, 1, :], ALU.add).then_inc(o_const, 1)
                pool.wait_ge(o_const, 49)

                def bias(m, s, h, first):
                    await_in_loop(pool, o_in[s], h * 48 + 48)
                    if not first:
                        await_in_loop(pool, o["sum"], m + 1 - OS)
                    pool.tensor_tensor(xb[s][:, :, :], xi[s][:, :, :],
                                       bsum[:, :].rearrange("p (o f) -> p o f", o=1).to_broadcast([P, ROWS, D]), ALU.add).then_inc(o["biased"], 1)

                pipeline(pool, NCHUNKS, [(bias, 0)], OS)

            @block.vector
            def _(dve):
                def scale(m, s, h, first):
                    dve.wait_ge(o_in[s], h * 48 + 48)
                    if not first:
                        dve.wait_ge(o["turned"], m + 1 - OS)
                    v.tensor_tensor(both[s][:, :, 0:D], hi[s][:, :, :],
                                    inv_deg[:, bass.ds(m, 1), :].rearrange("p o k -> p k o").to_broadcast([P, ROWS, D]),
                                    ALU.mult).then_inc(o["scaled"], 1)

                def add(m, s, h, first):
                    dve.wait_ge(o["prod"], m + 1)
                    dve.wait_ge(o["biased"], m + 1)
                    if not first:
                        dve.wait_ge(o_out[s], h * 16)
                    v.tensor_tensor(oo[s][:, :, :].rearrange("p k f -> p (k f)"), ps_o[s % 2][:, :],
                                    xb[s][:, :, :].rearrange("p k f -> p (k f)"), ALU.add).then_inc(o["sum"], 1)

                pipeline(dve, NCHUNKS, [(scale, 0), (add, 2)], OS)

            @block.scalar
            def _(act):
                def copy(m, s, h, first):
                    act.wait_ge(o["turned"], m + 1)
                    if not first:
                        act.wait_ge(o["prod"], m + 1 - OS)
                    nc.scalar.copy(bt[s][:, :], ps_bt[s % 2][:, :]).then_inc(o["copied"], 1)

                pipeline(act, NCHUNKS, [(copy, 0)], OS)

            @block.tensor
            def _(pe):
                pe.wait_ge(o_const, 48)

                def turn(m, s, h, first):
                    await_in_loop(pe, o_in[s], h * 48 + 48)
                    await_in_loop(pe, o["scaled"], m + 1)
                    if not fresh(m, 2):
                        await_in_loop(pe, o["copied"], m - 1)
                    for k in range(ROWS):
                        ins = nc.tensor.transpose(ps_bt[s % 2][:, k * P:(k + 1) * P], both[s][:, k, :], eye[:, :])
                    ins.then_inc(o["turned"], 1)

                def project(m, s, h, first):
                    await_in_loop(pe, o["copied"], m + 1)
                    if not fresh(m, 2):
                        await_in_loop(pe, o["sum"], m - 1)
                    for k in range(ROWS):
                        ins = nc.tensor.matmul(ps_o[s % 2][:, k * D:(k + 1) * D], bt[s][:, k * P:(k + 1) * P], w3_sb[:, :],
                                               start=True, stop=True)
                    ins.then_inc(o["prod"], 1)

                pipeline(pe, NCHUNKS, [(turn, 0), (project, 1)], OS)

def _layouts(a):
    import numpy as np

    f = np.float32
    def pad(t, n, fill):
        full = np.full((n,) + t.shape[1:], fill, t.dtype)
        full[:t.shape[0]] = t
        return full
    src, dst, typ = (np.asarray(a[k]) for k in ("src", "dst", "edge_type_64"))
    ea = np.ascontiguousarray(a["edge_attr_64"])
    rec = np.concatenate([pad(ea, NPAD, 0).view(np.int32), pad(dst, NPAD, N)[:, None], pad(typ, NPAD, 0)[:, None]], 1)
    att = np.asarray(a["L0_gnn_att"])
    att_sel = np.zeros((P, 4, HEADS), f)
    for side in range(2):
        for b in range(2):
            for hh in range(2):
                att_sel[hh * D:(hh + 1) * D, 2 * side + b, 2 * b + hh] = att[0, 2 * b + hh, side * D:(side + 1) * D]
    headsel = np.zeros((HEADS, 2, P), f)
    for h in range(HEADS):
        headsel[h, h // 2, (h % 2) * D:(h % 2 + 1) * D] = 1
    headsum = np.concatenate([np.eye(D, dtype=f)] * 2, 0)
    q = np.arange(P)
    samehead = (q[:, None] % HEADS == q[None] % HEADS).astype(f)
    w2 = np.zeros((P, P), f)
    for b in range(2):
        w2[b * D:(b + 1) * D, b * D:(b + 1) * D] = np.asarray(a["L2_gnn_W"]).T
    w3 = np.concatenate([np.asarray(a["L3_gnn_W"]).T, np.asarray(a["L3_gnn_Wr"]).T], 0)
    return {
        "x": pad(np.asarray(a["x"]), NPAD, 0), "rec": rec,
        "src": pad(src, SORT_N, N), "dst": pad(dst, SORT_N, N), "ident": np.eye(P, dtype=f),
        "w0": np.asarray(a["L0_gnn_W"]), "att": att_sel.reshape(P, 4 * HEADS), "bias0": np.asarray(a["L0_gnn_bias"])[None],
        "gamma": np.tile(np.asarray(a["L0_gnn_bn_gamma"]), SEGS)[:, None],
        "beta": np.tile(np.asarray(a["L0_gnn_bn_beta"]), SEGS)[:, None],
        "headsel": headsel.reshape(HEADS, 2 * P), "headsum": headsum, "samehead": samehead,
        "rel": np.asarray(a["L2_gnn_rel_embed"]), "w2": w2, "w3": w3,
        "b3": np.asarray(a["L3_gnn_b"])[None], "br3": np.asarray(a["L3_gnn_br"])[None],
    }

def kernel(**inputs):
    import numpy as _np
    import concourse.bacc as _bacc
    from concourse import mybir as _mybir
    from concourse.bass_utils import run_bass_kernel_spmd as _run

    nc = _bacc.Bacc("TRN2", target_bir_lowering=False, num_devices=1)
    arrays, args = {}, []
    for name, a in _layouts(inputs).items():
        a = _np.ascontiguousarray(a)
        arrays[f"in_{name}_dram"] = a
        args.append(nc.dram_tensor(f"in_{name}_dram", a.shape, _mybir.dt.from_np(a.dtype), kind="ExternalInput").ap())
    out = nc.dram_tensor("out_dram", (NPAD, D), _mybir.dt.float32, kind="ExternalOutput").ap()
    gnn_kernel(nc, *args, out)
    r = _run(nc, [arrays], core_ids=[0])
    return r.results[0]["out_dram"][:N]
```
